# Optimizing a Trainium2 kernel written in Bass

```python
import numpy as np
import jax
import jax.numpy as jnp

def _softmax(x, axis=-1):
    return jax.nn.softmax(x, axis=axis)

def _gelu(x):
    return jax.nn.gelu(x, approximate=True)

def _silu(x):
    return jax.nn.silu(x)

def _sigmoid(x):
    return jax.nn.sigmoid(x)

def _layernorm(x, axis=-1, eps=1e-05):
    m = jnp.mean(x, axis=axis, keepdims=True)
    v = jnp.var(x, axis=axis, keepdims=True)
    return (x - m) / jnp.sqrt(v + eps)

def _scatter_add(tgt, idx, src, axis=0):
    return tgt.at[idx].add(src)

def _segment_sum(src, seg, n):
    return jax.ops.segment_sum(src, seg, n)
kernel_name = 'mk_seq_preln_d2_jaxref_r8_551a5b'

def setup_inputs(seed: int=0):
    np.random.seed(seed)
    _w = jnp.asarray

    def _L0_attn_setup():
        import jax, jax.numpy as jnp
        import numpy as np
        EPS = 1e-06
        N_HEADS = 4
        N_KV = 2

        def rmsnorm(x, w):
            xf = x.astype(jnp.float32)
            n = jax.lax.rsqrt(jnp.mean(jnp.square(xf), axis=-1, keepdims=True) + EPS)
            return (xf * n).astype(x.dtype) * w

        def selective_scan(x, delta, A, Bp, Cp, D_skip):
            Bb, L, D = x.shape
            N = A.shape[1]

            def step(h, inp):
                x_t, d_t, B_t, C_t = inp
                dA = jnp.exp(d_t[:, :, None] * A)
                h = dA * h + d_t[:, :, None] * B_t[:, None, :] * x_t[:, :, None]
                y_t = jnp.sum(h * C_t[:, None, :], axis=-1)
                return (h, y_t)
            h0 = jnp.zeros((Bb, D, N), x.dtype)
            xs = (x.transpose(1, 0, 2), delta.transpose(1, 0, 2), Bp.transpose(1, 0, 2), Cp.transpose(1, 0, 2))
            _, ys = jax.lax.scan(step, h0, xs)
            return ys.transpose(1, 0, 2) + x * D_skip

        def mamba_block(x, norm_m_w, in_proj_w, conv_w, conv_b, x_proj_w, dt_w, dt_b, A_log, D_skip, out_proj_w):
            d_inner = conv_w.shape[0]
            d_conv = conv_w.shape[-1]
            d_state = (x_proj_w.shape[0] - 1) // 2
            residual = x
            xn = rmsnorm(x, norm_m_w)
            xz = xn @ in_proj_w.T
            x_ssm, z = jnp.split(xz, 2, axis=-1)
            xc = x_ssm.transpose(0, 2, 1)
            xc = jax.lax.conv_general_dilated(xc, conv_w, window_strides=(1,), padding=[(d_conv - 1, 0)], feature_group_count=d_inner, dimension_numbers=('NCH', 'OIH', 'NCH')) + conv_b[None, :, None]
            x_ssm = jax.nn.silu(xc.transpose(0, 2, 1))
            ssm_p = x_ssm @ x_proj_w.T
            Bp = ssm_p[..., :d_state]
            Cp = ssm_p[..., d_state:2 * d_state]
            dt_raw = ssm_p[..., -1:]
            delta = jax.nn.softplus(dt_raw @ dt_w.T + dt_b)
            A = -jnp.exp(A_log)
            y = selective_scan(x_ssm, delta, A, Bp, Cp, D_skip)
            y = y * jax.nn.silu(z)
            return residual + y @ out_proj_w.T

        def attention_block(x, norm_attn_w, q_w, k_w, v_w, o_w, norm_ffn_w, gate_w, up_w, down_w):
            B, L, D = x.shape
            head_dim = D // N_HEADS
            scale = head_dim ** (-0.5)
            residual = x
            xn = rmsnorm(x, norm_attn_w)
            q = (xn @ q_w.T).reshape(B, L, N_HEADS, head_dim).transpose(0, 2, 1, 3)
            k = (xn @ k_w.T).reshape(B, L, N_KV, head_dim).transpose(0, 2, 1, 3)
            v = (xn @ v_w.T).reshape(B, L, N_KV, head_dim).transpose(0, 2, 1, 3)
            hpg = N_HEADS // N_KV
            k = jnp.repeat(k, hpg, axis=1)
            v = jnp.repeat(v, hpg, axis=1)
            attn = jnp.einsum('bhqd,bhkd->bhqk', q, k) * scale
            causal = jnp.triu(jnp.ones((L, L), dtype=bool), k=1)
            attn = jnp.where(causal[None, None], -jnp.inf, attn)
            attn = jax.nn.softmax(attn, axis=-1)
            out = jnp.einsum('bhqk,bhkd->bhqd', attn, v)
            out = out.transpose(0, 2, 1, 3).reshape(B, L, D) @ o_w.T
            x = residual + out
            residual = x
            xn = rmsnorm(x, norm_ffn_w)
            x_ffn = jax.nn.silu(xn @ gate_w.T) * (xn @ up_w.T) @ down_w.T
            return residual + x_ffn
        key = jax.random.key(seed)
        ks = jax.random.split(key, 16)
        d_model, d_state, d_conv, expand = (128, 16, 4, 2)
        d_inner = d_model * expand
        head_dim = d_model // N_HEADS
        ffn_h = int(d_model * 2.667)
        B, L = (4, 256)
        s = 0.02

        def rn(k, shape):
            return jax.random.normal(k, shape, jnp.float32) * s
        return {'x': jax.random.normal(ks[0], (B, L, d_model), jnp.float32), 'norm_m_w': jnp.ones(d_model, jnp.float32), 'in_proj_w': rn(ks[1], (d_inner * 2, d_model)), 'conv_w': rn(ks[2], (d_inner, 1, d_conv)), 'conv_b': jnp.zeros(d_inner, jnp.float32), 'x_proj_w': rn(ks[3], (d_state * 2 + 1, d_inner)), 'dt_w': rn(ks[4], (d_inner, 1)), 'dt_b': jnp.zeros(d_inner, jnp.float32), 'A_log': jnp.log(jnp.broadcast_to(jnp.arange(1, d_state + 1, dtype=jnp.float32), (d_inner, d_state))), 'D_skip': jnp.ones(d_inner, jnp.float32), 'out_proj_w': rn(ks[5], (d_model, d_inner)), 'norm_attn_w': jnp.ones(d_model, jnp.float32), 'q_w': rn(ks[6], (d_model, d_model)), 'k_w': rn(ks[7], (head_dim * N_KV, d_model)), 'v_w': rn(ks[8], (head_dim * N_KV, d_model)), 'o_w': rn(ks[9], (d_model, d_model)), 'norm_ffn_w': jnp.ones(d_model, jnp.float32), 'gate_w': rn(ks[10], (ffn_h, d_model)), 'up_w': rn(ks[11], (ffn_h, d_model)), 'down_w': rn(ks[12], (d_model, ffn_h))}
    _L0_attn_in = _L0_attn_setup()

    def _L0_ffn_setup():
        import jax, jax.numpy as jnp
        import numpy as np
        EPS = 1e-06
        LN_EPS = 1e-05

        def _absmean_core(W):
            gamma = jnp.mean(jnp.abs(W)) + EPS
            Ws = W / gamma
            Wq = jnp.sign(Ws) * jnp.minimum(jnp.round(jnp.abs(Ws)), 1.0)
            return (Wq, gamma)

        @jax.custom_vjp
        def absmean(W):
            return _absmean_core(W)[0]

        def _absmean_fwd(W):
            Wq, gamma = _absmean_core(W)
            return (Wq, gamma)

        def _absmean_bwd(gamma, g):
            return (g / gamma,)
        absmean.defvjp(_absmean_fwd, _absmean_bwd)

        def layernorm(x, w, b, eps=LN_EPS):
            mu = jnp.mean(x, axis=-1, keepdims=True)
            var = jnp.mean((x - mu) ** 2, axis=-1, keepdims=True)
            return (x - mu) * jax.lax.rsqrt(var + eps) * w + b
        key = jax.random.key(seed)
        k1, k2, k3 = jax.random.split(key, 3)
        d, h = (128, 512)
        B, T = (8, 256)
        return {'x': jax.random.normal(k1, (B, T, d), jnp.float32), 'W_fc': jax.random.normal(k2, (h, d), jnp.float32), 'ln_w': jnp.ones((h,), jnp.float32), 'ln_b': jnp.zeros((h,), jnp.float32), 'W_proj': jax.random.normal(k3, (d, h), jnp.float32)}
    _L0_ffn_in = _L0_ffn_setup()

    def _L1_attn_setup():
        import jax, jax.numpy as jnp
        import numpy as np
        B, S, H = (1, 256, 128)
        INTER, K, DST, DTR = (256, 4, 16, 64)

        def _ssm(dA, dBu, C):
            xs = (jnp.moveaxis(dA, 1, 0), jnp.moveaxis(dBu, 1, 0), jnp.moveaxis(C, 1, 0))
            state0 = jnp.zeros(dA.shape[:1] + dA.shape[2:], dA.dtype)

            def step(state, inp):
                Ai, dBui, Ci = inp
                state = Ai * state + dBui
                y = jnp.einsum('bhd,bd->bh', state, Ci)
                return (state, y)
            _, ys = jax.lax.scan(step, state0, xs)
            return jnp.moveaxis(ys, 0, 1)
        key = jax.random.key(seed)
        ks = jax.random.split(key, 10)
        sc = 0.02
        return {'x': jax.random.normal(ks[0], (B, S, H), jnp.float32), 'W_in': jax.random.normal(ks[1], (H, 2 * INTER), jnp.float32) * sc, 'conv_w': jax.random.normal(ks[2], (K, 1, INTER), jnp.float32) * sc, 'conv_b': jax.random.normal(ks[3], (INTER,), jnp.float32) * sc, 'W_x': jax.random.normal(ks[4], (INTER, DTR + 2 * DST), jnp.float32) * sc, 'W_dt': jax.random.normal(ks[5], (DTR, INTER), jnp.float32) * sc, 'b_dt': jax.random.normal(ks[6], (INTER,), jnp.float32) * sc, 'A_log': jax.random.normal(ks[7], (INTER, DST), jnp.float32) * sc, 'D': jax.random.normal(ks[8], (INTER,), jnp.float32) * sc, 'W_out': jax.random.normal(ks[9], (INTER, H), jnp.float32) * sc}
    _L1_attn_in = _L1_attn_setup()

    def _L1_ffn_setup():
        import jax, jax.numpy as jnp
        import numpy as np
        B, S, DIM, FFN, E = (4, 256, 128, 512, 8)
        key = jax.random.key(seed)
        k0, k1, k2, k3 = jax.random.split(key, 4)
        scale = 0.02
        return {'hidden_states': jax.random.normal(k0, (B, S, DIM), jnp.float32), 'router_w': jax.random.normal(k1, (DIM, E), jnp.float32) * scale, 'router_b': jnp.zeros((E,), jnp.float32), 'w1': jax.random.normal(k2, (E, DIM, 2 * FFN), jnp.float32) * scale, 'w2': jax.random.normal(k3, (E, FFN, DIM), jnp.float32) * scale}
    _L1_ffn_in = _L1_ffn_setup()
    _d = {'L0_attn_x': _L0_attn_in['x'], 'L0_attn_norm_m_w': _L0_attn_in['norm_m_w'], 'L0_attn_in_proj_w': _L0_attn_in['in_proj_w'], 'L0_attn_conv_w': _L0_attn_in['conv_w'], 'L0_attn_conv_b': _L0_attn_in['conv_b'], 'L0_attn_x_proj_w': _L0_attn_in['x_proj_w'], 'L0_attn_dt_w': _L0_attn_in['dt_w'], 'L0_attn_dt_b': _L0_attn_in['dt_b'], 'L0_attn_A_log': _L0_attn_in['A_log'], 'L0_attn_D_skip': _L0_attn_in['D_skip'], 'L0_attn_out_proj_w': _L0_attn_in['out_proj_w'], 'L0_attn_norm_attn_w': _L0_attn_in['norm_attn_w'], 'L0_attn_q_w': _L0_attn_in['q_w'], 'L0_attn_k_w': _L0_attn_in['k_w'], 'L0_attn_v_w': _L0_attn_in['v_w'], 'L0_attn_o_w': _L0_attn_in['o_w'], 'L0_attn_norm_ffn_w': _L0_attn_in['norm_ffn_w'], 'L0_attn_gate_w': _L0_attn_in['gate_w'], 'L0_attn_up_w': _L0_attn_in['up_w'], 'L0_attn_down_w': _L0_attn_in['down_w'], 'L0_ffn_W_fc': _L0_ffn_in['W_fc'], 'L0_ffn_ln_w': _L0_ffn_in['ln_w'], 'L0_ffn_ln_b': _L0_ffn_in['ln_b'], 'L0_ffn_W_proj': _L0_ffn_in['W_proj'], 'L1_attn_W_in': _L1_attn_in['W_in'], 'L1_attn_conv_w': _L1_attn_in['conv_w'], 'L1_attn_conv_b': _L1_attn_in['conv_b'], 'L1_attn_W_x': _L1_attn_in['W_x'], 'L1_attn_W_dt': _L1_attn_in['W_dt'], 'L1_attn_b_dt': _L1_attn_in['b_dt'], 'L1_attn_A_log': _L1_attn_in['A_log'], 'L1_attn_D': _L1_attn_in['D'], 'L1_attn_W_out': _L1_attn_in['W_out'], 'L1_ffn_router_w': _L1_ffn_in['router_w'], 'L1_ffn_router_b': _L1_ffn_in['router_b'], 'L1_ffn_w1': _L1_ffn_in['w1'], 'L1_ffn_w2': _L1_ffn_in['w2']}
    _x0 = _d['L0_attn_x']
    _d['L0_attn_x'] = jax.random.normal(jax.random.fold_in(jax.random.key(seed), 1), (4, 512, 128), dtype=_x0.dtype)
    del _x0
    return _d

def reference(L0_attn_x, L0_attn_norm_m_w, L0_attn_in_proj_w, L0_attn_conv_w, L0_attn_conv_b, L0_attn_x_proj_w, L0_attn_dt_w, L0_attn_dt_b, L0_attn_A_log, L0_attn_D_skip, L0_attn_out_proj_w, L0_attn_norm_attn_w, L0_attn_q_w, L0_attn_k_w, L0_attn_v_w, L0_attn_o_w, L0_attn_norm_ffn_w, L0_attn_gate_w, L0_attn_up_w, L0_attn_down_w, L0_ffn_W_fc, L0_ffn_ln_w, L0_ffn_ln_b, L0_ffn_W_proj, L1_attn_W_in, L1_attn_conv_w, L1_attn_conv_b, L1_attn_W_x, L1_attn_W_dt, L1_attn_b_dt, L1_attn_A_log, L1_attn_D, L1_attn_W_out, L1_ffn_router_w, L1_ffn_router_b, L1_ffn_w1, L1_ffn_w2):

    def _L0_attn_ref(x, norm_m_w, in_proj_w, conv_w, conv_b, x_proj_w, dt_w, dt_b, A_log, D_skip, out_proj_w, norm_attn_w, q_w, k_w, v_w, o_w, norm_ffn_w, gate_w, up_w, down_w):
        import jax, jax.numpy as jnp
        import numpy as np
        EPS = 1e-06
        N_HEADS = 4
        N_KV = 2

        def rmsnorm(x, w):
            xf = x.astype(jnp.float32)
            n = jax.lax.rsqrt(jnp.mean(jnp.square(xf), axis=-1, keepdims=True) + EPS)
            return (xf * n).astype(x.dtype) * w

        def selective_scan(x, delta, A, Bp, Cp, D_skip):
            Bb, L, D = x.shape
            N = A.shape[1]

            def step(h, inp):
                x_t, d_t, B_t, C_t = inp
                dA = jnp.exp(d_t[:, :, None] * A)
                h = dA * h + d_t[:, :, None] * B_t[:, None, :] * x_t[:, :, None]
                y_t = jnp.sum(h * C_t[:, None, :], axis=-1)
                return (h, y_t)
            h0 = jnp.zeros((Bb, D, N), x.dtype)
            xs = (x.transpose(1, 0, 2), delta.transpose(1, 0, 2), Bp.transpose(1, 0, 2), Cp.transpose(1, 0, 2))
            _, ys = jax.lax.scan(step, h0, xs)
            return ys.transpose(1, 0, 2) + x * D_skip

        def mamba_block(x, norm_m_w, in_proj_w, conv_w, conv_b, x_proj_w, dt_w, dt_b, A_log, D_skip, out_proj_w):
            d_inner = conv_w.shape[0]
            d_conv = conv_w.shape[-1]
            d_state = (x_proj_w.shape[0] - 1) // 2
            residual = x
            xn = rmsnorm(x, norm_m_w)
            xz = xn @ in_proj_w.T
            x_ssm, z = jnp.split(xz, 2, axis=-1)
            xc = x_ssm.transpose(0, 2, 1)
            xc = jax.lax.conv_general_dilated(xc, conv_w, window_strides=(1,), padding=[(d_conv - 1, 0)], feature_group_count=d_inner, dimension_numbers=('NCH', 'OIH', 'NCH')) + conv_b[None, :, None]
            x_ssm = jax.nn.silu(xc.transpose(0, 2, 1))
            ssm_p = x_ssm @ x_proj_w.T
            Bp = ssm_p[..., :d_state]
            Cp = ssm_p[..., d_state:2 * d_state]
            dt_raw = ssm_p[..., -1:]
            delta = jax.nn.softplus(dt_raw @ dt_w.T + dt_b)
            A = -jnp.exp(A_log)
            y = selective_scan(x_ssm, delta, A, Bp, Cp, D_skip)
            y = y * jax.nn.silu(z)
            return residual + y @ out_proj_w.T

        def attention_block(x, norm_attn_w, q_w, k_w, v_w, o_w, norm_ffn_w, gate_w, up_w, down_w):
            B, L, D = x.shape
            head_dim = D // N_HEADS
            scale = head_dim ** (-0.5)
            residual = x
            xn = rmsnorm(x, norm_attn_w)
            q = (xn @ q_w.T).reshape(B, L, N_HEADS, head_dim).transpose(0, 2, 1, 3)
            k = (xn @ k_w.T).reshape(B, L, N_KV, head_dim).transpose(0, 2, 1, 3)
            v = (xn @ v_w.T).reshape(B, L, N_KV, head_dim).transpose(0, 2, 1, 3)
            hpg = N_HEADS // N_KV
            k = jnp.repeat(k, hpg, axis=1)
            v = jnp.repeat(v, hpg, axis=1)
            attn = jnp.einsum('bhqd,bhkd->bhqk', q, k) * scale
            causal = jnp.triu(jnp.ones((L, L), dtype=bool), k=1)
            attn = jnp.where(causal[None, None], -jnp.inf, attn)
            attn = jax.nn.softmax(attn, axis=-1)
            out = jnp.einsum('bhqk,bhkd->bhqd', attn, v)
            out = out.transpose(0, 2, 1, 3).reshape(B, L, D) @ o_w.T
            x = residual + out
            residual = x
            xn = rmsnorm(x, norm_ffn_w)
            x_ffn = jax.nn.silu(xn @ gate_w.T) * (xn @ up_w.T) @ down_w.T
            return residual + x_ffn
        h = mamba_block(x, norm_m_w, in_proj_w, conv_w, conv_b, x_proj_w, dt_w, dt_b, A_log, D_skip, out_proj_w)
        return attention_block(h, norm_attn_w, q_w, k_w, v_w, o_w, norm_ffn_w, gate_w, up_w, down_w)

    def _L0_ffn_ref(x, W_fc, ln_w, ln_b, W_proj):
        import jax, jax.numpy as jnp
        import numpy as np
        EPS = 1e-06
        LN_EPS = 1e-05

        def _absmean_core(W):
            gamma = jnp.mean(jnp.abs(W)) + EPS
            Ws = W / gamma
            Wq = jnp.sign(Ws) * jnp.minimum(jnp.round(jnp.abs(Ws)), 1.0)
            return (Wq, gamma)

        @jax.custom_vjp
        def absmean(W):
            return _absmean_core(W)[0]

        def _absmean_fwd(W):
            Wq, gamma = _absmean_core(W)
            return (Wq, gamma)

        def _absmean_bwd(gamma, g):
            return (g / gamma,)
        absmean.defvjp(_absmean_fwd, _absmean_bwd)

        def layernorm(x, w, b, eps=LN_EPS):
            mu = jnp.mean(x, axis=-1, keepdims=True)
            var = jnp.mean((x - mu) ** 2, axis=-1, keepdims=True)
            return (x - mu) * jax.lax.rsqrt(var + eps) * w + b
        h = jnp.einsum('btd,hd->bth', x, absmean(W_fc))
        h = jax.nn.gelu(h, approximate=False)
        h = layernorm(h, ln_w, ln_b)
        return jnp.einsum('bth,dh->btd', h, absmean(W_proj))

    def _L1_attn_ref(x, W_in, conv_w, conv_b, W_x, W_dt, b_dt, A_log, D, W_out):
        import jax, jax.numpy as jnp
        import numpy as np
        B, S, H = (1, 256, 128)
        INTER, K, DST, DTR = (256, 4, 16, 64)

        def _ssm(dA, dBu, C):
            xs = (jnp.moveaxis(dA, 1, 0), jnp.moveaxis(dBu, 1, 0), jnp.moveaxis(C, 1, 0))
            state0 = jnp.zeros(dA.shape[:1] + dA.shape[2:], dA.dtype)

            def step(state, inp):
                Ai, dBui, Ci = inp
                state = Ai * state + dBui
                y = jnp.einsum('bhd,bd->bh', state, Ci)
                return (state, y)
            _, ys = jax.lax.scan(step, state0, xs)
            return jnp.moveaxis(ys, 0, 1)
        proj = x @ W_in
        raw, gate = jnp.split(proj, 2, axis=-1)
        conv = jax.lax.conv_general_dilated(raw, conv_w, window_strides=(1,), padding=[(K - 1, 0)], dimension_numbers=('NWC', 'WIO', 'NWC'), feature_group_count=INTER)
        h = jax.nn.silu(conv + conv_b)
        ssm_p = h @ W_x
        ts, Bmat, C = jnp.split(ssm_p, [DTR, DTR + DST], axis=-1)
        dt = jax.nn.softplus(ts @ W_dt + b_dt)
        A = -jnp.exp(A_log)
        dA = jnp.exp(dt[..., None] * A)
        dBu = dt[..., None] * Bmat[:, :, None, :] * h[..., None]
        y = _ssm(dA, dBu, C)
        y = y + h * D
        y = y * jax.nn.silu(gate)
        return y @ W_out

    def _L1_ffn_ref(hidden_states, router_w, router_b, w1, w2):
        import jax, jax.numpy as jnp
        import numpy as np
        B, S, DIM, FFN, E = (4, 256, 128, 512, 8)
        b, s, d = hidden_states.shape
        x = hidden_states.reshape(-1, d)
        logits = x @ router_w + router_b
        route = jax.nn.softmax(logits, axis=1)
        max_prob = jnp.max(route, axis=1, keepdims=True)
        max_ind = jnp.argmax(route, axis=1)
        out = jnp.zeros_like(x)
        num_experts = w1.shape[0]
        for e in range(num_experts):
            h = x @ w1[e]
            a, g = jnp.split(h, 2, axis=1)
            y = jax.nn.silu(a) * g @ w2[e]
            out = jnp.where((max_ind == e)[:, None], y, out)
        out = out * max_prob
        return out.reshape(b, s, d)
    x = L0_attn_x
    x = x + _L0_attn_ref(_layernorm(x, axis=-1), L0_attn_norm_m_w, L0_attn_in_proj_w, L0_attn_conv_w, L0_attn_conv_b, L0_attn_x_proj_w, L0_attn_dt_w, L0_attn_dt_b, L0_attn_A_log, L0_attn_D_skip, L0_attn_out_proj_w, L0_attn_norm_attn_w, L0_attn_q_w, L0_attn_k_w, L0_attn_v_w, L0_attn_o_w, L0_attn_norm_ffn_w, L0_attn_gate_w, L0_attn_up_w, L0_attn_down_w)
    x = x + _L0_ffn_ref(_layernorm(x, axis=-1), L0_ffn_W_fc, L0_ffn_ln_w, L0_ffn_ln_b, L0_ffn_W_proj)
    x = x + _L1_attn_ref(_layernorm(x, axis=-1), L1_attn_W_in, L1_attn_conv_w, L1_attn_conv_b, L1_attn_W_x, L1_attn_W_dt, L1_attn_b_dt, L1_attn_A_log, L1_attn_D, L1_attn_W_out)
    x = x + _L1_ffn_ref(_layernorm(x, axis=-1), L1_ffn_router_w, L1_ffn_router_b, L1_ffn_w1, L1_ffn_w2)
    return x

_drawn_inputs = setup_inputs


def setup_inputs(seed=0):
    import zlib

    import numpy as np

    out = dict(_drawn_inputs(seed))
    spreads = {'L0_attn_norm_m_w': (1.0, 0.6),
     'L0_attn_conv_b': (0.0, 0.8),
     'L0_attn_dt_b': (0.0, 0.8),
     'L0_attn_D_skip': (1.0, 0.6),
     'L0_attn_norm_attn_w': (1.0, 0.6),
     'L0_attn_norm_ffn_w': (1.0, 0.6),
     'L0_ffn_ln_w': (1.0, 0.2),
     'L0_ffn_ln_b': (0.0, 0.1),
     'L1_ffn_router_b': (0.0, 0.8)}
    factors = {'L0_attn_in_proj_w': 8.0,
     'L0_attn_conv_w': 8.0,
     'L0_attn_x_proj_w': 8.0,
     'L0_attn_dt_w': 8.0,
     'L0_attn_A_log': 8.0,
     'L0_attn_out_proj_w': 8.0,
     'L0_attn_q_w': 8.0,
     'L0_attn_k_w': 8.0,
     'L0_attn_v_w': 8.0,
     'L0_attn_o_w': 8.0,
     'L0_attn_gate_w': 8.0,
     'L0_attn_up_w': 8.0,
     'L0_attn_down_w': 8.0,
     'L1_attn_W_in': 8.0,
     'L1_attn_conv_w': 8.0,
     'L1_attn_conv_b': 8.0,
     'L1_attn_W_x': 8.0,
     'L1_attn_A_log': 55.688,
     'L1_attn_D': 64.0,
     'L1_attn_W_out': 8.0,
     'L1_ffn_router_w': 8.0,
     'L1_ffn_w1': 8.0,
     'L1_ffn_w2': 8.0,
     'L1_attn_W_dt': 7.071,
     'L1_attn_b_dt': 46.931}
    for name, (base, spread) in spreads.items():
        noise = np.random.default_rng([zlib.crc32(name.encode()), seed]).standard_normal(out[name].shape)
        drawn = base * np.exp(spread * noise) if base else spread * noise
        out[name] = jnp.asarray(drawn.astype(out[name].dtype))
    for name, factor in factors.items():
        out[name] = (out[name] * factor).astype(out[name].dtype)
    return out
```

```python
from contextlib import ExitStack

import concourse.bass as bass
from concourse import mybir

P = 128
F32 = mybir.dt.float32
BF16 = mybir.dt.bfloat16
ALU = mybir.AluOpType
ACT = mybir.ActivationFunctionType
AX = mybir.AxisListType

LN_EPS = 1e-5
RMS_EPS = 1e-6
QUANT_EPS = 1e-6
N_HEADS = 4
EXP_LN = "natural_log_exp_and_others"

PER = {}
BEFORE = {}


def build(nc, d, out):
    SEQS, D, T = d["xT"].shape
    TAPS = d["m0_cw"].shape[0]
    PAD = TAPS - 1
    STATE = d["m0_Alog"].shape[2]
    HALVES = d["m0_Alog"].shape[0]
    FFN_H = d["gateT"].shape[1]
    FB = (FFN_H + P - 1) // P
    FFN_ROWS = [min(P, FFN_H - P * j) for j in range(FB)]
    MH = d["fcT"].shape[1] // P
    E = d["w1"].shape[0]
    MOE_H = d["w2"].shape[1]
    MB = MOE_H // P
    QB = T // P
    HD = D // N_HEADS
    SCALE = float(HD) ** -0.5
    BCR = 2 * STATE
    DTR = {0: 1, 1: d["m1_dtT"].shape[0]}
    assert D == P and T == 512 and HALVES == 2

    with ExitStack() as ctx:
        def sb(name, shape, dt=F32):
            return ctx.enter_context(nc.sbuf_tensor(name, shape, dt))

        bank = ctx.enter_context(nc.psum_tensor("bank", [P, 8, T], F32))
        sems = {}

        def new_sem(name, per=1, uses=("",)):
            handle = ctx.enter_context(nc.semaphore(name))
            for i, use in enumerate(uses):
                sems[use + name] = handle
                PER[use + name] = per * len(uses)
                BEFORE[use + name] = per * i

        ident = sb("ident", [P, P])
        center = sb("center", [P, P])
        mean_d = sb("mean_d", [P, P])
        mean_h = sb("mean_h", [P, P])
        ones = sb("ones", [P, P])
        causal = sb("causal", [P, P])
        pick = sb("pick", [3 * BCR, BCR, P], BF16)
        eminus = sb("eminus", [P, QB, E])
        rowpick = sb("rowpick", [E, E, P])
        eps_ln = sb("eps_ln", [P, 1])
        eps_rms = sb("eps_rms", [P, 1])
        one_col = sb("one_col", [P, 1])
        M = []
        for m in range(2):
            M.append(dict(
                cw=sb(f"m{m}_cw_s", [P, TAPS, HALVES * P]), winx=sb(f"m{m}_winx_s", [P, HALVES * P]),
                wz=sb(f"m{m}_wz_s", [P, HALVES * P]), cb=sb(f"m{m}_cb_s", [P, HALVES]),
                wx=sb(f"m{m}_wx_s", [P, HALVES, DTR[m] + BCR]), wdt=sb(f"m{m}_wdt_s", [DTR[m], HALVES * P]),
                db=sb(f"m{m}_db_s", [P, HALVES]), A=sb(f"m{m}_A_s", [P, HALVES, STATE]),
                dskip=sb(f"m{m}_dskip_s", [P, HALVES]), wo=sb(f"m{m}_wo_s", [P, HALVES, D])))
        norm_m = sb("norm_m", [P, 1])
        norm_a = sb("norm_a", [P, 1])
        norm_f = sb("norm_f", [P, 1])
        wq = sb("wq", [P, D])
        wk = sb("wk", [P, D])
        wv = sb("wv", [P, D])
        wo = sb("wo", [P, D])
        wgate = sb("wgate", [P, FFN_H])
        wup = sb("wup", [P, FFN_H])
        wdown = sb("wdown", [P, FB, D])
        fc = sb("fc", [P, MH * P])
        proj = sb("proj", [P, MH, D])
        lnw = sb("lnw", [P, MH])
        lnb = sb("lnb", [P, MH])
        projw = sb("projw", [P, MH, D])
        projb = sb("projb", [P, 1])
        router = sb("router", [P, E])
        router_b = sb("router_b", [1, E])
        w1 = sb("w1", [P, E, 2 * MOE_H])
        w2 = sb("w2", [P, E, MB, D])

        xin = sb("xin", [P, T])
        xl = sb("xl", [P, T])
        xn = [sb(f"xn{m}", [P, PAD + T]) for m in range(2)]
        nrm = sb("nrm", [P, T])
        sq = sb("sq", [P, T])
        lnv = sb("lnv", [P, T])
        rstd = sb("rstd", [P, T])
        xs = sb("xs", [P, HALVES, T])
        zs = sb("zs", [P, HALVES, T])
        dt_rows = sb("dt_rows", [DTR[1], T])
        parts = sb("parts", [3 * BCR, T], BF16)
        rest = sb("rest", [BCR, T])
        mid = sb("mid", [BCR, T], BF16)
        sp_abs = sb("sp_abs", [P, HALVES, T])
        sp_max = sb("sp_max", [P, HALVES, T])
        delta = sb("delta", [P, HALVES, T])
        du = sb("du", [P, HALVES, T])
        dbu = sb("dbu", [P, 2, HALVES, T])
        hst = sb("hst", [P, 2, HALVES, T])
        hc = sb("hc", [P, 2, HALVES, T])
        csb = sb("csb", [P, 2, T])
        yd = sb("yd", [P, HALVES, T])
        h0 = sb("h0", [P, T])
        qs = sb("qs", [P, T])
        ks = sb("ks", [P, T])
        vs = sb("vs", [P, QB, D])
        nmax = sb("nmax", [P, N_HEADS * QB])
        psums = sb("psums", [P, QB, N_HEADS])
        rsums = sb("rsums", [P, QB, N_HEADS])
        prob, probT = delta, du
        att = sb("att", [P, QB, D])
        attT = sb("attT", [P, T])
        h1 = sb("h1", [P, T])
        gs = dbu[:].rearrange("p a h t -> p (a h) t")
        gc = hst[:].rearrange("p a h t -> p (a h) t")
        x1 = sb("x1", [P, T])
        x2 = sb("x2", [P, T])
        x3 = sb("x3", [P, T])
        lg = sb("lg", [P, QB, E])
        lmax = sb("lmax", [P, QB])
        le = sb("le", [P, QB, E])
        lsum = sb("lsum", [P, QB])
        lprob = sb("lprob", [P, QB])
        eqm = sb("eqm", [P, QB, E])
        cand = sb("cand", [P, QB, E])
        first = sb("first", [P, QB])
        onehot = sb("onehot", [P, QB, E])
        gate = sb("gate", [P, QB, E])
        gateT = sb("gateT", [E, T])
        gbc, es, eg, ey = sp_abs, sp_max, delta, du
        outs = sb("outs", [P, T])
        absr = sb("absr", [P, 2])
        thr = sb("thr", [P, 4])
        qtmp, qtmp2 = x1, x2

        for name, per in (
                ("w_loaded", 0), ("setup_dve", 0), ("setup_act", 0), ("setup_pe", 0),
                ("io", 32), ("outs_ready", 1)):
            new_sem(name, per)
        norms = ("ln0", "rms0", "rmsA", "rmsF", "ln1", "lnH", "ln2", "ln3")
        for part in ("_squared", "_var", "_logged", "_rstd"):
            new_sem(part, 1, norms)
        new_sem("_centered", 1, ("ln0", "ln1", "ln2", "ln3"))
        new_sem("_done", 1, [n for n in norms if n != "lnH"])
        for part, per in (("conv", 2), ("z", 2), ("xs", 2), ("zs", 2), ("proj", 1), ("dtrows", 1),
                          ("hi", 1), ("rest", 1), ("mid", 1), ("midcopy", 1), ("lo", 1), ("dtp", 2),
                          ("spabs", 2), ("spmax", 2), ("spexp", 1), ("spln", 1), ("delta", 1), ("du", 1),
                          ("bbc", STATE), ("cbc", STATE), ("dA", 2 * STATE), ("ccopy", STATE),
                          ("dbu", STATE), ("scan", 2 * STATE), ("hc", STATE), ("yacc", STATE),
                          ("yd", 2), ("yg", 1), ("out", 1), ("res", 1)):
            new_sem("_" + part, per, ("m0", "m1"))
        TILES = N_HEADS * QB
        for name, per in (("q_mm", 1), ("k_mm", 1), ("v_mm", 1), ("q_copy", 1), ("k_copy", 1), ("v_copy", 1),
                          ("score", TILES), ("smax", TILES), ("prob", TILES), ("probT_mm", TILES),
                          ("probT", TILES), ("pv", TILES), ("recip", 1), ("att", 1), ("attT_mm", 1),
                          ("attT", 1), ("o_mm", 1), ("h1", 1),
                          ("gate_mm", FB), ("up_mm", FB), ("gs", FB), ("gu", FB), ("down_mm", 1),
                          ("ffn_res", 1), ("x1", 1),
                          ("fc_mm", MH), ("gelu", MH), ("gmean", 1), ("gcen", 1), ("pj_mm", 1), ("pj_scaled", 1),
                          ("pj_bias", 1),
                          ("logit_mm", 1), ("lmax", 1), ("lsub", 1), ("lexp", 1), ("lsum", 1), ("lprob", 1),
                          ("eqm", 1), ("cand", 1), ("first", 1), ("onehot", 1), ("gate", 1), ("gateT_mm", 1),
                          ("gateT", 1), ("gbc_mm", E), ("gbc", E), ("ea_mm", E * MB), ("eg_mm", E * MB),
                          ("es", E * MB), ("eg", E * MB), ("ey", E * MB), ("ew2", E * MB)):
            new_sem(name, per)

        def nth(b, name, k):
            return b * PER[name] + BEFORE[name] + k

        def mean_of(m):
            return mean_h if m == "lnH" else mean_d

        loads = []

        def load(dst, src):
            loads.append((dst, src))

        for dst, key in ((ident, "ident"), (center, "center"), (mean_d, "mean_d"), (mean_h, "mean_h"),
                         (causal, "causal"), (pick, "pick"), (eminus, "eminus"), (rowpick, "rowpick"),
                         (norm_m, "norm_m"), (norm_a, "norm_a"), (norm_f, "norm_f"), (wq, "qT"), (wk, "kT"),
                         (wv, "vT"), (wo, "oT"), (wgate, "gateT"), (wup, "upT"), (fc, "fcT"),
                         (router, "router"), (router_b, "router_b"), (lnw, "lnw"), (lnb, "lnb")):
            load(dst[:], d[key])
        for m in range(2):
            load(M[m]["winx"][:], d[f"m{m}_win"][:, 0:HALVES * P])
            load(M[m]["wz"][:], d[f"m{m}_win"][:, HALVES * P:])
            for k in range(TAPS):
                load(M[m]["cw"][:, k, :], d[f"m{m}_cw"][k:k + 1, :].partition_broadcast(P)
                     if False else d[f"m{m}_cw"][k:k + 1, :].to_broadcast([P, HALVES * P]))
            load(M[m]["cb"][:], d[f"m{m}_cb"])
            load(M[m]["wx"][:], d[f"m{m}_wx"].rearrange("(h p) n -> p h n", p=P))
            load(M[m]["wdt"][:], d[f"m{m}_dtT"])
            load(M[m]["db"][:], d[f"m{m}_db"])
            load(M[m]["A"][:], d[f"m{m}_Alog"].rearrange("h p n -> p h n"))
            load(M[m]["dskip"][:], d[f"m{m}_D"])
            load(M[m]["wo"][:], d[f"m{m}_wo"].rearrange("(h p) n -> p h n", p=P))
        for j, rows in enumerate(FFN_ROWS):
            load(wdown[0:rows, j, :], d["downT"][P * j:P * j + rows, :])
        load(proj[:], d["projT"].rearrange("(j p) n -> p j n", p=P))
        load(w1[:], d["w1"].rearrange("e p n -> p e n"))
        load(w2[:], d["w2"].rearrange("e (j p) n -> p e j n", p=P))
        ALL_LOADED = 16 * len(loads)

        block = ctx.enter_context(nc.Block())

        @block.sync
        def _(sp):
            for dst, src in loads:
                sp.dma_start(dst, src).then_inc(sems["w_loaded"], 16)

            def load_x(b):
                sp.dma_start(xin[:], d["xT"][bass.ds(b, 1), :, :].rearrange("o p t -> (o p) t")) \
                    .then_inc(sems["io"], 16)

            def store_out(b):
                sp.wait_ge(sems["outs_ready"], nth(b, "outs_ready", 1))
                sp.dma_start(out[bass.ds(b, 1), :, :].rearrange("o p t -> (o p) t"), outs[:]) \
                    .then_inc(sems["io"], 16)

            load_x(0)
            with sp.Fori(0, SEQS - 1) as b:
                sp.wait_ge(sems["x1"], nth(b, "x1", 1))
                load_x(b + 1)
                store_out(b)
            store_out(SEQS - 1)
            sp.wait_ge(sems["io"], 32 * SEQS)

        @block.gpsimd
        def _(pool):
            def mamba(b, m):
                s = f"m{m}_"
                pool.wait_ge(sems[s + "spln"], nth(b, s + "spln", 1))
                pool.wait_ge(sems[s + "spmax"], nth(b, s + "spmax", 2))
                pool.tensor_tensor(delta[:], sp_max[:], sp_abs[:], ALU.add).then_inc(sems[s + "delta"], 1)
                pool.wait_ge(sems[s + "delta"], nth(b, s + "delta", 1))
                pool.tensor_tensor(du[:], delta[:], xs[:], ALU.mult).then_inc(sems[s + "du"], 1)
                for n in range(STATE):
                    pool.wait_ge(sems[s + "scan"], nth(b, s + "scan", 2 * n + 2))
                    pool.wait_ge(sems[s + "ccopy"], nth(b, s + "ccopy", n + 1))
                    if n >= 2:
                        pool.wait_ge(sems[s + "yacc"], nth(b, s + "yacc", n - 1))
                    pool.tensor_tensor(hc[:, n % 2], hst[:, n % 2],
                                       csb[:, n % 2:n % 2 + 1, :].to_broadcast([P, HALVES, T]),
                                       ALU.mult).then_inc(sems[s + "hc"], 1)
                pool.wait_ge(sems[s + "yd"], nth(b, s + "yd", 2))
                pool.tensor_tensor(yd[:], yd[:], zs[:], ALU.mult).then_inc(sems[s + "yg"], 1)

            with pool.Fori(0, SEQS) as b:
                mamba(b, 0)
                pool.wait_ge(sems["ffn_res"], nth(b, "ffn_res", 1))
                pool.tensor_tensor(x1[:], h0[:], xin[:], ALU.add).then_inc(sems["x1"], 1)
                mamba(b, 1)

        @block.scalar
        def _(act):
            act.wait_ge(sems["w_loaded"], ALL_LOADED)
            for m in range(2):
                act.activation(M[m]["A"][:], M[m]["A"][:], ACT.Exp).then_inc(sems["setup_act"], 1)
            act.wait_ge(sems["setup_dve"], 1)

            def rstd_of(b, n, src, src_ready, wide=False):
                act.wait_ge(sems[src_ready], nth(b, src_ready, 1))
                act.activation(gs if wide else sq[:], src, ACT.Square).then_inc(sems[n + "_squared"], 1)
                act.wait_ge(sems[n + "_var"], nth(b, n + "_var", 1))
                eps = eps_rms if n.startswith("rms") else eps_ln
                act.activation(lnv[:], bank[:, 1, :], ACT.Ln, bias=eps[:]).then_inc(sems[n + "_logged"], 1)
                act.wait_ge(sems[n + "_logged"], nth(b, n + "_logged", 1))
                act.activation(rstd[:], lnv[:], ACT.Exp, scale=-0.5).then_inc(sems[n + "_rstd"], 1)

            def mamba(b, m):
                s, w = f"m{m}_", M[m]
                for h in range(HALVES):
                    act.wait_ge(sems[s + "conv"], nth(b, s + "conv", h + 1))
                    act.activation(xs[:, h], bank[:, 2 + h, :], ACT.Silu, bias=w["cb"][:, h:h + 1]) \
                        .then_inc(sems[s + "xs"], 1)
                for h in range(HALVES):
                    act.wait_ge(sems[s + "z"], nth(b, s + "z", h + 1))
                    act.activation(zs[:, h], bank[:, 4 + h, :], ACT.Silu).then_inc(sems[s + "zs"], 1)
                act.preload_act_table_set(EXP_LN)
                act.wait_ge(sems[s + "proj"], nth(b, s + "proj", 1))
                bc0 = 0 if m == 0 else DTR[1]
                dt0 = BCR if m == 0 else 0
                act.activation(dt_rows[0:DTR[m], :], bank[dt0:dt0 + DTR[m], 0, :], ACT.Copy) \
                    .then_inc(sems[s + "dtrows"], 1)
                act.activation(parts[0:BCR, :], bank[bc0:bc0 + BCR, 0, :], ACT.Copy) \
                    .then_inc(sems[s + "hi"], 1)
                for h in range(HALVES):
                    act.wait_ge(sems[s + "dtp"], nth(b, s + "dtp", h + 1))
                    act.activation(sp_abs[:, h], bank[:, 2 + h, :], ACT.Abs, bias=w["db"][:, h:h + 1]) \
                        .then_inc(sems[s + "spabs"], 1)
                    act.activation(sp_max[:, h], bank[:, 2 + h, :], ACT.Relu, bias=w["db"][:, h:h + 1]) \
                        .then_inc(sems[s + "spmax"], 1)
                act.wait_ge(sems[s + "spabs"], nth(b, s + "spabs", 2))
                act.activation(sp_abs[:], sp_abs[:], ACT.Exp, scale=-1.0).then_inc(sems[s + "spexp"], 1)
                act.wait_ge(sems[s + "spexp"], nth(b, s + "spexp", 1))
                act.activation(sp_abs[:], sp_abs[:], ACT.Ln, bias=one_col[:]).then_inc(sems[s + "spln"], 1)
                act.wait_ge(sems[s + "mid"], nth(b, s + "mid", 1))
                act.activation(parts[BCR:2 * BCR, :], mid[:], ACT.Copy).then_inc(sems[s + "midcopy"], 1)
                act.wait_ge(sems[s + "delta"], nth(b, s + "delta", 1))
                for n in range(STATE):
                    if n >= 2:
                        act.wait_ge(sems[s + "scan"], nth(b, s + "scan", 2 * n - 2))
                    for h in range(HALVES):
                        act.activation(bank[:, 2 + 2 * (n % 2) + h, :], delta[:, h], ACT.Exp,
                                       scale=w["A"][:, h, n:n + 1]).then_inc(sems[s + "dA"], 1)
                    act.wait_ge(sems[s + "cbc"], nth(b, s + "cbc", n + 1))
                    if n >= 2:
                        act.wait_ge(sems[s + "hc"], nth(b, s + "hc", n - 1))
                    act.activation(csb[:, n % 2], bank[:, 1, :], ACT.Copy).then_inc(sems[s + "ccopy"], 1)

            with act.Fori(0, SEQS) as b:
                act.preload_act_table_set(EXP_LN)
                rstd_of(b, "ln0", bank[:, 0, :], "ln0_centered")
                rstd_of(b, "rms0", xl[:], "ln0_done")
                mamba(b, 0)
                rstd_of(b, "rmsA", h0[:], "m0_res")
                act.wait_ge(sems["q_mm"], nth(b, "q_mm", 1))
                act.activation(qs[:], bank[:, 2, :], ACT.Copy, scale=SCALE).then_inc(sems["q_copy"], 1)
                act.wait_ge(sems["v_mm"], nth(b, "v_mm", 1))
                act.activation(vs[:], bank[:, 4, :].rearrange("p (j n) -> p j n", j=QB), ACT.Copy) \
                    .then_inc(sems["v_copy"], 1)

                def copy_probT(i):
                    keys = P * (i % QB + 1)
                    act.wait_ge(sems["probT_mm"], nth(b, "probT_mm", i + 1))
                    if i >= 2:
                        act.wait_ge(sems["pv"], nth(b, "pv", i - 1))
                    act.activation(probT[:, i % 2, 0:keys], bank[:, 4 + i % 2, 0:keys], ACT.Copy) \
                        .then_inc(sems["probT"], 1)

                for i in range(TILES):
                    h, j = i // QB, i % QB
                    keys = P * (j + 1)
                    act.wait_ge(sems["smax"], nth(b, "smax", i + 1))
                    if i >= 2:
                        act.wait_ge(sems["probT_mm"], nth(b, "probT_mm", i - 1))
                    act.activation(prob[:, i % 2, 0:keys], bank[:, 2 + i % 2, 0:keys], ACT.Exp,
                                   bias=nmax[:, i:i + 1], accum_out=psums[:, j, h:h + 1]) \
                        .then_inc(sems["prob"], 1)
                    if i >= 1:
                        copy_probT(i - 1)
                copy_probT(TILES - 1)
                act.wait_ge(sems["attT_mm"], nth(b, "attT_mm", 1))
                act.activation(attT[:], bank[:, 2, :], ACT.Copy).then_inc(sems["attT"], 1)
                rstd_of(b, "rmsF", h1[:], "h1")
                for j, rows in enumerate(FFN_ROWS):
                    act.wait_ge(sems["gate_mm"], nth(b, "gate_mm", j + 1))
                    act.activation(gs[0:rows, j], bank[0:rows, 2 + j % 2, :], ACT.Silu).then_inc(sems["gs"], 1)
                act.preload_act_table_set(EXP_LN)
                rstd_of(b, "ln1", bank[:, 0, :], "ln1_centered")
                for j in range(MH):
                    act.wait_ge(sems["fc_mm"], nth(b, "fc_mm", j + 1))
                    act.activation(gs[:, j], bank[:, 2 + j, :], ACT.Gelu).then_inc(sems["gelu"], 1)
                act.preload_act_table_set(EXP_LN)
                rstd_of(b, "lnH", gc, "gcen", wide=True)
                rstd_of(b, "ln2", bank[:, 0, :], "ln2_centered")
                mamba(b, 1)
                rstd_of(b, "ln3", bank[:, 0, :], "ln3_centered")
                act.wait_ge(sems["lsub"], nth(b, "lsub", 1))
                act.activation(le[:], lg[:], ACT.Exp).then_inc(sems["lexp"], 1)
                act.wait_ge(sems["gateT_mm"], nth(b, "gateT_mm", 1))
                act.activation(gateT[:], bank[0:E, 0, :], ACT.Copy).then_inc(sems["gateT"], 1)
                for e in range(E):
                    act.wait_ge(sems["gbc_mm"], nth(b, "gbc_mm", e + 1))
                    if e >= 2:
                        act.wait_ge(sems["ey"], nth(b, "ey", MB * (e - 1)))
                    act.activation(gbc[:, e % 2], bank[:, 0, :], ACT.Copy).then_inc(sems["gbc"], 1)
                    for j in range(MB):
                        i = e * MB + j
                        act.wait_ge(sems["ea_mm"], nth(b, "ea_mm", i + 1))
                        if i >= 2:
                            act.wait_ge(sems["eg"], nth(b, "eg", i - 1))
                        act.activation(es[:, i % 2], bank[:, 2 + i % 2, :], ACT.Silu).then_inc(sems["es"], 1)

        @block.vector
        def _(dve):
            dve.memset(eps_ln[:], LN_EPS)
            dve.memset(eps_rms[:], RMS_EPS)
            dve.memset(ones[:], 1.0)
            for m in range(2):
                dve.memset(xn[m][:, 0:PAD], 0.0)
            dve.memset(one_col[:], 1.0).then_inc(sems["setup_dve"], 1)
            dve.wait_ge(sems["w_loaded"], ALL_LOADED)
            for m in range(2):
                dve.wait_ge(sems["setup_act"], m + 1)
                w = M[m]
                dve.tensor_scalar(w["A"][:], w["A"][:], -1.0, None, ALU.mult)
                dve.tensor_tensor(w["cw"][:], w["cw"][:], w["winx"][:].unsqueeze(1).to_broadcast([P, TAPS, HALVES * P]),
                                  ALU.mult)
            last = [1]

            def step(ins):
                ins.then_inc(sems["setup_dve"], 1)
                last[0] += 1
                dve.wait_ge(sems["setup_dve"], last[0])

            fcv, prv = fc[:], proj[:].rearrange("p j n -> p (j n)")
            step(dve.tensor_reduce(absr[:, 0:1], fcv, AX.X, ALU.add, apply_absolute_value=True))
            step(dve.tensor_reduce(absr[:, 1:2], prv, AX.X, ALU.add, apply_absolute_value=True))
            dve.wait_ge(sems["setup_pe"], 1)
            half = 0.5 / (MH * P * D)
            step(dve.tensor_scalar(thr[:, 0:2], bank[:, 0, 0:2], half, 0.5 * QUANT_EPS, ALU.mult, ALU.add))
            step(dve.tensor_scalar(thr[:, 2:4], thr[:, 0:2], -1.0, None, ALU.mult))
            for i, v in enumerate((fcv, prv)):
                step(dve.tensor_scalar(qtmp[:], v, thr[:, i:i + 1], None, ALU.is_gt))
                step(dve.tensor_scalar(qtmp2[:], v, thr[:, 2 + i:3 + i], None, ALU.is_lt))
                step(dve.tensor_tensor(v, qtmp[:], qtmp2[:], ALU.subtract))
            for j in range(MH):
                step(dve.tensor_scalar(projw[:, j, :], proj[:, j, :], lnw[:, j:j + 1], None, ALU.mult))
            dve.wait_ge(sems["setup_pe"], 2)
            step(dve.tensor_copy(projb[:], bank[:, 0, 2:3]))
            SETUP_DONE.append(last[0])

            def layer_norm(b, n, dst):
                dve.wait_ge(sems[n + "_rstd"], nth(b, n + "_rstd", 1))
                dve.tensor_tensor(dst, bank[:, 0, :], rstd[:], ALU.mult).then_inc(sems[n + "_done"], 1)

            def rms_norm(b, n, src, weight, dst):
                dve.wait_ge(sems[n + "_rstd"], nth(b, n + "_rstd", 1))
                dve.scalar_tensor_tensor(dst, src, weight[:], rstd[:], ALU.mult, ALU.mult) \
                    .then_inc(sems[n + "_done"], 1)

            def mamba(b, m):
                s, w = f"m{m}_", M[m]
                bc0 = 0 if m == 0 else DTR[1]
                dve.wait_ge(sems[s + "hi"], nth(b, s + "hi", 1))
                dve.tensor_tensor(rest[:], bank[bc0:bc0 + BCR, 0, :], parts[0:BCR, :], ALU.subtract) \
                    .then_inc(sems[s + "rest"], 1)
                dve.wait_ge(sems[s + "rest"], nth(b, s + "rest", 1))
                dve.tensor_copy(mid[:], rest[:]).then_inc(sems[s + "mid"], 1)
                dve.wait_ge(sems[s + "mid"], nth(b, s + "mid", 1))
                dve.tensor_tensor(parts[2 * BCR:3 * BCR, :], rest[:], mid[:], ALU.subtract) \
                    .then_inc(sems[s + "lo"], 1)
                dve.wait_ge(sems[s + "du"], nth(b, s + "du", 1))

                def input_of(n):
                    dve.wait_ge(sems[s + "bbc"], nth(b, s + "bbc", n + 1))
                    dve.tensor_tensor(dbu[:, n % 2], du[:], bank[:, 0:1, :].to_broadcast([P, HALVES, T]),
                                      ALU.mult).then_inc(sems[s + "dbu"], 1)

                input_of(0)
                for n in range(STATE):
                    if n + 1 < STATE:
                        if n >= 1:
                            dve.wait_ge(sems[s + "scan"], nth(b, s + "scan", 2 * n))
                        input_of(n + 1)
                    dve.wait_ge(sems[s + "dbu"], nth(b, s + "dbu", n + 1))
                    if n >= 2:
                        dve.wait_ge(sems[s + "hc"], nth(b, s + "hc", n - 1))
                    for h in range(HALVES):
                        dve.wait_ge(sems[s + "dA"], nth(b, s + "dA", 2 * n + h + 1))
                        dve.tensor_tensor_scan(hst[:, n % 2, h], bank[:, 2 + 2 * (n % 2) + h, :],
                                               dbu[:, n % 2, h], 0.0, ALU.mult, ALU.add) \
                            .then_inc(sems[s + "scan"], 1)
                dve.wait_ge(sems[s + "yacc"], nth(b, s + "yacc", STATE))
                for h in range(HALVES):
                    dve.scalar_tensor_tensor(yd[:, h], xs[:, h], w["dskip"][:, h:h + 1], bank[:, 6 + h, :],
                                             ALU.mult, ALU.add).then_inc(sems[s + "yd"], 1)
                dve.wait_ge(sems[s + "out"], nth(b, s + "out", 1))
                dve.tensor_tensor((h0 if m == 0 else x3)[:], bank[:, 0, :], (xl if m == 0 else x2)[:],
                                  ALU.add).then_inc(sems[s + "res"], 1)

            with dve.Fori(0, SEQS) as b:
                layer_norm(b, "ln0", xl[:])
                rms_norm(b, "rms0", xl[:], norm_m, xn[0][:, PAD:])
                mamba(b, 0)
                rms_norm(b, "rmsA", h0[:], norm_a, nrm[:])
                dve.wait_ge(sems["k_mm"], nth(b, "k_mm", 1))
                dve.tensor_copy(ks[:], bank[:, 3, :]).then_inc(sems["k_copy"], 1)
                for i in range(TILES):
                    keys = P * (i % QB + 1)
                    dve.wait_ge(sems["score"], nth(b, "score", i + 1))
                    dve.tensor_reduce(nmax[:, i:i + 1], bank[:, 2 + i % 2, 0:keys], AX.X, ALU.max,
                                      negate=True).then_inc(sems["smax"], 1)
                dve.wait_ge(sems["prob"], nth(b, "prob", TILES))
                dve.reciprocal(rsums[:], psums[:]).then_inc(sems["recip"], 1)
                dve.wait_ge(sems["recip"], nth(b, "recip", 1))
                dve.wait_ge(sems["pv"], nth(b, "pv", TILES))
                dve.tensor_tensor(att[:].rearrange("p j (h n) -> p (j h) n", h=N_HEADS),
                                  bank[:, 6, :].rearrange("p (j n) -> p j n", n=HD),
                                  rsums[:].rearrange("p j h -> p (j h)").unsqueeze(2).to_broadcast(
                                      [P, QB * N_HEADS, HD]), ALU.mult).then_inc(sems["att"], 1)
                dve.wait_ge(sems["o_mm"], nth(b, "o_mm", 1))
                dve.tensor_tensor(h1[:], bank[:, 0, :], h0[:], ALU.add).then_inc(sems["h1"], 1)
                rms_norm(b, "rmsF", h1[:], norm_f, nrm[:])
                for j, rows in enumerate(FFN_ROWS):
                    dve.wait_ge(sems["gs"], nth(b, "gs", j + 1))
                    dve.wait_ge(sems["up_mm"], nth(b, "up_mm", j + 1))
                    dve.tensor_tensor(gc[0:rows, j], gs[0:rows, j], bank[0:rows, 4 + j % 2, :], ALU.mult) \
                        .then_inc(sems["gu"], 1)
                dve.wait_ge(sems["down_mm"], nth(b, "down_mm", 1))
                dve.tensor_tensor(h0[:], bank[:, 0, :], h1[:], ALU.add).then_inc(sems["ffn_res"], 1)
                layer_norm(b, "ln1", nrm[:])
                dve.wait_ge(sems["gmean"], nth(b, "gmean", 1))
                dve.tensor_tensor(gc, gs, bank[:, 0:1, :].to_broadcast([P, MH, T]), ALU.subtract) \
                    .then_inc(sems["gcen"], 1)
                dve.wait_ge(sems["pj_mm"], nth(b, "pj_mm", 1))
                dve.wait_ge(sems["lnH_rstd"], nth(b, "lnH_rstd", 1))
                dve.tensor_tensor(h1[:], bank[:, 0, :], rstd[:], ALU.mult).then_inc(sems["pj_scaled"], 1)
                dve.wait_ge(sems["pj_scaled"], nth(b, "pj_scaled", 1))
                dve.scalar_tensor_tensor(x2[:], h1[:], projb[:], x1[:], ALU.add, ALU.add) \
                    .then_inc(sems["pj_bias"], 1)
                layer_norm(b, "ln2", xn[1][:, PAD:])
                mamba(b, 1)
                layer_norm(b, "ln3", nrm[:])
                dve.wait_ge(sems["logit_mm"], nth(b, "logit_mm", 1))
                logits = bank[:, 2, 0:QB * E].rearrange("p (j e) -> p j e", e=E)
                dve.tensor_reduce(lmax[:], logits, AX.X, ALU.max).then_inc(sems["lmax"], 1)
                dve.wait_ge(sems["lmax"], nth(b, "lmax", 1))
                dve.tensor_tensor(lg[:], logits, lmax[:].unsqueeze(2).to_broadcast([P, QB, E]),
                                  ALU.subtract).then_inc(sems["lsub"], 1)
                dve.wait_ge(sems["lsub"], nth(b, "lsub", 1))
                dve.tensor_scalar(eqm[:], lg[:], 0.0, None, ALU.is_ge).then_inc(sems["eqm"], 1)
                dve.wait_ge(sems["eqm"], nth(b, "eqm", 1))
                dve.tensor_tensor(cand[:], eqm[:], eminus[:], ALU.mult).then_inc(sems["cand"], 1)
                dve.wait_ge(sems["cand"], nth(b, "cand", 1))
                dve.tensor_reduce(first[:], cand[:], AX.X, ALU.min).then_inc(sems["first"], 1)
                dve.wait_ge(sems["first"], nth(b, "first", 1))
                dve.tensor_tensor(onehot[:], eminus[:], first[:].unsqueeze(2).to_broadcast([P, QB, E]),
                                  ALU.is_equal).then_inc(sems["onehot"], 1)
                dve.wait_ge(sems["lexp"], nth(b, "lexp", 1))
                dve.tensor_reduce(lsum[:], le[:], AX.X, ALU.add).then_inc(sems["lsum"], 1)
                dve.wait_ge(sems["lsum"], nth(b, "lsum", 1))
                dve.reciprocal(lprob[:], lsum[:]).then_inc(sems["lprob"], 1)
                dve.wait_ge(sems["lprob"], nth(b, "lprob", 1))
                dve.wait_ge(sems["onehot"], nth(b, "onehot", 1))
                dve.tensor_tensor(gate[:], onehot[:], lprob[:].unsqueeze(2).to_broadcast([P, QB, E]),
                                  ALU.mult).then_inc(sems["gate"], 1)
                for e in range(E):
                    for j in range(MB):
                        i = e * MB + j
                        dve.wait_ge(sems["es"], nth(b, "es", i + 1))
                        dve.wait_ge(sems["eg_mm"], nth(b, "eg_mm", i + 1))
                        dve.tensor_tensor(eg[:, i % 2], es[:, i % 2], bank[:, 4 + i % 2, :], ALU.mult) \
                            .then_inc(sems["eg"], 1)
                        dve.wait_ge(sems["eg"], nth(b, "eg", i + 1))
                        dve.wait_ge(sems["gbc"], nth(b, "gbc", e + 1))
                        if i >= 2:
                            dve.wait_ge(sems["ew2"], nth(b, "ew2", i - 1))
                        dve.tensor_tensor(ey[:, i % 2], eg[:, i % 2], gbc[:, e % 2], ALU.mult) \
                            .then_inc(sems["ey"], 1)
                dve.wait_ge(sems["ew2"], nth(b, "ew2", E * MB))
                dve.tensor_tensor(outs[:], bank[:, 6, :], x3[:], ALU.add).then_inc(sems["outs_ready"], 1)

        @block.tensor
        def _(pe):
            def mm(dst, lhsT, rhs, start=True, stop=True):
                return pe.matmul(dst, lhsT, rhs, start=start, stop=stop)

            pe.wait_ge(sems["w_loaded"], ALL_LOADED)
            pe.wait_ge(sems["setup_dve"], 3)
            mm(bank[:, 0, 0:2], ones[:], absr[:]).then_inc(sems["setup_pe"], 1)
            pe.wait_ge(sems["setup_dve"], SETUP_DONE[0] - 1)
            for j in range(MH):
                last = mm(bank[:, 0, 2:3], proj[:, j, :], lnb[:, j:j + 1], j == 0, j == MH - 1)
            last.then_inc(sems["setup_pe"], 1)
            pe.wait_ge(sems["setup_dve"], SETUP_DONE[0])

            def centered(b, n, src):
                mm(bank[:, 0, :], center[:], src).then_inc(sems[n + "_centered"], 1)

            def variance(b, n):
                pe.wait_ge(sems[n + "_squared"], nth(b, n + "_squared", 1))
                mm(bank[:, 1, :], mean_d[:], sq[:]).then_inc(sems[n + "_var"], 1)

            def mamba(b, m):
                s, w = f"m{m}_", M[m]
                for h in range(HALVES):
                    for k in range(TAPS):
                        last = mm(bank[:, 2 + h, :], w["cw"][:, k, P * h:P * h + P], xn[m][:, k:k + T],
                                  k == 0, k == TAPS - 1)
                    last.then_inc(sems[s + "conv"], 1)
                for h in range(HALVES):
                    mm(bank[:, 4 + h, :], w["wz"][:, P * h:P * h + P], xn[m][:, PAD:]) \
                        .then_inc(sems[s + "z"], 1)
                rows = DTR[m] + BCR
                for h in range(HALVES):
                    pe.wait_ge(sems[s + "xs"], nth(b, s + "xs", h + 1))
                    last = mm(bank[0:rows, 0, :], w["wx"][:, h, :], xs[:, h], h == 0, h == HALVES - 1)
                last.then_inc(sems[s + "proj"], 1)
                pe.wait_ge(sems[s + "dtrows"], nth(b, s + "dtrows", 1))
                for h in range(HALVES):
                    mm(bank[:, 2 + h, :], w["wdt"][:, P * h:P * h + P], dt_rows[0:DTR[m], :]) \
                        .then_inc(sems[s + "dtp"], 1)
                pe.wait_ge(sems[s + "hi"], nth(b, s + "hi", 1))
                pe.wait_ge(sems[s + "midcopy"], nth(b, s + "midcopy", 1))
                pe.wait_ge(sems[s + "lo"], nth(b, s + "lo", 1))

                def accumulate(n):
                    pe.wait_ge(sems[s + "hc"], nth(b, s + "hc", n + 1))
                    for h in range(HALVES):
                        last = mm(bank[:, 6 + h, :], ident[:], hc[:, n % 2, h], n == 0, n == STATE - 1)
                    last.then_inc(sems[s + "yacc"], 1)

                for n in range(STATE):
                    if n >= 1:
                        pe.wait_ge(sems[s + "dbu"], nth(b, s + "dbu", n))
                    mm(bank[:, 0, :], pick[:, n, :], parts[:]).then_inc(sems[s + "bbc"], 1)
                    if n >= 1:
                        pe.wait_ge(sems[s + "ccopy"], nth(b, s + "ccopy", n))
                    mm(bank[:, 1, :], pick[:, STATE + n, :], parts[:]).then_inc(sems[s + "cbc"], 1)
                    if n >= 2:
                        accumulate(n - 2)
                accumulate(STATE - 2)
                accumulate(STATE - 1)
                pe.wait_ge(sems[s + "yg"], nth(b, s + "yg", 1))
                for h in range(HALVES):
                    last = mm(bank[:, 0, :], w["wo"][:, h, :], yd[:, h], h == 0, h == HALVES - 1)
                last.then_inc(sems[s + "out"], 1)

            with pe.Fori(0, SEQS) as b:
                pe.wait_ge(sems["io"], nth(b, "io", 16))
                centered(b, "ln0", xin[:])
                variance(b, "ln0")
                variance(b, "rms0")
                pe.wait_ge(sems["rms0_done"], nth(b, "rms0_done", 1))
                mamba(b, 0)
                variance(b, "rmsA")
                pe.wait_ge(sems["rmsA_done"], nth(b, "rmsA_done", 1))
                mm(bank[:, 2, :], wq[:], nrm[:]).then_inc(sems["q_mm"], 1)
                mm(bank[:, 3, :], wk[:], nrm[:]).then_inc(sems["k_mm"], 1)
                for j in range(QB):
                    last = mm(bank[:, 4, P * j:P * j + P], nrm[:, P * j:P * j + P], wv[:])
                last.then_inc(sems["v_mm"], 1)
                pe.wait_ge(sems["q_copy"], nth(b, "q_copy", 1))
                pe.wait_ge(sems["k_copy"], nth(b, "k_copy", 1))
                pe.wait_ge(sems["v_copy"], nth(b, "v_copy", 1))

                def scores(i):
                    h, j = i // QB, i % QB
                    if i >= 2:
                        pe.wait_ge(sems["prob"], nth(b, "prob", i - 1))
                    hd = slice(HD * h, HD * h + HD)
                    pe.matmul(bank[:, 2 + i % 2, 0:P * (j + 1)], qs[hd, P * j:P * j + P], ks[hd, 0:P * (j + 1)],
                              start=True, stop=False)
                    pe.matmul(bank[:, 2 + i % 2, P * j:P * j + P], ident[:], causal[:], start=False, stop=True) \
                        .then_inc(sems["score"], 1)

                def weigh(i):
                    h, j = i // QB, i % QB
                    pe.wait_ge(sems["prob"], nth(b, "prob", i + 1))
                    if i >= 2:
                        pe.wait_ge(sems["probT"], nth(b, "probT", i - 1))
                    for k in range(j + 1):
                        last = pe.transpose(bank[:, 4 + i % 2, P * k:P * k + P], prob[:, i % 2, P * k:P * k + P],
                                            ident[:])
                    last.then_inc(sems["probT_mm"], 1)

                def attend(i):
                    h, j = i // QB, i % QB
                    g = slice(HD * h, HD * h + HD)
                    pe.wait_ge(sems["probT"], nth(b, "probT", i + 1))
                    for k in range(j + 1):
                        last = mm(bank[:, 6, D * j + HD * h:D * j + HD * h + HD],
                                  probT[:, i % 2, P * k:P * k + P], vs[:, k, g], k == 0, k == j)
                    last.then_inc(sems["pv"], 1)

                for i in range(TILES + 2):
                    if i < TILES:
                        scores(i)
                    if 1 <= i <= TILES:
                        weigh(i - 1)
                    if i >= 2:
                        attend(i - 2)
                pe.wait_ge(sems["att"], nth(b, "att", 1))
                for j in range(QB):
                    last = pe.transpose(bank[:, 2, P * j:P * j + P], att[:, j, :], ident[:])
                last.then_inc(sems["attT_mm"], 1)
                pe.wait_ge(sems["attT"], nth(b, "attT", 1))
                mm(bank[:, 0, :], wo[:], attT[:]).then_inc(sems["o_mm"], 1)
                variance(b, "rmsF")
                pe.wait_ge(sems["rmsF_done"], nth(b, "rmsF_done", 1))
                for j, rows in enumerate(FFN_ROWS):
                    if j >= 2:
                        pe.wait_ge(sems["gu"], nth(b, "gu", j - 1))
                    mm(bank[0:rows, 2 + j % 2, :], wgate[:, P * j:P * j + rows], nrm[:]) \
                        .then_inc(sems["gate_mm"], 1)
                    mm(bank[0:rows, 4 + j % 2, :], wup[:, P * j:P * j + rows], nrm[:]) \
                        .then_inc(sems["up_mm"], 1)
                for j, rows in enumerate(FFN_ROWS):
                    pe.wait_ge(sems["gu"], nth(b, "gu", j + 1))
                    last = mm(bank[:, 0, :], wdown[0:rows, j, :], gc[0:rows, j], j == 0, j == FB - 1)
                last.then_inc(sems["down_mm"], 1)
                pe.wait_ge(sems["x1"], nth(b, "x1", 1))
                centered(b, "ln1", x1[:])
                variance(b, "ln1")
                pe.wait_ge(sems["ln1_done"], nth(b, "ln1_done", 1))
                for j in range(MH):
                    mm(bank[:, 2 + j, :], fc[:, P * j:P * j + P], nrm[:]).then_inc(sems["fc_mm"], 1)
                for j in range(MH):
                    pe.wait_ge(sems["gelu"], nth(b, "gelu", j + 1))
                    last = mm(bank[:, 0, :], mean_h[:], gs[:, j], j == 0, j == MH - 1)
                last.then_inc(sems["gmean"], 1)
                pe.wait_ge(sems["lnH_squared"], nth(b, "lnH_squared", 1))
                for j in range(MH):
                    last = mm(bank[:, 1, :], mean_h[:], gs[:, j], j == 0, j == MH - 1)
                last.then_inc(sems["lnH_var"], 1)
                for j in range(MH):
                    last = mm(bank[:, 0, :], projw[:, j, :], gc[:, j], j == 0, j == MH - 1)
                last.then_inc(sems["pj_mm"], 1)
                pe.wait_ge(sems["pj_bias"], nth(b, "pj_bias", 1))
                centered(b, "ln2", x2[:])
                variance(b, "ln2")
                pe.wait_ge(sems["ln2_done"], nth(b, "ln2_done", 1))
                mamba(b, 1)
                pe.wait_ge(sems["m1_res"], nth(b, "m1_res", 1))
                centered(b, "ln3", x3[:])
                variance(b, "ln3")
                pe.wait_ge(sems["ln3_done"], nth(b, "ln3_done", 1))
                for j in range(QB):
                    mm(bank[:, 2, E * j:E * j + E], nrm[:, P * j:P * j + P], router[:], True, False)
                    last = mm(bank[:, 2, E * j:E * j + E], ones[0:1, :], router_b[:], False, True)
                last.then_inc(sems["logit_mm"], 1)
                pe.wait_ge(sems["gate"], nth(b, "gate", 1))
                for j in range(QB):
                    last = pe.transpose(bank[0:E, 0, P * j:P * j + P], gate[:, j, :], ident[:])
                last.then_inc(sems["gateT_mm"], 1)
                pe.wait_ge(sems["gateT"], nth(b, "gateT", 1))

                def down(i):
                    pe.wait_ge(sems["ey"], nth(b, "ey", i + 1))
                    mm(bank[:, 6, :], w2[:, i // MB, i % MB, :], ey[:, i % 2], i == 0, i == E * MB - 1) \
                        .then_inc(sems["ew2"], 1)

                for e in range(E):
                    if e >= 1:
                        pe.wait_ge(sems["gbc"], nth(b, "gbc", e))
                    mm(bank[:, 0, :], rowpick[:, e, :], gateT[:]).then_inc(sems["gbc_mm"], 1)
                    for j in range(MB):
                        i = e * MB + j
                        if i >= 2:
                            pe.wait_ge(sems["eg"], nth(b, "eg", i - 1))
                        mm(bank[:, 2 + i % 2, :], w1[:, e, P * j:P * j + P], nrm[:]) \
                            .then_inc(sems["ea_mm"], 1)
                        mm(bank[:, 4 + i % 2, :], w1[:, e, MOE_H + P * j:MOE_H + P * j + P], nrm[:]) \
                            .then_inc(sems["eg_mm"], 1)
                        if i >= 2:
                            down(i - 2)
                down(E * MB - 2)
                down(E * MB - 1)


SETUP_DONE = []


def kernel(**a):
    import numpy as np
    import concourse.bacc as bacc
    from concourse import mybir
    from concourse.bass_utils import run_bass_kernel_spmd

    a = {k: np.asarray(v) for k, v in a.items()}
    x = a["L0_attn_x"]
    SEQS, T, D = x.shape
    f32 = np.float32
    half_cols = lambda v: v.reshape(2, 128).T

    def rows(v, order):
        return v[order]

    STATE, E, QB, BCR = 16, 8, T // 128, 32
    xp = a["L0_attn_x_proj_w"]
    eye = np.eye(128, dtype=f32)
    pick = np.zeros((3 * BCR, BCR, 128), f32)
    for part in range(3):
        for n in range(BCR):
            pick[part * BCR + n, n, :] = 1
    rowpick = np.zeros((E, E, 128), f32)
    for e in range(E):
        rowpick[e, e, :] = 1
    heads = np.repeat(np.arange(2), 2)

    def per_head(w):
        return w.reshape(2, 32, D)[heads].reshape(128, D).T

    put = {
        "xT": x.transpose(0, 2, 1),
        "ident": eye, "center": eye - f32(1 / 128), "mean_d": np.full((128, 128), 1 / 128, f32),
        "mean_h": np.full((128, 128), 1 / 512, f32),
        "causal": np.triu(np.full((128, 128), -1e30, f32), 1),
        "pick": pick, "rowpick": rowpick,
        "eminus": np.broadcast_to(np.arange(E, dtype=f32) - E, (128, QB, E)),
        "norm_m": a["L0_attn_norm_m_w"][:, None], "norm_a": a["L0_attn_norm_attn_w"][:, None],
        "norm_f": a["L0_attn_norm_ffn_w"][:, None],
        "m0_win": a["L0_attn_in_proj_w"].T, "m0_cw": a["L0_attn_conv_w"][:, 0, :].T,
        "m0_cb": half_cols(a["L0_attn_conv_b"]), "m0_wx": xp.T, "m0_dtT": a["L0_attn_dt_w"].T,
        "m0_db": half_cols(a["L0_attn_dt_b"]), "m0_Alog": a["L0_attn_A_log"].reshape(2, 128, STATE),
        "m0_D": half_cols(a["L0_attn_D_skip"]), "m0_wo": a["L0_attn_out_proj_w"].T,
        "m1_win": a["L1_attn_W_in"], "m1_cw": a["L1_attn_conv_w"][:, 0, :],
        "m1_cb": half_cols(a["L1_attn_conv_b"]), "m1_wx": a["L1_attn_W_x"], "m1_dtT": a["L1_attn_W_dt"],
        "m1_db": half_cols(a["L1_attn_b_dt"]), "m1_Alog": a["L1_attn_A_log"].reshape(2, 128, STATE),
        "m1_D": half_cols(a["L1_attn_D"]), "m1_wo": a["L1_attn_W_out"],
        "qT": a["L0_attn_q_w"].T, "kT": per_head(a["L0_attn_k_w"]), "vT": per_head(a["L0_attn_v_w"]),
        "oT": a["L0_attn_o_w"].T, "gateT": a["L0_attn_gate_w"].T, "upT": a["L0_attn_up_w"].T,
        "downT": a["L0_attn_down_w"].T, "fcT": a["L0_ffn_W_fc"].T, "projT": a["L0_ffn_W_proj"].T,
        "lnw": a["L0_ffn_ln_w"].reshape(4, 128).T, "lnb": a["L0_ffn_ln_b"].reshape(4, 128).T,
        "router": a["L1_ffn_router_w"], "router_b": a["L1_ffn_router_b"][None, :],
        "w1": a["L1_ffn_w1"], "w2": a["L1_ffn_w2"],
    }
    bf = mybir.dt.np(mybir.dt.bfloat16) if hasattr(mybir.dt, "np") else None
    import ml_dtypes
    put["pick"] = put["pick"].astype(ml_dtypes.bfloat16)
    nc = bacc.Bacc("TRN2", target_bir_lowering=False, num_devices=1)
    arrays, dram = {}, {}
    for name, v in put.items():
        v = np.ascontiguousarray(v)
        arrays["in_" + name] = v
        dram[name] = nc.dram_tensor("in_" + name, v.shape, mybir.dt.from_np(v.dtype), kind="ExternalInput").ap()
    out = nc.dram_tensor("out_xT", (SEQS, D, T), mybir.dt.float32, kind="ExternalOutput").ap()
    build(nc, dram, out)
    r = run_bass_kernel_spmd(nc, [arrays], core_ids=[0])
    return r.results[0]["out_xT"].transpose(0, 2, 1)
```

```python
from contextlib import ExitStack

import concourse.bass as bass
from concourse import mybir

P = 128
F32 = mybir.dt.float32
BF16 = mybir.dt.bfloat16
ALU = mybir.AluOpType
ACT = mybir.ActivationFunctionType
AX = mybir.AxisListType

LN_EPS = 1e-5
RMS_EPS = 1e-6
QUANT_EPS = 1e-6
N_HEADS = 4
EXP_LN = "natural_log_exp_and_others"

PAIR_EVERY = 16

HBUF = 3
CBUF = 3
YLAG = 3

PER = {}
SETUP_DONE = []


def build(nc, d, sorted_rows, out):
    SEQS, D, T = d["xT"].shape
    TAPS = d["m0_cw"].shape[0]
    PAD = TAPS - 1
    STATE = d["m0_Alog"].shape[2]
    HALVES = d["m0_Alog"].shape[0]
    FFN_H = d["gateT"].shape[1]
    FB = (FFN_H + P - 1) // P
    FFN_ROWS = [min(P, FFN_H - P * j) for j in range(FB)]
    MH = d["fcT"].shape[1] // P
    E = d["w1"].shape[0]
    MOE_H = d["w2"].shape[1]
    MB = MOE_H // P
    QB = T // P
    HD = D // N_HEADS
    SCALE = float(HD) ** -0.5
    BCR = 2 * STATE
    G = SEQS * QB
    NT = d["blank"].shape[0] // P
    ROW = d["blank"].shape[1]
    MEAN, RSTD, PROB, TOKEN = D, D + 1, D + 2, D + 3
    DTR = {0: 1, 1: d["m1_dtT"].shape[0]}
    assert D == P and T == 512 and HALVES == 2

    with ExitStack() as ctx:
        def sb(name, shape, dt=F32):
            return ctx.enter_context(nc.sbuf_tensor(name, shape, dt))

        bank = ctx.enter_context(nc.psum_tensor("bank", [P, 8, T], F32))
        sems = {}

        def new_sem(name, per=1, uses=("",)):
            handle = ctx.enter_context(nc.semaphore(name))
            for i, use in enumerate(uses):
                sems[use + name] = handle
                PER[use + name] = per * len(uses)
                BEFORE[use + name] = per * i

        ident = sb("ident", [P, P])
        center = sb("center", [P, P])
        mean_d = sb("mean_d", [P, P])
        mean_h = sb("mean_h", [P, P])
        ones = sb("ones", [P, P])
        causal = sb("causal", [P, P], BF16)
        pick = sb("pick", [3 * BCR, BCR, P], BF16)
        eminus = sb("eminus", [P, E])
        token_id = sb("token_id", [P, G])
        earlier = sb("earlier", [P, P])
        new_expert = sb("new_expert", [P, E, G])
        tile_starts = sb("tile_starts", [P, G])
        tile_id = sb("tile_id", [P, NT])
        ident16 = sb("ident16", [P, P], BF16)
        eps_ln = sb("eps_ln", [P, 1])
        eps_rms = sb("eps_rms", [P, 1])
        one_col = sb("one_col", [P, 1])
        M = []
        for m in range(2):
            M.append(dict(
                cw=sb(f"m{m}_cw_s", [P, TAPS, HALVES * P]),
                wz=sb(f"m{m}_wz_s", [P, HALVES * P]), cb=sb(f"m{m}_cb_s", [P, HALVES]),
                wx=sb(f"m{m}_wx_s", [P, HALVES, DTR[m] + BCR]), wdt=sb(f"m{m}_wdt_s", [DTR[m], HALVES * P]),
                db=sb(f"m{m}_db_s", [P, HALVES]), A=sb(f"m{m}_A_s", [P, HALVES, STATE]),
                dskip=sb(f"m{m}_dskip_s", [P, HALVES]), wo=sb(f"m{m}_wo_s", [P, HALVES, D])))
        norm_m = sb("norm_m", [P, 1])
        norm_a = sb("norm_a", [P, 1])
        norm_f = sb("norm_f", [P, 1])
        wq = sb("wq", [P, D])
        wk = sb("wk", [P, D])
        wv = sb("wv", [P, D])
        wo = sb("wo", [P, D])
        wgate = sb("wgate", [P, FFN_H])
        wup = sb("wup", [P, FFN_H])
        wdown = sb("wdown", [P, FB, D])
        fc = sb("fc", [P, MH * P])
        proj = sb("proj", [P, MH, D])
        lnw = sb("lnw", [P, MH])
        lnb = sb("lnb", [P, MH])
        projw = sb("projw", [P, MH, D])
        projb = sb("projb", [P, 1])
        router = sb("router", [P, E])
        router_b = sb("router_b", [P, E])
        w1 = sb("w1", [P, E, 2 * MOE_H])
        w2 = sb("w2", [P, E, MB, D])

        xin = sb("xin", [P, T])
        xl = sb("xl", [P, T])
        xn = [sb(f"xn{m}", [P, PAD + T]) for m in range(2)]
        rstd_m = sb("rstd_m", [P, T])
        xs = sb("xs", [P, HALVES, T])
        zs = sb("zs", [P, HALVES, T])
        dt_rows = sb("dt_rows", [DTR[1], T])
        parts = sb("parts", [3 * BCR, T], BF16)
        rest = sb("rest", [BCR, T])
        mid = sb("mid", [BCR, T], BF16)
        delta = sb("delta", [P, HALVES, T])
        du = sb("du", [P, HALVES, T])
        yd = du
        dbu = sb("dbu", [P, 2, HALVES, T])
        hst = sb("hst", [P, HBUF, HALVES, T])
        sp_abs, sp_max = hst[:, 0], hst[:, 1]
        hc = sb("hc", [P, 4, HALVES, T])
        csb = sb("csb", [P, CBUF, T])
        winx = [hst[:, 0, 0, 0:HALVES * P], hst[:, 1, 0, 0:HALVES * P]]
        xkeep = sb("xkeep", [P, T])
        h0 = sb("h0", [P, T])
        nrm = sb("nrm", [P, T])
        rstd_d = sb("rstd_d", [P, T])
        qs = sb("qs", [P, T])
        ks = sb("ks", [P, T])
        vs = sb("vs", [P, QB, D])
        nmax = sb("nmax", [P, N_HEADS * QB])
        psums = sb("psums", [P, QB, N_HEADS])
        rsums = sb("rsums", [P, QB, N_HEADS])
        attT = qs
        h1 = sb("h1", [P, T])
        gs = sb("gs", [P, 4, T])
        gc = sb("gc", [P, 4, T])
        prob, probT = gs, gc
        x1 = sb("x1", [P, T])
        att = x1[:].rearrange("p (j n) -> p j n", j=QB)
        x2 = sb("x2", [P, T])
        x3 = sb("x3", [P, SEQS, T])
        router_c = sb("router_c", [P, E])
        carved = [0]

        def in_gc(*dims):
            size = 1
            for n in dims:
                size *= n
            at = carved[0]
            carved[0] += size
            flat_tile = gc[:].rearrange("p j t -> p (j t)")[:, at:at + size]
            return flat_tile.rearrange("p (a b) -> p a b", b=dims[1]) if len(dims) == 2 else flat_tile

        stats = sb("stats", [P, G, 6])
        meanvar = sb("meanvar", [P, G, 2])
        lg = in_gc(G, E)
        lmax = sb("lmax", [P, G])
        le = in_gc(G, E)
        lsum = sb("lsum", [P, G])
        cand = in_gc(G, E)
        first = sb("first", [P, G])
        onehot = in_gc(E, G)
        upto = in_gc(E, G)
        place = in_gc(E, G)
        starts = in_gc(E, G)
        tiles_of = sb("tiles_of", [P, E])
        tiles_upto = sb("tiles_upto", [P, E])
        tiles_before = sb("tiles_before", [P, E])
        row_f = sb("row_f", [P, G])
        row_of = sb("row_of", [P, G], mybir.dt.uint32)
        past = in_gc(NT, E)
        expert_f = sb("expert_f", [P, NT])
        expert_of = sb("expert_of", [P, NT], mybir.dt.int32)
        target = sb("target", [P, 2], mybir.dt.uint32)
        trows = hc[:].rearrange("p a h t -> p (a h t)")[:, 0:G * ROW].rearrange("p (g w) -> p g w", w=ROW)
        srows = hc[:].rearrange("p a h t -> p (a h t)")[:, 0:NT * ROW].rearrange("p (g w) -> p g w", w=ROW)
        nrow = gs[:, 0, 0:2 * D].rearrange("p (s n) -> p s n", s=2)
        xT = gs[:, 1, 0:2 * P].rearrange("p (s n) -> p s n", s=2)
        orow = gs[:, 2, 0:2 * D].rearrange("p (s n) -> p s n", s=2)
        es, ey, eyT = delta, du, xs
        absr = sb("absr", [P, 2])
        thr = sb("thr", [P, 4])
        qtmp, qtmp2 = x1, x2

        MBANK, DBANK = 0, 6
        GROUPS, n = [], 0
        while n < STATE:
            size = 2 if n % PAIR_EVERY == 0 and n + 1 < STATE else 1
            GROUPS.append(tuple(range(n, n + size)))
            n += size
        GROUP_OF = [g for g, group in enumerate(GROUPS) for _ in group]
        PAIRS_UP_TO = [sum(len(x) == 2 for x in GROUPS[:g + 1]) for g in range(len(GROUPS))]
        TILES = N_HEADS * QB
        for name, per in (
                ("early_loaded", 0), ("late_loaded", 0), ("folded", 0), ("setup_dve", 0), ("setup_act", 0), ("setup_pe", 0),
                ("x_loaded", 16), ("even_stored", 16), ("odd_stored", 16), ("xkeep", 1),
                ("ln_centered", 1), ("ln_squared", 1), ("ln_var", 1), ("ln_logged", 1), ("ln_rstd", 1), ("ln_done", 1),
                ("rms_squared", 1), ("rms_var", 1), ("rms_logged", 1), ("rms_rstd", 1), ("rms_done", 1),
                ("dn_squared", 1), ("dn_var", 1), ("dn_logged", 1), ("dn_rstd", 1), ("dn_done", 1), ("dn_centered", 1),
                ("conv", 2), ("z", 2), ("xs", 2), ("zs", 2), ("proj", 1), ("dtrows", 1),
                ("hi", 1), ("rest", 1), ("mid", 1), ("midcopy", 1), ("lo", 1), ("dtp", 2),
                ("spabs", 2), ("spmax", 2), ("spexp", 1), ("spln", 1), ("delta", 1), ("du", 1),
                ("bbc", STATE), ("cbc", STATE), ("dA", 2 * STATE), ("ccopy", STATE),
                ("dbu", STATE), ("scan", 2 * STATE), ("hc", STATE), ("pair", PAIRS_UP_TO[-1]), ("yacc", len(GROUPS)),
                ("yd", 2), ("yg", 2), ("out", 1), ("res", 1),
                ("q_mm", 1), ("k_mm", 1), ("v_mm", 1), ("q_copy", 1), ("k_copy", 1), ("v_copy", 1),
                ("score", TILES), ("smax", TILES), ("prob", TILES), ("probT_mm", TILES),
                ("probT", TILES), ("pv", TILES), ("pv_copy", TILES), ("recip", 1), ("att", 1), ("attT_mm", 1),
                ("attT", 1), ("o_mm", 1), ("h1", 1),
                ("gate_mm", FB), ("up_mm", FB), ("gs", FB), ("gu", FB), ("down_mm", 1),
                ("ffn_res", 1), ("x1", 1),
                ("fc_mm", MH), ("gelu", MH), ("gmean", 1), ("gcen", 1), ("pj_mm", 1), ("pj_scaled", 1),
                ("x2", 1),
("router_mm", 1), ("router_c", 1), ("xrow_mm", SEQS), ("xrow", SEQS), ("logit_mm", 1), ("stats", G),
                ("meanvar", G), ("mlog", 1), ("rstd", 1), ("lscaled", 1), ("lbiased", 1), ("lmax", 1), ("lsub", 1),
                ("lexp", 1), ("lsum", 1), ("eqm", 1), ("cand", 1), ("first", 1), ("onehot", 1), ("count_mm", 1),
                ("route", 0), ("rows_made", 0), ("row_of", 1), ("experts", 1), ("scattered", 16), ("blanked", 16),
                ("srows_first", 16), ("srows_rest", 16),
                ("nrow", 1), ("xT_mm", 1), ("xT", 1), ("ea_mm", 1), ("eg_mm", 1), ("es", 1), ("ey", 1),
                ("eyT_mm", 1), ("eyT", 1), ("down_e", 1), ("target", 1), ("orow", 1)):
            PER[name] = per
            sems[name] = ctx.enter_context(nc.semaphore(name))

        def nth(i, name, k=1):
            return i * PER[name] + k

        STORED = ("even_stored", "odd_stored")
        FIRST_TILES = 4
        HEAD = 6
        SIDE_STEPS = HEAD + STATE
        TILE0 = 3

        def seq(t, k):
            return t[:, k, :] if isinstance(k, int) else t[:, bass.ds(k, 1), :].rearrange("p o t -> p (o t)")

        early, late = [], []
        early += [(dst[:], d[key]) for dst, key in ((center, "center"), (mean_d, "mean_d"), (norm_m, "norm_m"))]
        for m in range(2):
            early.append((winx[m], d[f"m{m}_win"][:, 0:HALVES * P]))
            for k in range(TAPS):
                early.append((M[m]["cw"][:, k, :], d[f"m{m}_cw"][k:k + 1, :].to_broadcast([P, HALVES * P])))
            early.append((M[m]["wz"][:], d[f"m{m}_win"][:, HALVES * P:]))
            early.append((M[m]["cb"][:], d[f"m{m}_cb"]))
            early.append((M[m]["wx"][:], d[f"m{m}_wx"].rearrange("(h p) n -> p h n", p=P)))
            early.append((M[m]["wdt"][:], d[f"m{m}_dtT"]))
            early.append((M[m]["db"][:], d[f"m{m}_db"]))
            early.append((M[m]["A"][:], d[f"m{m}_Alog"].rearrange("h p n -> p h n")))
            early.append((M[m]["dskip"][:], d[f"m{m}_D"]))
            early.append((M[m]["wo"][:], d[f"m{m}_wo"].rearrange("(h p) n -> p h n", p=P)))
        early += [(pick[:], d["pick"]), (ident[:], d["ident"])]
        late += [(dst[:], d[key]) for dst, key in (
            (mean_h, "mean_h"), (causal, "causal"), (ident16, "ident16"), (eminus, "eminus"), (token_id, "token_id"),
            (earlier, "earlier"), (new_expert, "new_expert"), (tile_starts, "tile_starts"), (tile_id, "tile_id"),
            (norm_a, "norm_a"), (norm_f, "norm_f"), (wq, "qT"), (wk, "kT"), (wv, "vT"), (wo, "oT"),
            (wgate, "gateT"), (wup, "upT"), (fc, "fcT"), (router, "router"),
            (lnw, "lnw"), (lnb, "lnb"))]
        for j, rows in enumerate(FFN_ROWS):
            late.append((wdown[0:rows, j, :], d["downT"][P * j:P * j + rows, :]))
        late.append((proj[:], d["projT"].rearrange("(j p) n -> p j n", p=P)))
        late.append((router_b[:], d["router_b"].to_broadcast([P, E])))
        late.append((w1[:], d["w1"].rearrange("e p n -> p e n")))
        late.append((w2[:], d["w2"].rearrange("e (j p) n -> p e j n", p=P)))

        block = ctx.enter_context(nc.Block())

        @block.sync
        def _(sp):
            def load_x(k):
                sp.dma_start(xin[:], d["xT"][bass.ds(k, 1), :, :].rearrange("o p t -> (o p) t")) \
                    .then_inc(sems["x_loaded"], 16)

            load_x(0)
            for dst, src in early:
                sp.dma_start(dst, src).then_inc(sems["early_loaded"], 16)
            for dst, src in late:
                sp.dma_start(dst, src).then_inc(sems["late_loaded"], 16)
            sp.dma_start(sorted_rows, d["blank"]).then_inc(sems["blanked"], 16)
            with sp.Fori(1, SEQS) as k:
                sp.wait_ge(sems["xkeep"], nth(k - 1, "xkeep"))
                load_x(k)
            sp.wait_ge(sems["scattered"], nth(0, "scattered", 16 * G))
            by_tile = sorted_rows.rearrange("(i p) w -> p i w", p=P)
            sp.dma_start(srows[:, 0:FIRST_TILES, :], by_tile[:, 0:FIRST_TILES, :]).then_inc(sems["srows_first"], 16)
            sp.dma_start(srows[:, FIRST_TILES:, :], by_tile[:, FIRST_TILES:, :]).then_inc(sems["srows_rest"], 16)

        @block.gpsimd
        def _(pool):
            def ff_side(k, step):
                if step == 3:
                    pool.wait_ge(sems["ffn_res"], nth(k, "ffn_res"))
                    pool.tensor_tensor(x1[:], nrm[:], xkeep[:], ALU.add).then_inc(sems["x1"], 1)

            def mamba(c, side):
                for step in range(HEAD):
                    side(step)
                for n in range(STATE):
                    side(HEAD + n)
                    pool.wait_ge(sems["scan"], nth(c, "scan", 2 * n + 2))
                    pool.wait_ge(sems["ccopy"], nth(c, "ccopy", n + 1))
                    if n >= 4:
                        pool.wait_ge(sems["yacc"], nth(c, "yacc", GROUP_OF[n - 4] + 1))
                    pool.tensor_tensor(hc[:, n % 4], hst[:, n % HBUF],
                                       csb[:, n % CBUF:n % CBUF + 1, :].to_broadcast([P, HALVES, T]),
                                       ALU.mult).then_inc(sems["hc"], 1)
                    if len(GROUPS[GROUP_OF[n]]) == 2 and GROUPS[GROUP_OF[n]][1] == n:
                        pool.wait_ge(sems["hc"], nth(c, "hc", n + 1))
                        pool.tensor_tensor(hc[:, (n - 1) % 4], hc[:, (n - 1) % 4], hc[:, n % 4], ALU.add) \
                            .then_inc(sems["pair"], 1)

            mamba(0, lambda step: None)
            with pool.Fori(1, SEQS) as k:
                mamba(2 * k - 1, lambda step: ff_side(k - 1, step))
                mamba(2 * k, lambda step: None)
            ff_side(SEQS - 1, 3)
            mamba(2 * SEQS - 1, lambda step: None)

            pool.wait_ge(sems["blanked"], 16)
            pool.wait_ge(sems["rows_made"], 5)
            pool.wait_ge(sems["row_of"], 1)
            for g in range(G):
                pool.indirect_dma_start(sorted_rows, bass.IndirectOffsetOnAxis(row_of[:, g:g + 1], 0),
                                        trows[:, g, :], None).then_inc(sems["scattered"], 16)

            for i in range(NT):
                pool.wait_ge(sems["orow"], nth(i, "orow"))
                pool.indirect_dma_start(out, bass.IndirectOffsetOnAxis(target[:, i % 2:i % 2 + 1], 0),
                                        orow[:, i % 2, :], None).then_inc(sems[STORED[i % 2]], 16)
            pool.wait_ge(sems["even_stored"], 16 * NT // 2)
            pool.wait_ge(sems["odd_stored"], 16 * NT // 2)

        @block.scalar
        def _(act):
            act.preload_act_table_set(EXP_LN)
            act.wait_ge(sems["early_loaded"], 16 * len(early))
            for m in range(2):
                act.activation(M[m]["A"][:], M[m]["A"][:], ACT.Exp).then_inc(sems["setup_act"], 1)
            act.wait_ge(sems["setup_dve"], 1)

            def inverse_root(norm, i, var_bank, eps, tile):
                act.wait_ge(sems[norm + "_var"], nth(i, norm + "_var"))
                act.activation(tile[:], bank[:, var_bank, :], ACT.Ln, bias=eps[:]).then_inc(sems[norm + "_logged"], 1)
                act.wait_ge(sems[norm + "_logged"], nth(i, norm + "_logged"))
                act.activation(tile[:], tile[:], ACT.Exp, scale=-0.5).then_inc(sems[norm + "_rstd"], 1)

            def head_norm(c, m, k):
                act.wait_ge(sems["ln_centered"], nth(c, "ln_centered"))
                act.activation(rstd_m[:], bank[:, 0, :], ACT.Square).then_inc(sems["ln_squared"], 1)
                inverse_root("ln", c, 1, eps_ln, rstd_m)
                if m == 0:
                    act.wait_ge(sems["ln_done"], nth(c, "ln_done"))
                    act.activation(rstd_m[:], xl[:], ACT.Square).then_inc(sems["rms_squared"], 1)
                    inverse_root("rms", k, 1, eps_rms, rstd_m)

            def head_silu(c, m, follows):
                for h in range(HALVES):
                    act.wait_ge(sems["conv"], nth(c, "conv", h + 1))
                    if follows and h == 0:
                        act.wait_ge(sems["yd"], nth(c - 1, "yd", HALVES))
                    act.activation(xs[:, h], bank[:, 2 + h, :], ACT.Silu, bias=M[m]["cb"][:, h:h + 1]) \
                        .then_inc(sems["xs"], 1)
                for h in range(HALVES):
                    act.wait_ge(sems["z"], nth(c, "z", h + 1))
                    if follows and h == 0:
                        act.wait_ge(sems["yg"], nth(c - 1, "yg", HALVES))
                    act.activation(zs[:, h], bank[:, 4 + h, :], ACT.Silu).then_inc(sems["zs"], 1)
                act.preload_act_table_set(EXP_LN)

            def mamba(c, m, side, follower=None):
                w = M[m]
                side(0)
                side(1)
                bc0 = 0 if m == 0 else DTR[1]
                dt0 = BCR if m == 0 else 0
                act.wait_ge(sems["proj"], nth(c, "proj"))
                act.activation(dt_rows[0:DTR[m], :], bank[dt0:dt0 + DTR[m], 0, :], ACT.Copy) \
                    .then_inc(sems["dtrows"], 1)
                act.activation(parts[0:BCR, :], bank[bc0:bc0 + BCR, 0, :], ACT.Copy).then_inc(sems["hi"], 1)
                side(2)
                for h in range(HALVES):
                    act.wait_ge(sems["dtp"], nth(c, "dtp", h + 1))
                    act.activation(sp_abs[:, h], bank[:, 2 + h, :], ACT.Abs, bias=w["db"][:, h:h + 1]) \
                        .then_inc(sems["spabs"], 1)
                act.wait_ge(sems["spabs"], nth(c, "spabs", 2))
                act.activation(sp_abs[:], sp_abs[:], ACT.Exp, scale=-1.0).then_inc(sems["spexp"], 1)
                side(3)
                act.wait_ge(sems["spexp"], nth(c, "spexp"))
                act.activation(sp_abs[:], sp_abs[:], ACT.Ln, bias=one_col[:]).then_inc(sems["spln"], 1)
                side(4)
                act.wait_ge(sems["mid"], nth(c, "mid"))
                act.activation(parts[BCR:2 * BCR, :], mid[:], ACT.Copy).then_inc(sems["midcopy"], 1)
                side(5)
                act.wait_ge(sems["delta"], nth(c, "delta"))
                act.wait_ge(sems["spmax"], nth(c, "spmax", 2))
                for n in range(STATE):
                    act.wait_ge(sems["cbc"], nth(c, "cbc", n + 1))
                    if n >= CBUF:
                        act.wait_ge(sems["hc"], nth(c, "hc", n - CBUF + 1))
                    act.activation(csb[:, n % CBUF], bank[:, 1, :], ACT.Copy).then_inc(sems["ccopy"], 1)
                    for h in range(HALVES):
                        if n >= 1:
                            act.wait_ge(sems["scan"], nth(c, "scan", 2 * n - 1 + h))
                        act.activation(bank[:, 2 + h, :], delta[:, h], ACT.Exp,
                                       scale=w["A"][:, h, n:n + 1]).then_inc(sems["dA"], 1)
                    side(HEAD + n)
                if follower:
                    head_norm(*follower)
                    head_silu(follower[0], follower[1], True)

            def attention_side(k, step):
                if step == 0:
                    act.wait_ge(sems["res"], nth(side_res(k), "res"))
                    act.activation(rstd_d[:], h0[:], ACT.Square).then_inc(sems["dn_squared"], 1)
                    act.activation(xkeep[:], xin[:], ACT.Copy).then_inc(sems["xkeep"], 1)
                    inverse_root("dn", 4 * k, DBANK + 1, eps_rms, rstd_d)
                if step == 1:
                    act.wait_ge(sems["q_mm"], nth(k, "q_mm"))
                    act.activation(qs[:], bank[:, DBANK, :], ACT.Copy, scale=SCALE).then_inc(sems["q_copy"], 1)
                if step == 2:
                    act.wait_ge(sems["v_mm"], nth(k, "v_mm"))
                    act.activation(vs[:], bank[:, DBANK, :].rearrange("p (j n) -> p j n", j=QB), ACT.Copy) \
                        .then_inc(sems["v_copy"], 1)
                i = step - TILE0 - 2
                if 0 <= i < TILES:
                    keys = P * (i % QB + 1)
                    act.wait_ge(sems["probT_mm"], nth(k, "probT_mm", i + 1))
                    if i >= 2:
                        act.wait_ge(sems["pv"], nth(k, "pv", i - 1))
                    act.activation(probT[:, i % 2, 0:keys], bank[:, DBANK + i % 2, 0:keys], ACT.Copy) \
                        .then_inc(sems["probT"], 1)
                i = step - TILE0 - 1
                if 0 <= i < TILES:
                    h, j = i // QB, i % QB
                    keys = P * (j + 1)
                    act.wait_ge(sems["smax"], nth(k, "smax", i + 1))
                    if i >= 2:
                        act.wait_ge(sems["probT_mm"], nth(k, "probT_mm", i - 1))
                    act.activation(prob[:, i % 2, 0:keys], bank[:, DBANK + i % 2, 0:keys], ACT.Exp,
                                   bias=nmax[:, i:i + 1], accum_out=psums[:, j, h:h + 1]) \
                        .then_inc(sems["prob"], 1)
                i = step - TILE0 - 2
                if 0 <= i < TILES:
                    h, j = i // QB, i % QB
                    act.wait_ge(sems["pv"], nth(k, "pv", i + 1))
                    act.activation(att[:, j, HD * h:HD * h + HD], bank[:, DBANK + i % 2, 0:HD], ACT.Copy) \
                        .then_inc(sems["pv_copy"], 1)
                if step == SIDE_STEPS - 1:
                    act.wait_ge(sems["attT_mm"], nth(k, "attT_mm"))
                    act.activation(attT[:], bank[:, DBANK, :], ACT.Copy).then_inc(sems["attT"], 1)

            def ff_side(k, step):
                if step == 0:
                    act.wait_ge(sems["h1"], nth(k, "h1"))
                    act.activation(rstd_d[:], h1[:], ACT.Square).then_inc(sems["dn_squared"], 1)
                    inverse_root("dn", 4 * k + 1, DBANK + 1, eps_rms, rstd_d)
                if step == 1:
                    for j, rows in enumerate(FFN_ROWS):
                        act.wait_ge(sems["gate_mm"], nth(k, "gate_mm", j + 1))
                        act.activation(gs[0:rows, j], bank[0:rows, DBANK + j % 2, :], ACT.Silu) \
                            .then_inc(sems["gs"], 1)
                    act.preload_act_table_set(EXP_LN)
                if step == 4:
                    act.wait_ge(sems["dn_centered"], nth(k, "dn_centered"))
                    act.activation(rstd_d[:], bank[:, DBANK, :], ACT.Square).then_inc(sems["dn_squared"], 1)
                if step == 5:
                    inverse_root("dn", 4 * k + 2, DBANK + 1, eps_ln, rstd_d)
                if step == 8:
                    for j in range(MH):
                        act.wait_ge(sems["fc_mm"], nth(k, "fc_mm", j + 1))
                        act.activation(gs[:, j], bank[:, DBANK + j % 2, :], ACT.Gelu).then_inc(sems["gelu"], 1)
                    act.preload_act_table_set(EXP_LN)
                if step == 12:
                    act.wait_ge(sems["gcen"], nth(k, "gcen"))
                    act.activation(gs[:], gc[:], ACT.Square).then_inc(sems["dn_squared"], 1)
                if step == 14:
                    inverse_root("dn", 4 * k + 3, DBANK + 1, eps_ln, rstd_d)

            def side_res(k):
                return 0 if isinstance(k, int) and k == 0 else 2 * k - 1

            def slot_pair(k, last):
                act.preload_act_table_set(EXP_LN)
                mamba(2 * k - 1, 0, lambda step: ff_side(k - 1, step), (2 * k, 1, k - 1))
                mamba(2 * k, 1, lambda step: attention_side(k, step), None if last else (2 * k + 1, 0, k + 1))

            head_norm(0, 0, 0)
            head_silu(0, 0, False)
            mamba(0, 0, lambda step: None)
            for step in range(SIDE_STEPS):
                attention_side(0, step)
            head_norm(1, 0, 1)
            head_silu(1, 0, True)
            with act.Fori(1, SEQS - 1) as k:
                slot_pair(k, False)
            slot_pair(SEQS - 1, True)
            for step in range(SIDE_STEPS):
                ff_side(SEQS - 1, step)
            head_norm(2 * SEQS - 1, 1, SEQS - 1)
            head_silu(2 * SEQS - 1, 1, True)
            mamba(2 * SEQS - 1, 1, lambda step: None)

            act.preload_act_table_set(EXP_LN)
            act.wait_ge(sems["router_mm"], 1)
            act.activation(router_c[:], bank[:, 4, 0:E], ACT.Copy).then_inc(sems["router_c"], 1)
            act.wait_ge(sems["res"], nth(2 * SEQS - 1, "res"))
            for b in range(SEQS):
                act.wait_ge(sems["xrow_mm"], nth(0, "xrow_mm", b + 1))
                act.activation(trows[:, QB * b:QB * b + QB, 0:D], bank[:, b, :].rearrange("p (j n) -> p j n", n=D),
                               ACT.Copy).then_inc(sems["xrow"], 1)
            act.wait_ge(sems["meanvar"], nth(0, "meanvar", G))
            act.activation(trows[:, :, RSTD], meanvar[:, :, 1], ACT.Ln, bias=eps_ln[:]).then_inc(sems["mlog"], 1)
            act.wait_ge(sems["mlog"], 1)
            act.activation(trows[:, :, RSTD], trows[:, :, RSTD], ACT.Exp, scale=-0.5).then_inc(sems["rstd"], 1)
            act.wait_ge(sems["lsub"], 1)
            act.activation(le[:], lg[:], ACT.Exp).then_inc(sems["lexp"], 1)

            def turned(i, s):
                act.wait_ge(sems["xT_mm"], nth(i, "xT_mm"))
                act.activation(xT[:, s], bank[:, 0, 0:P], ACT.Copy).then_inc(sems["xT"], 1)

            def silu_of(i, s, reused):
                act.wait_ge(sems["ea_mm"], nth(i, "ea_mm"))
                if reused:
                    act.wait_ge(sems["ey"], nth(i - 2, "ey"))
                act.activation(es[:, s], bank[:, 1 + s, :], ACT.Silu).then_inc(sems["es"], 1)

            def hidden_turned(i, s, reused):
                act.wait_ge(sems["eyT_mm"], nth(i, "eyT_mm"))
                if reused:
                    act.wait_ge(sems["down_e"], nth(i - 2, "down_e"))
                act.activation(eyT[:, s], bank[:, 5, :], ACT.Copy).then_inc(sems["eyT"], 1)

            turned(0, 0)
            for i in range(2):
                silu_of(i, i, False)
                turned(i + 1, 1 - i)
                if i >= 1:
                    hidden_turned(0, 0, False)
            with act.Fori(1, NT // 2 - 1) as pair:
                for s in range(2):
                    silu_of(2 * pair + s, s, True)
                    turned(2 * pair + s + 1, 1 - s)
                    hidden_turned(2 * pair + s - 1, 1 - s, True)
            for i in range(NT - 2, NT + 1):
                if i < NT:
                    silu_of(i, i % 2, True)
                if i + 1 < NT:
                    turned(i + 1, (i + 1) % 2)
                hidden_turned(i - 1, (i - 1) % 2, True)

        @block.vector
        def _(dve):
            dve.memset(eps_ln[:], LN_EPS)
            dve.memset(eps_rms[:], RMS_EPS)
            dve.memset(ones[:], 1.0)
            for m in range(2):
                dve.memset(xn[m][:, 0:PAD], 0.0)
            dve.memset(one_col[:], 1.0).then_inc(sems["setup_dve"], 1)
            dve.wait_ge(sems["early_loaded"], 16 * len(early))
            for m in range(2):
                dve.wait_ge(sems["setup_act"], m + 1)
                w = M[m]
                dve.tensor_scalar(w["A"][:], w["A"][:], -1.0, None, ALU.mult)
                dve.tensor_tensor(w["cw"][:], w["cw"][:], winx[m].unsqueeze(1).to_broadcast([P, TAPS, HALVES * P]),
                                  ALU.mult).then_inc(sems["folded"], 1)

            def ternary_weights():
                dve.wait_ge(sems["late_loaded"], 16 * len(late))
                last = [1]

                def step_done(ins):
                    ins.then_inc(sems["setup_dve"], 1)
                    last[0] += 1
                    dve.wait_ge(sems["setup_dve"], last[0])

                fcv, prv = fc[:], proj[:].rearrange("p j n -> p (j n)")
                step_done(dve.tensor_reduce(absr[:, 0:1], fcv, AX.X, ALU.add, apply_absolute_value=True))
                step_done(dve.tensor_reduce(absr[:, 1:2], prv, AX.X, ALU.add, apply_absolute_value=True))
                dve.wait_ge(sems["setup_pe"], 1)
                half = 0.5 / (MH * P * D)
                step_done(dve.tensor_scalar(thr[:, 0:2], bank[:, 0, 0:2], half, 0.5 * QUANT_EPS, ALU.mult, ALU.add))
                step_done(dve.tensor_scalar(thr[:, 2:4], thr[:, 0:2], -1.0, None, ALU.mult))
                for i, v in enumerate((fcv, prv)):
                    step_done(dve.tensor_scalar(qtmp[:], v, thr[:, i:i + 1], None, ALU.is_gt))
                    step_done(dve.tensor_scalar(qtmp2[:], v, thr[:, 2 + i:3 + i], None, ALU.is_lt))
                    step_done(dve.tensor_tensor(v, qtmp[:], qtmp2[:], ALU.subtract))
                for j in range(MH):
                    step_done(dve.tensor_scalar(projw[:, j, :], proj[:, j, :], lnw[:, j:j + 1], None, ALU.mult))
                dve.wait_ge(sems["setup_pe"], 2)
                step_done(dve.tensor_copy(projb[:], bank[:, 0, 2:3]))
                SETUP_DONE.append(last[0])

            def head_ln(c, m):
                dve.wait_ge(sems["ln_rstd"], nth(c, "ln_rstd"))
                dve.tensor_tensor(xl[:] if m == 0 else xn[1][:, PAD:], bank[:, 0, :], rstd_m[:], ALU.mult) \
                    .then_inc(sems["ln_done"], 1)

            def head_rms(m, k):
                if m == 0:
                    dve.wait_ge(sems["rms_rstd"], nth(k, "rms_rstd"))
                    dve.scalar_tensor_tensor(xn[0][:, PAD:], xl[:], norm_m[:], rstd_m[:], ALU.mult, ALU.mult) \
                        .then_inc(sems["rms_done"], 1)

            def mamba(c, m, k, side, follower=None):
                w = M[m]
                side(0)
                side(1)
                bc0 = 0 if m == 0 else DTR[1]
                dve.wait_ge(sems["hi"], nth(c, "hi"))
                dve.tensor_tensor(rest[:], bank[bc0:bc0 + BCR, 0, :], parts[0:BCR, :], ALU.subtract) \
                    .then_inc(sems["rest"], 1)
                dve.wait_ge(sems["rest"], nth(c, "rest"))
                dve.tensor_copy(mid[:], rest[:]).then_inc(sems["mid"], 1)
                dve.wait_ge(sems["mid"], nth(c, "mid"))
                dve.tensor_tensor(parts[2 * BCR:3 * BCR, :], rest[:], mid[:], ALU.subtract).then_inc(sems["lo"], 1)
                side(2)
                for h in range(HALVES):
                    dve.wait_ge(sems["spabs"], nth(c, "spabs", h + 1))
                    dve.tensor_scalar(sp_max[:, h], bank[:, 2 + h, :], w["db"][:, h:h + 1], 0.0, ALU.add, ALU.max) \
                        .then_inc(sems["spmax"], 1)
                side(3)
                dve.wait_ge(sems["spmax"], nth(c, "spmax", 2))
                dve.wait_ge(sems["spln"], nth(c, "spln"))
                dve.tensor_tensor(delta[:], sp_max, sp_abs, ALU.add).then_inc(sems["delta"], 1)
                dve.wait_ge(sems["delta"], nth(c, "delta"))
                dve.tensor_tensor(du[:], delta[:], xs[:], ALU.mult).then_inc(sems["du"], 1)
                side(4)
                side(5)
                dve.wait_ge(sems["du"], nth(c, "du"))

                def input_of(n):
                    dve.wait_ge(sems["bbc"], nth(c, "bbc", n + 1))
                    dve.tensor_tensor(dbu[:, n % 2], du[:], bank[:, 0:1, :].to_broadcast([P, HALVES, T]),
                                      ALU.mult).then_inc(sems["dbu"], 1)

                input_of(0)
                for n in range(STATE):
                    side(HEAD + n)
                    if n + 1 < STATE:
                        if n >= 1:
                            dve.wait_ge(sems["scan"], nth(c, "scan", 2 * n))
                        input_of(n + 1)
                    dve.wait_ge(sems["dbu"], nth(c, "dbu", n + 1))
                    if n >= HBUF:
                        dve.wait_ge(sems["hc"], nth(c, "hc", n - HBUF + 1))
                    for h in range(HALVES):
                        dve.wait_ge(sems["dA"], nth(c, "dA", 2 * n + h + 1))
                        dve.tensor_tensor_scan(hst[:, n % HBUF, h], bank[:, 2 + h, :], dbu[:, n % 2, h],
                                               0.0, ALU.mult, ALU.add).then_inc(sems["scan"], 1)
                if follower:
                    head_ln(*follower[:2])
                dve.wait_ge(sems["yacc"], nth(c, "yacc", len(GROUPS)))
                for h in range(HALVES):
                    dve.scalar_tensor_tensor(yd[:, h], xs[:, h], w["dskip"][:, h:h + 1], bank[:, 4 + h, :],
                                             ALU.mult, ALU.add).then_inc(sems["yd"], 1)
                for h in range(HALVES):
                    dve.wait_ge(sems["yd"], nth(c, "yd", h + 1))
                    dve.tensor_tensor(yd[:, h], yd[:, h], zs[:, h], ALU.mult).then_inc(sems["yg"], 1)
                if follower:
                    head_rms(*follower[1:])
                dve.wait_ge(sems["out"], nth(c, "out"))
                dst, res = (h0[:], xl[:]) if m == 0 else (seq(x3, k), x2[:])
                dve.tensor_tensor(dst, bank[:, 1, :], res, ALU.add).then_inc(sems["res"], 1)

            def attention_side(k, step):
                if step == 0:
                    dve.wait_ge(sems["dn_rstd"], nth(4 * k, "dn_rstd"))
                    dve.scalar_tensor_tensor(nrm[:], h0[:], norm_a[:], rstd_d[:], ALU.mult, ALU.mult) \
                        .then_inc(sems["dn_done"], 1)
                if step == 1:
                    dve.wait_ge(sems["k_mm"], nth(k, "k_mm"))
                    dve.tensor_copy(ks[:], bank[:, DBANK + 1, :]).then_inc(sems["k_copy"], 1)
                i = step - TILE0 - 1
                if 0 <= i < TILES:
                    keys = P * (i % QB + 1)
                    dve.wait_ge(sems["score"], nth(k, "score", i + 1))
                    dve.tensor_reduce(nmax[:, i:i + 1], bank[:, DBANK + i % 2, 0:keys], AX.X, ALU.max,
                                      negate=True).then_inc(sems["smax"], 1)
                if step == SIDE_STEPS - 1:
                    dve.wait_ge(sems["prob"], nth(k, "prob", TILES))
                    dve.reciprocal(rsums[:], psums[:]).then_inc(sems["recip"], 1)
                    dve.wait_ge(sems["recip"], nth(k, "recip"))
                    dve.wait_ge(sems["pv_copy"], nth(k, "pv_copy", TILES))
                    heads = x1[:].rearrange("p (j n) -> p j n", n=HD)
                    dve.tensor_tensor(heads, heads, rsums[:].rearrange("p j h -> p (j h)").unsqueeze(2)
                                      .to_broadcast([P, QB * N_HEADS, HD]), ALU.mult).then_inc(sems["att"], 1)
                    dve.wait_ge(sems["o_mm"], nth(k, "o_mm"))
                    dve.tensor_tensor(h1[:], bank[:, DBANK + 1, :], h0[:], ALU.add).then_inc(sems["h1"], 1)

            def ff_side(k, step):
                if step == 0:
                    dve.wait_ge(sems["dn_rstd"], nth(4 * k + 1, "dn_rstd"))
                    dve.scalar_tensor_tensor(nrm[:], h1[:], norm_f[:], rstd_d[:], ALU.mult, ALU.mult) \
                        .then_inc(sems["dn_done"], 1)
                if step == 2:
                    for j, rows in enumerate(FFN_ROWS):
                        dve.wait_ge(sems["gs"], nth(k, "gs", j + 1))
                        dve.wait_ge(sems["up_mm"], nth(k, "up_mm", j + 1))
                        dve.tensor_tensor(gc[0:rows, j], gs[0:rows, j], bank[0:rows, DBANK + (j + 1) % 2, :],
                                          ALU.mult).then_inc(sems["gu"], 1)
                if step == 3:
                    dve.wait_ge(sems["down_mm"], nth(k, "down_mm"))
                    dve.tensor_tensor(nrm[:], bank[:, DBANK, :], h1[:], ALU.add).then_inc(sems["ffn_res"], 1)
                if step == 6:
                    dve.wait_ge(sems["dn_rstd"], nth(4 * k + 2, "dn_rstd"))
                    dve.tensor_tensor(nrm[:], bank[:, DBANK, :], rstd_d[:], ALU.mult).then_inc(sems["dn_done"], 1)
                if step == 11:
                    dve.wait_ge(sems["gmean"], nth(k, "gmean"))
                    dve.tensor_tensor(gc[:], gs[:], bank[:, DBANK:DBANK + 1, :].to_broadcast([P, MH, T]),
                                      ALU.subtract).then_inc(sems["gcen"], 1)
                if step == 15:
                    dve.wait_ge(sems["pj_mm"], nth(k, "pj_mm"))
                    dve.wait_ge(sems["dn_rstd"], nth(4 * k + 3, "dn_rstd"))
                    dve.tensor_tensor(h1[:], bank[:, DBANK, :], rstd_d[:], ALU.mult).then_inc(sems["pj_scaled"], 1)
                if step == 16:
                    dve.wait_ge(sems["pj_scaled"], nth(k, "pj_scaled"))
                    dve.scalar_tensor_tensor(x2[:], h1[:], projb[:], x1[:], ALU.add, ALU.add) \
                        .then_inc(sems["x2"], 1)

            def slot_pair(k, last):
                mamba(2 * k - 1, 0, k, lambda step: ff_side(k - 1, step), (2 * k, 1, k - 1))
                mamba(2 * k, 1, k - 1, lambda step: attention_side(k, step), None if last else (2 * k + 1, 0, k + 1))

            head_ln(0, 0)
            head_rms(0, 0)
            mamba(0, 0, 0, lambda step: None)
            ternary_weights()
            for step in range(SIDE_STEPS):
                attention_side(0, step)
            head_ln(1, 0)
            head_rms(0, 1)
            with dve.Fori(1, SEQS - 1) as k:
                slot_pair(k, False)
            slot_pair(SEQS - 1, True)
            for step in range(SIDE_STEPS):
                ff_side(SEQS - 1, step)
            head_ln(2 * SEQS - 1, 1)
            mamba(2 * SEQS - 1, 1, SEQS - 1, lambda step: None)

            for g in range(G):
                if g % QB == 0:
                    dve.wait_ge(sems["xrow"], nth(0, "xrow", g // QB + 1))
                dve.bn_stats(stats[:, g, :], trows[:, g, 0:D]).then_inc(sems["stats"], 1)
            for g in range(G):
                dve.wait_ge(sems["stats"], nth(0, "stats", g + 1))
                dve.bn_aggr(meanvar[:, g, :], stats[:, g, :]).then_inc(sems["meanvar"], 1)
            dve.tensor_copy(trows[:, :, TOKEN], token_id[:]).then_inc(sems["rows_made"], 1)
            dve.wait_ge(sems["meanvar"], nth(0, "meanvar", G))
            dve.tensor_copy(trows[:, :, MEAN], meanvar[:, :, 0]).then_inc(sems["rows_made"], 1)
            dve.wait_ge(sems["logit_mm"], 1)
            dve.wait_ge(sems["rstd"], 1)
            logits = bank[:, 4, 0:G * E].rearrange("p (g e) -> p g e", e=E)
            dve.tensor_tensor(lg[:], logits, trows[:, :, RSTD:RSTD + 1].to_broadcast([P, G, E]), ALU.mult) \
                .then_inc(sems["lscaled"], 1)
            dve.wait_ge(sems["lscaled"], 1)
            dve.tensor_tensor(lg[:], lg[:], router_b[:].unsqueeze(1).to_broadcast([P, G, E]), ALU.add) \
                .then_inc(sems["lbiased"], 1)
            dve.wait_ge(sems["lbiased"], 1)
            dve.tensor_reduce(lmax[:], lg[:], AX.X, ALU.max).then_inc(sems["lmax"], 1)
            dve.wait_ge(sems["lmax"], 1)
            dve.tensor_tensor(lg[:], lg[:], lmax[:].unsqueeze(2).to_broadcast([P, G, E]),
                              ALU.subtract).then_inc(sems["lsub"], 1)
            dve.wait_ge(sems["lsub"], 1)
            dve.scalar_tensor_tensor(cand[:], lg[:], 0.0, eminus[:].unsqueeze(1).to_broadcast([P, G, E]),
                                     ALU.is_ge, ALU.mult).then_inc(sems["cand"], 1)
            dve.wait_ge(sems["cand"], 1)
            dve.tensor_reduce(first[:], cand[:], AX.X, ALU.min).then_inc(sems["first"], 1)
            dve.wait_ge(sems["first"], 1)
            dve.tensor_tensor(onehot[:], eminus[:].unsqueeze(2).to_broadcast([P, E, G]),
                              first[:].unsqueeze(1).to_broadcast([P, E, G]), ALU.is_equal).then_inc(sems["onehot"], 1)
            dve.wait_ge(sems["lexp"], 1)
            dve.tensor_reduce(lsum[:], le[:], AX.X, ALU.add).then_inc(sems["lsum"], 1)
            dve.wait_ge(sems["lsum"], 1)
            dve.reciprocal(trows[:, :, PROB], lsum[:]).then_inc(sems["rows_made"], 1)

            step = [0]

            def routed(ins):
                ins.then_inc(sems["route"], 1)
                step[0] += 1
                dve.wait_ge(sems["route"], step[0])

            flat = lambda t: t[:].rearrange("p e g -> p (e g)")
            ranks = bank[:, 5, 0:E * G].rearrange("p (e g) -> p e g", g=G)
            totals = bank[:, 6, 0:E * G].rearrange("p (e g) -> p e g", g=G)
            dve.wait_ge(sems["count_mm"], 1)
            routed(dve.tensor_tensor_scan(flat(upto), flat(new_expert), bank[:, 6, 0:E * G], 0.0, ALU.mult, ALU.add))
            dve.tensor_tensor(place[:], upto[:], totals, ALU.subtract).then_inc(sems["rows_made"], 1)
            routed(dve.tensor_tensor(starts[:], upto[:, :, G - 1:G].to_broadcast([P, E, G]),
                                     tile_starts[:].unsqueeze(1).to_broadcast([P, E, G]), ALU.is_gt))
            dve.wait_ge(sems["rows_made"], 4)
            dve.tensor_tensor(place[:], place[:], ranks, ALU.add).then_inc(sems["rows_made"], 1)
            routed(dve.tensor_reduce(tiles_of[:], starts[:], AX.X, ALU.add))
            routed(dve.tensor_tensor_scan(tiles_upto[:], ones[:, 0:E], tiles_of[:], 0.0, ALU.mult, ALU.add))
            dve.tensor_tensor(past[:], tiles_upto[:].unsqueeze(1).to_broadcast([P, NT, E]),
                              tile_id[:].unsqueeze(2).to_broadcast([P, NT, E]), ALU.is_le).then_inc(sems["route"], 1)
            routed(dve.tensor_tensor(tiles_before[:], tiles_upto[:], tiles_of[:], ALU.subtract))
            step[0] += 1
            dve.wait_ge(sems["route"], step[0])
            dve.wait_ge(sems["rows_made"], 5)
            routed(dve.scalar_tensor_tensor(place[:], tiles_before[:].unsqueeze(2).to_broadcast([P, E, G]), float(P),
                                            place[:], ALU.mult, ALU.add))
            routed(dve.tensor_tensor(place[:], place[:], onehot[:], ALU.mult))
            routed(dve.tensor_reduce(row_f[:], place[:].rearrange("p e g -> p g e"), AX.X, ALU.add))
            dve.tensor_copy(row_of[:], row_f[:]).then_inc(sems["row_of"], 1)
            routed(dve.tensor_reduce(expert_f[:], past[:], AX.X, ALU.add))
            dve.tensor_scalar(expert_of[:], expert_f[:], float(E - 1), None, ALU.min).then_inc(sems["experts"], 1)

            def normalized(i, s, reused, index):
                if reused:
                    dve.wait_ge(sems["xT_mm"], nth(i - 2, "xT_mm"))
                dve.tensor_scalar(nrow[:, s], index(0, D), index(MEAN, MEAN + 1), index(RSTD, RSTD + 1),
                                  ALU.subtract, ALU.mult).then_inc(sems["nrow"], 1)

            def gated(i, s, reused):
                dve.wait_ge(sems["es"], nth(i, "es"))
                dve.wait_ge(sems["eg_mm"], nth(i, "eg_mm"))
                if reused:
                    dve.wait_ge(sems["eyT_mm"], nth(i - 2, "eyT_mm"))
                dve.tensor_tensor(ey[:, s], es[:, s], bank[:, 3 + s, :], ALU.mult).then_inc(sems["ey"], 1)

            def finished(i, s, pair, index):
                if not (isinstance(pair, int) and pair == 0):
                    dve.wait_ge(sems[STORED[s]], nth(pair - 1, STORED[s], 16))
                dve.tensor_scalar(target[:, s:s + 1], index(TOKEN, TOKEN + 1), 0.0, None, ALU.add) \
                    .then_inc(sems["target"], 1)
                dve.wait_ge(sems["down_e"], nth(i, "down_e"))
                dve.scalar_tensor_tensor(orow[:, s], bank[:, 6 + s, 0:D], index(PROB, PROB + 1), index(0, D),
                                         ALU.mult, ALU.add).then_inc(sems["orow"], 1)

            def of_tile(i):
                if isinstance(i, int):
                    return lambda a, b: srows[:, i, a:b]
                return lambda a, b: srows[:, bass.ds(i, 1), a:b].rearrange("p o w -> p (o w)")

            dve.wait_ge(sems["srows_first"], 16)
            for i in range(2):
                normalized(i, i, False, of_tile(i))
            for i in range(2):
                gated(i, i, False)
                normalized(i + 2, i, True, of_tile(i + 2))
            dve.wait_ge(sems["srows_rest"], 16)
            for i in range(2, 4):
                gated(i, i - 2, True)
                normalized(i + 2, i - 2, True, of_tile(i + 2))
                finished(i - 2, i - 2, 0, of_tile(i - 2))
            with dve.Fori(2, NT // 2 - 1) as pair:
                for s in range(2):
                    gated(2 * pair + s, s, True)
                    normalized(2 * pair + s + 2, s, True, of_tile(2 * pair + s + 2))
                    finished(2 * pair + s - 2, s, pair - 1, of_tile(2 * pair + s - 2))
            for i in range(NT - 2, NT + 2):
                if i < NT:
                    gated(i, i % 2, True)
                finished(i - 2, i % 2, (i - 2) // 2, of_tile(i - 2))

        @block.tensor
        def _(pe):
            def mm(dst, lhsT, rhs, start=True, stop=True):
                return pe.matmul(dst, lhsT, rhs, start=start, stop=stop)

            def ternary_weights():
                pe.wait_ge(sems["setup_dve"], 3)
                pe.wait_ge(sems["res"], 1)
                mm(bank[:, 0, 0:2], ones[:], absr[:]).then_inc(sems["setup_pe"], 1)
                pe.wait_ge(sems["setup_dve"], SETUP_DONE[0] - 1)
                for j in range(MH):
                    last = mm(bank[:, 0, 2:3], proj[:, j, :], lnb[:, j:j + 1], j == 0, j == MH - 1)
                last.then_inc(sems["setup_pe"], 1)
                pe.wait_ge(sems["setup_dve"], SETUP_DONE[0])

            def variance(norm, i, dst_bank, tile):
                pe.wait_ge(sems[norm + "_squared"], nth(i, norm + "_squared"))
                mm(bank[:, dst_bank, :], mean_d[:], tile[:]).then_inc(sems[norm + "_var"], 1)

            def head_norm(c, m, k):
                if m == 0:
                    pe.wait_ge(sems["x_loaded"], nth(k, "x_loaded", 16))
                else:
                    pe.wait_ge(sems["x2"], nth(k, "x2"))
                mm(bank[:, 0, :], center[:], (xin if m == 0 else x2)[:]).then_inc(sems["ln_centered"], 1)
                variance("ln", c, 1, rstd_m)

            def head_conv(c, m, k, follows):
                if m == 0:
                    variance("rms", k, 1, rstd_m)
                    pe.wait_ge(sems["rms_done"], nth(k, "rms_done"))
                else:
                    pe.wait_ge(sems["ln_done"], nth(c, "ln_done"))
                for h in range(HALVES):
                    for tap in range(TAPS):
                        last = mm(bank[:, 2 + h, :], M[m]["cw"][:, tap, P * h:P * h + P], xn[m][:, tap:tap + T],
                                  tap == 0, tap == TAPS - 1)
                    last.then_inc(sems["conv"], 1)
                if follows:
                    pe.wait_ge(sems["yd"], nth(c - 1, "yd", HALVES))
                for h in range(HALVES):
                    mm(bank[:, 4 + h, :], M[m]["wz"][:, P * h:P * h + P], xn[m][:, PAD:]).then_inc(sems["z"], 1)

            def mamba(c, m, k, side, late_side, follower=None):
                w = M[m]
                side(0)
                late_side(0)
                side(1)
                late_side(1)
                rows = DTR[m] + BCR
                for h in range(HALVES):
                    pe.wait_ge(sems["xs"], nth(c, "xs", h + 1))
                    last = mm(bank[0:rows, 0, :], w["wx"][:, h, :], xs[:, h], h == 0, h == HALVES - 1)
                last.then_inc(sems["proj"], 1)
                side(2)
                late_side(2)
                pe.wait_ge(sems["dtrows"], nth(c, "dtrows"))
                for h in range(HALVES):
                    mm(bank[:, 2 + h, :], w["wdt"][:, P * h:P * h + P], dt_rows[0:DTR[m], :]) \
                        .then_inc(sems["dtp"], 1)
                for step in range(3, HEAD):
                    side(step)
                    late_side(step)
                pe.wait_ge(sems["hi"], nth(c, "hi"))
                pe.wait_ge(sems["midcopy"], nth(c, "midcopy"))
                pe.wait_ge(sems["lo"], nth(c, "lo"))

                def spread(n):
                    if n >= 1:
                        pe.wait_ge(sems["dbu"], nth(c, "dbu", n))
                    mm(bank[:, 0, :], pick[:, n, :], parts[:]).then_inc(sems["bbc"], 1)
                    if n >= 1:
                        pe.wait_ge(sems["ccopy"], nth(c, "ccopy", n))
                    mm(bank[:, 1, :], pick[:, STATE + n, :], parts[:]).then_inc(sems["cbc"], 1)

                def accumulate(g):
                    first = GROUPS[g][0]
                    if len(GROUPS[g]) == 2:
                        pe.wait_ge(sems["pair"], nth(c, "pair", PAIRS_UP_TO[g]))
                    else:
                        pe.wait_ge(sems["hc"], nth(c, "hc", first + 1))
                    for h in range(HALVES):
                        last = mm(bank[:, 4 + h, :], ident[:], hc[:, first % 4, h], g == 0, g == len(GROUPS) - 1)
                    last.then_inc(sems["yacc"], 1)

                spread(0)
                spread(1)
                for n in range(STATE):
                    side(HEAD + n)
                    late_side(HEAD + n)
                    if n + 2 < STATE:
                        spread(n + 2)
                    for g, group in enumerate(GROUPS):
                        if group[-1] == n - YLAG:
                            accumulate(g)
                if follower:
                    pe.wait_ge(sems["dbu"], nth(c, "dbu", STATE))
                    pe.wait_ge(sems["ccopy"], nth(c, "ccopy", STATE))
                    head_norm(*follower)
                for g, group in enumerate(GROUPS):
                    if group[-1] >= STATE - YLAG:
                        accumulate(g)
                if follower:
                    pe.wait_ge(sems["scan"], nth(c, "scan", 2 * STATE))
                    head_conv(*follower, True)
                for h in range(HALVES):
                    pe.wait_ge(sems["yg"], nth(c, "yg", h + 1))
                    last = mm(bank[:, 1, :], w["wo"][:, h, :], yd[:, h], h == 0, h == HALVES - 1)
                last.then_inc(sems["out"], 1)

            def attention_side(k, step):
                if step == 0:
                    variance("dn", 4 * k, DBANK + 1, rstd_d)
                if step == 1:
                    pe.wait_ge(sems["dn_done"], nth(3 * k, "dn_done"))
                    mm(bank[:, DBANK, :], wq[:], nrm[:]).then_inc(sems["q_mm"], 1)
                    mm(bank[:, DBANK + 1, :], wk[:], nrm[:]).then_inc(sems["k_mm"], 1)
                if step == 2:
                    pe.wait_ge(sems["q_copy"], nth(k, "q_copy"))
                    for j in range(QB):
                        last = mm(bank[:, DBANK, P * j:P * j + P], nrm[:, P * j:P * j + P], wv[:])
                    last.then_inc(sems["v_mm"], 1)
                    pe.wait_ge(sems["k_copy"], nth(k, "k_copy"))
                i = step - TILE0 - 2
                if 0 <= i < TILES:
                    h, j = i // QB, i % QB
                    pe.wait_ge(sems["probT"], nth(k, "probT", i + 1))
                    for t in range(j + 1):
                        last = mm(bank[:, DBANK + i % 2, 0:HD], probT[:, i % 2, P * t:P * t + P],
                                  vs[:, t, HD * h:HD * h + HD], t == 0, t == j)
                    last.then_inc(sems["pv"], 1)

            def attention_late(k, step):
                i = step - TILE0 - 1
                if 0 <= i < TILES:
                    pe.wait_ge(sems["prob"], nth(k, "prob", i + 1))
                    for t in range(i % QB + 1):
                        last = pe.transpose(bank[:, DBANK + i % 2, P * t:P * t + P], prob[:, i % 2, P * t:P * t + P],
                                            ident[:])
                    last.then_inc(sems["probT_mm"], 1)
                i = step - TILE0
                if 0 <= i < TILES:
                    h, j = i // QB, i % QB
                    if i == 0:
                        pe.wait_ge(sems["v_copy"], nth(k, "v_copy"))
                    if i >= 2:
                        pe.wait_ge(sems["pv_copy"], nth(k, "pv_copy", i - 1))
                    hd = slice(HD * h, HD * h + HD)
                    mm(bank[:, DBANK + i % 2, 0:P * (j + 1)], qs[hd, P * j:P * j + P], ks[hd, 0:P * (j + 1)],
                       True, False)
                    mm(bank[:, DBANK + i % 2, P * j:P * j + P], ident16[:], causal[:], False, True) \
                        .then_inc(sems["score"], 1)
                if step == SIDE_STEPS - 1:
                    pe.wait_ge(sems["att"], nth(k, "att"))
                    for j in range(QB):
                        last = pe.transpose(bank[:, DBANK, P * j:P * j + P], att[:, j, :], ident[:])
                    last.then_inc(sems["attT_mm"], 1)
                    pe.wait_ge(sems["attT"], nth(k, "attT"))
                    mm(bank[:, DBANK + 1, :], wo[:], attT[:]).then_inc(sems["o_mm"], 1)

            def ff_side(k, step):
                if step == 0:
                    variance("dn", 4 * k + 1, DBANK + 1, rstd_d)
                if step == 1:
                    pe.wait_ge(sems["dn_done"], nth(3 * k, "dn_done", 2))
                    for j, rows in enumerate(FFN_ROWS):
                        if j >= 2:
                            pe.wait_ge(sems["gs"], nth(k, "gs", j - 1))
                        mm(bank[0:rows, DBANK + j % 2, :], wgate[:, P * j:P * j + rows], nrm[:]) \
                            .then_inc(sems["gate_mm"], 1)
                if step == 2:
                    for j, rows in enumerate(FFN_ROWS):
                        if j < 2:
                            pe.wait_ge(sems["gs"], nth(k, "gs", j + 2))
                        else:
                            pe.wait_ge(sems["gu"], nth(k, "gu", j - 1))
                        mm(bank[0:rows, DBANK + (j + 1) % 2, :], wup[:, P * j:P * j + rows], nrm[:]) \
                            .then_inc(sems["up_mm"], 1)
                if step == 3:
                    for j, rows in enumerate(FFN_ROWS):
                        pe.wait_ge(sems["gu"], nth(k, "gu", max(j + 1, 2)))
                        last = mm(bank[:, DBANK, :], wdown[0:rows, j, :], gc[0:rows, j], j == 0, j == FB - 1)
                    last.then_inc(sems["down_mm"], 1)
                if step == 4:
                    pe.wait_ge(sems["x1"], nth(k, "x1"))
                    mm(bank[:, DBANK, :], center[:], x1[:]).then_inc(sems["dn_centered"], 1)
                if step == 5:
                    variance("dn", 4 * k + 2, DBANK + 1, rstd_d)
                if step == 7:
                    pe.wait_ge(sems["dn_done"], nth(3 * k, "dn_done", 3))
                    for j in range(2):
                        mm(bank[:, DBANK + j, :], fc[:, P * j:P * j + P], nrm[:]).then_inc(sems["fc_mm"], 1)
                if step == 8:
                    for j in range(2, MH):
                        pe.wait_ge(sems["gelu"], nth(k, "gelu", j - 1))
                        mm(bank[:, DBANK + j % 2, :], fc[:, P * j:P * j + P], nrm[:]).then_inc(sems["fc_mm"], 1)
                if step == 10:
                    pe.wait_ge(sems["gelu"], nth(k, "gelu", MH))
                    for j in range(MH):
                        last = mm(bank[:, DBANK, :], mean_h[:], gs[:, j], j == 0, j == MH - 1)
                    last.then_inc(sems["gmean"], 1)
                if step == 13:
                    pe.wait_ge(sems["dn_squared"], nth(4 * k + 3, "dn_squared"))
                    for j in range(MH):
                        last = mm(bank[:, DBANK + 1, :], mean_h[:], gs[:, j], j == 0, j == MH - 1)
                    last.then_inc(sems["dn_var"], 1)
                if step == 14:
                    for j in range(MH):
                        last = mm(bank[:, DBANK, :], projw[:, j, :], gc[:, j], j == 0, j == MH - 1)
                    last.then_inc(sems["pj_mm"], 1)

            def nothing(step):
                pass

            def slot_pair(k, last):
                mamba(2 * k - 1, 0, k, lambda step: ff_side(k - 1, step), nothing, (2 * k, 1, k - 1))
                mamba(2 * k, 1, k - 1, lambda step: attention_side(k, step), lambda step: attention_late(k, step),
                      None if last else (2 * k + 1, 0, k + 1))

            pe.wait_ge(sems["folded"], 2)
            head_norm(0, 0, 0)
            head_conv(0, 0, 0, False)
            mamba(0, 0, 0, nothing, nothing)
            ternary_weights()
            for step in range(SIDE_STEPS):
                attention_side(0, step)
                attention_late(0, step)
            head_norm(1, 0, 1)
            head_conv(1, 0, 1, True)
            with pe.Fori(1, SEQS - 1) as k:
                slot_pair(k, False)
            slot_pair(SEQS - 1, True)
            for step in range(SIDE_STEPS):
                ff_side(SEQS - 1, step)
            pe.wait_ge(sems["res"], nth(2 * SEQS - 2, "res"))
            head_norm(2 * SEQS - 1, 1, SEQS - 1)
            head_conv(2 * SEQS - 1, 1, SEQS - 1, True)
            mamba(2 * SEQS - 1, 1, SEQS - 1, nothing, nothing)

            pe.wait_ge(sems["res"], nth(2 * SEQS - 1, "res"))
            mm(bank[:, 4, 0:E], center[:], router[:]).then_inc(sems["router_mm"], 1)
            for b in range(SEQS):
                for j in range(QB):
                    last = pe.transpose(bank[:, b, P * j:P * j + P], x3[:, b, P * j:P * j + P], ident[:])
                last.then_inc(sems["xrow_mm"], 1)
            pe.wait_ge(sems["router_c"], 1)
            for g in range(G):
                last = mm(bank[:, 4, E * g:E * g + E], x3[:, g // QB, P * (g % QB):P * (g % QB) + P], router_c[:])
            last.then_inc(sems["logit_mm"], 1)
            pe.wait_ge(sems["onehot"], 1)
            mm(bank[:, 5, 0:E * G], earlier[:], onehot[:].rearrange("p e g -> p (e g)"))
            mm(bank[:, 6, 0:E * G], ones[:], onehot[:].rearrange("p e g -> p (e g)")).then_inc(sems["count_mm"], 1)

            def turn(i, s):
                pe.wait_ge(sems["nrow"], nth(i, "nrow"))
                pe.transpose(bank[:, 0, 0:P], nrow[:, s], ident[:]).then_inc(sems["xT_mm"], 1)

            def expert(i):
                return nc.values_load(expert_of[0:1, i:i + 1] if isinstance(i, int) else expert_of[0:1, bass.ds(i, 1)],
                                      engines=[mybir.EngineType.PE], min_val=0, max_val=E - 1,
                                      skip_runtime_bounds_check_because="clamped to the last expert on the chip")

            def up(i, s, reused):
                e = expert(i)
                of_expert = w1[:, bass.ds(e, 1), :].rearrange("p o n -> p (o n)")
                pe.wait_ge(sems["xT"], nth(i, "xT"))
                if reused:
                    pe.wait_ge(sems["es"], nth(i - 2, "es"))
                mm(bank[:, 1 + s, :], xT[:, s], of_expert[:, 0:MOE_H]).then_inc(sems["ea_mm"], 1)
                if reused:
                    pe.wait_ge(sems["ey"], nth(i - 2, "ey"))
                mm(bank[:, 3 + s, :], xT[:, s], of_expert[:, MOE_H:]).then_inc(sems["eg_mm"], 1)

            def turn_hidden(i, s):
                pe.wait_ge(sems["ey"], nth(i, "ey"))
                if not (isinstance(i, int) and i == 0):
                    pe.wait_ge(sems["eyT"], nth(i - 1, "eyT"))
                for j in range(MB):
                    last = pe.transpose(bank[:, 5, P * j:P * j + P], ey[:, s, P * j:P * j + P], ident[:])
                last.then_inc(sems["eyT_mm"], 1)

            def down(i, s, reused):
                e = expert(i)
                of_expert = w2[:, bass.ds(e, 1), :, :].rearrange("p o j n -> p (o j) n")
                pe.wait_ge(sems["eyT"], nth(i, "eyT"))
                if reused:
                    pe.wait_ge(sems["orow"], nth(i - 2, "orow"))
                for j in range(MB):
                    last = mm(bank[:, 6 + s, 0:D], eyT[:, s, P * j:P * j + P], of_expert[:, j, :], j == 0, j == MB - 1)
                last.then_inc(sems["down_e"], 1)

            pe.wait_ge(sems["experts"], 1)
            turn(0, 0)
            for i in range(4):
                up(i, i % 2, i >= 2)
                turn(i + 1, 1 - i % 2)
                if i >= 1:
                    turn_hidden(i - 1, 1 - i % 2)
                if i >= 2:
                    down(i - 2, i % 2, False)
            with pe.Fori(2, NT // 2 - 1) as pair:
                for s in range(2):
                    i = 2 * pair + s
                    up(i, s, True)
                    turn(i + 1, 1 - s)
                    turn_hidden(i - 1, 1 - s)
                    down(i - 2, s, True)
            for i in range(NT - 2, NT + 2):
                if i < NT:
                    up(i, i % 2, True)
                if i + 1 < NT:
                    turn(i + 1, (i + 1) % 2)
                if i - 1 < NT:
                    turn_hidden(i - 1, (i - 1) % 2)
                down(i - 2, i % 2, True)


def kernel(**a):
    import numpy as np
    import concourse.bacc as bacc
    from concourse import mybir
    from concourse.bass_utils import run_bass_kernel_spmd

    a = {k: np.asarray(v) for k, v in a.items()}
    x = a["L0_attn_x"]
    SEQS, T, D = x.shape
    f32 = np.float32
    half_cols = lambda v: v.reshape(2, 128).T

    STATE, E, QB, BCR = 16, 8, T // 128, 32
    xp = a["L0_attn_x_proj_w"]
    eye = np.eye(128, dtype=f32)
    pick = np.zeros((3 * BCR, BCR, 128), f32)
    for part in range(3):
        for n in range(BCR):
            pick[part * BCR + n, n, :] = 1
    TOKENS = SEQS * T
    G = TOKENS // 128
    NT = G + E + (G + E) % 2
    blank = np.zeros((NT * 128, D + 4), f32)
    blank[:, -1] = TOKENS + np.arange(NT * 128)
    heads = np.repeat(np.arange(2), 2)

    def per_head(w):
        return w.reshape(2, 32, D)[heads].reshape(128, D).T

    put = {
        "xT": x.transpose(0, 2, 1),
        "ident": eye, "ident16": eye, "center": eye - f32(1 / 128), "mean_d": np.full((128, 128), 1 / 128, f32),
        "mean_h": np.full((128, 128), 1 / 512, f32),
        "causal": np.triu(np.full((128, 128), -1e30, f32), 1),
        "pick": pick, "blank": blank,
        "eminus": np.broadcast_to(np.arange(E, dtype=f32) - E, (128, E)),
        "token_id": np.arange(TOKENS, dtype=f32).reshape(G, 128).T,
        "earlier": np.triu(np.ones((128, 128), f32), 1),
        "new_expert": np.broadcast_to((np.arange(G) > 0).astype(f32), (128, E, G)),
        "tile_starts": np.broadcast_to(128 * np.arange(G, dtype=f32), (128, G)),
        "tile_id": np.broadcast_to(np.arange(NT, dtype=f32), (128, NT)),
        "norm_m": a["L0_attn_norm_m_w"][:, None], "norm_a": a["L0_attn_norm_attn_w"][:, None],
        "norm_f": a["L0_attn_norm_ffn_w"][:, None],
        "m0_win": a["L0_attn_in_proj_w"].T, "m0_cw": a["L0_attn_conv_w"][:, 0, :].T,
        "m0_cb": half_cols(a["L0_attn_conv_b"]), "m0_wx": xp.T, "m0_dtT": a["L0_attn_dt_w"].T,
        "m0_db": half_cols(a["L0_attn_dt_b"]), "m0_Alog": a["L0_attn_A_log"].reshape(2, 128, STATE),
        "m0_D": half_cols(a["L0_attn_D_skip"]), "m0_wo": a["L0_attn_out_proj_w"].T,
        "m1_win": a["L1_attn_W_in"], "m1_cw": a["L1_attn_conv_w"][:, 0, :],
        "m1_cb": half_cols(a["L1_attn_conv_b"]), "m1_wx": a["L1_attn_W_x"], "m1_dtT": a["L1_attn_W_dt"],
        "m1_db": half_cols(a["L1_attn_b_dt"]), "m1_Alog": a["L1_attn_A_log"].reshape(2, 128, STATE),
        "m1_D": half_cols(a["L1_attn_D"]), "m1_wo": a["L1_attn_W_out"],
        "qT": a["L0_attn_q_w"].T, "kT": per_head(a["L0_attn_k_w"]), "vT": per_head(a["L0_attn_v_w"]),
        "oT": a["L0_attn_o_w"].T, "gateT": a["L0_attn_gate_w"].T, "upT": a["L0_attn_up_w"].T,
        "downT": a["L0_attn_down_w"].T, "fcT": a["L0_ffn_W_fc"].T, "projT": a["L0_ffn_W_proj"].T,
        "lnw": a["L0_ffn_ln_w"].reshape(4, 128).T, "lnb": a["L0_ffn_ln_b"].reshape(4, 128).T,
        "router": a["L1_ffn_router_w"], "router_b": a["L1_ffn_router_b"][None, :],
        "w1": a["L1_ffn_w1"], "w2": a["L1_ffn_w2"],
    }
    import ml_dtypes
    for name in ("pick", "ident16", "causal"):
        put[name] = put[name].astype(ml_dtypes.bfloat16)
    nc = bacc.Bacc("TRN2", target_bir_lowering=False, num_devices=1)
    arrays, dram = {}, {}
    for name, v in put.items():
        v = np.ascontiguousarray(v)
        arrays["in_" + name] = v
        dram[name] = nc.dram_tensor("in_" + name, v.shape, mybir.dt.from_np(v.dtype), kind="ExternalInput").ap()
    out = nc.dram_tensor("out_rows", (TOKENS + NT * 128, D), mybir.dt.float32, kind="ExternalOutput").ap()
    sorted_rows = nc.dram_tensor("sorted_rows", (NT * 128, D + 4), mybir.dt.float32).ap()
    build(nc, dram, sorted_rows, out)
    r = run_bass_kernel_spmd(nc, [arrays], core_ids=[0])
    return r.results[0]["out_rows"][0:TOKENS].reshape(SEQS, T, D)
```

```python
from contextlib import ExitStack

import concourse.bass as bass
from concourse import mybir

P = 128
F32 = mybir.dt.float32
BF16 = mybir.dt.bfloat16
ALU = mybir.AluOpType
ACT = mybir.ActivationFunctionType
AX = mybir.AxisListType

LN_EPS = 1e-5
RMS_EPS = 1e-6
QUANT_EPS = 1e-6
N_HEADS = 4
EXP_LN = "natural_log_exp_and_others"


HBUF = 3
CBUF = 3
YLAG = 3

PER = {}
SETUP_DONE = []


def build(nc, d, sorted_rows, out):
    SEQS, D, T = d["xT"].shape
    TAPS = d["m0_cw"].shape[2]
    STATE = d["m0_Alog"].shape[2]
    HALVES = d["m0_Alog"].shape[0]
    FFN_H = d["gateT"].shape[1]
    FB = (FFN_H + P - 1) // P
    FFN_ROWS = [min(P, FFN_H - P * j) for j in range(FB)]
    MH = d["fcT"].shape[1] // P
    E = d["w1"].shape[0]
    MOE_H = d["w2"].shape[1]
    MB = MOE_H // P
    QB = T // P
    HD = D // N_HEADS
    SCALE = float(HD) ** -0.5
    BCR = 2 * STATE
    G = SEQS * QB
    NT = d["blank"].shape[0] // P
    ROW = d["blank"].shape[1]
    MEAN, RSTD, PROB, TOKEN = D, D + 1, D + 2, D + 3
    DTR = {0: 1, 1: d["m1_dtT"].shape[0]}
    assert D == P and T == 512 and HALVES == 2

    with ExitStack() as ctx:
        def sb(name, shape, dt=F32):
            return ctx.enter_context(nc.sbuf_tensor(name, shape, dt))

        bank = ctx.enter_context(nc.psum_tensor("bank", [P, 8, T], F32))
        sems = {}

        def new_sem(name, per=1, uses=("",)):
            handle = ctx.enter_context(nc.semaphore(name))
            for i, use in enumerate(uses):
                sems[use + name] = handle
                PER[use + name] = per * len(uses)
                BEFORE[use + name] = per * i

        ident = sb("ident", [P, P])
        center = sb("center", [P, P])
        mean_d = sb("mean_d", [P, P])
        mean_h = sb("mean_h", [P, P])
        ones = sb("ones", [P, P])
        causal = sb("causal", [P, P], BF16)
        pick = sb("pick", [3 * BCR, BCR, P], BF16)
        eminus = sb("eminus", [P, E])
        token_id = sb("token_id", [P, G])
        earlier = sb("earlier", [P, P])
        new_expert = sb("new_expert", [P, E, G])
        tile_starts = sb("tile_starts", [P, G])
        tile_id = sb("tile_id", [P, NT])
        ident16 = sb("ident16", [P, P], BF16)
        eps_ln = sb("eps_ln", [P, 1])
        eps_rms = sb("eps_rms", [P, 1])
        one_col = sb("one_col", [P, 1])
        M = []
        for m in range(2):
            M.append(dict(
                win=sb(f"m{m}_win_s", [P, 2 * HALVES * P]), cw=sb(f"m{m}_cw_s", [P, HALVES, TAPS]),
                cb=sb(f"m{m}_cb_s", [P, HALVES]),
                wx=sb(f"m{m}_wx_s", [P, HALVES, DTR[m] + BCR]), wdt=sb(f"m{m}_wdt_s", [DTR[m], HALVES * P]),
                db=sb(f"m{m}_db_s", [P, HALVES]), A=sb(f"m{m}_A_s", [P, HALVES, STATE]),
                dskip=sb(f"m{m}_dskip_s", [P, HALVES]), wo=sb(f"m{m}_wo_s", [P, HALVES, D])))
        norm_m = sb("norm_m", [P, 1])
        norm_a = sb("norm_a", [P, 1])
        norm_f = sb("norm_f", [P, 1])
        wq = sb("wq", [P, D])
        wk = sb("wk", [P, D])
        wv = sb("wv", [P, D])
        wo = sb("wo", [P, D])
        wgate = sb("wgate", [P, FFN_H])
        wup = sb("wup", [P, FFN_H])
        wdown = sb("wdown", [P, FB, D])
        fc = sb("fc", [P, MH * P])
        proj = sb("proj", [P, MH, D])
        lnw = sb("lnw", [P, MH])
        lnb = sb("lnb", [P, MH])
        projw = sb("projw", [P, MH, D])
        projb = sb("projb", [P, 1])
        router = sb("router", [P, E])
        router_b = sb("router_b", [P, E])
        w1 = sb("w1", [P, E, 2 * MOE_H])
        w2 = sb("w2", [P, E, MB, D])

        xin = sb("xin", [P, T])
        xl = sb("xl", [P, T])
        xn = [sb(f"xn{m}", [P, T]) for m in range(2)]
        rstd_m = sb("rstd_m", [P, T])
        xs_sets = [sb(f"xs{i}", [P, HALVES, T]) for i in range(2)]
        zs_sets = [sb(f"zs{i}", [P, HALVES, T]) for i in range(2)]
        dt_rows = sb("dt_rows", [DTR[1], T])
        parts = sb("parts", [3 * BCR, T], BF16)
        mid = sb("mid", [BCR, T], BF16)
        delta = sb("delta", [P, HALVES, T])
        du = sb("du", [P, HALVES, T])
        yd = du
        dbu = sb("dbu", [P, 2, HALVES, T])
        hst = sb("hst", [P, HBUF, HALVES, T])
        sp_abs, sp_max = hst[:, 0], hst[:, 1]
        hc = sb("hc", [P, 4, HALVES, T])
        csb = sb("csb", [P, CBUF, T])
        rest = csb[0:BCR, 0, :]
        xkeep = sb("xkeep", [P, T])
        h0 = sb("h0", [P, T])
        nrm = sb("nrm", [P, T])
        rstd_d = sb("rstd_d", [P, T])
        qs = sb("qs", [P, T])
        ks = sb("ks", [P, T])
        vs = sb("vs", [P, QB, D])
        nmax = sb("nmax", [P, N_HEADS * QB])
        psums = sb("psums", [P, QB, N_HEADS])
        rsums = sb("rsums", [P, QB, N_HEADS])
        attT = qs
        h1 = sb("h1", [P, T])
        gs = sb("gs", [P, 4, T])
        gc = sb("gc", [P, 4, T])
        prob, probT = gs, gc
        x1 = sb("x1", [P, T])
        att = x1[:].rearrange("p (j n) -> p j n", j=QB)
        x2 = sb("x2", [P, T])
        x3 = sb("x3", [P, SEQS, T])
        router_c = sb("router_c", [P, E])
        carved = [0]

        def in_gc(*dims):
            size = 1
            for n in dims:
                size *= n
            at = carved[0]
            carved[0] += size
            flat_tile = gc[:].rearrange("p j t -> p (j t)")[:, at:at + size]
            return flat_tile.rearrange("p (a b) -> p a b", b=dims[1]) if len(dims) == 2 else flat_tile

        stats = sb("stats", [P, G, 6])
        meanvar = sb("meanvar", [P, G, 2])
        lg = in_gc(G, E)
        lmax = sb("lmax", [P, G])
        le = in_gc(G, E)
        lsum = sb("lsum", [P, G])
        cand = in_gc(G, E)
        first_of = sb("first_of", [P, G])
        onehot = in_gc(E, G)
        upto = in_gc(E, G)
        place = in_gc(E, G)
        starts = in_gc(E, G)
        tiles_of = sb("tiles_of", [P, E])
        tiles_upto = sb("tiles_upto", [P, E])
        tiles_before = sb("tiles_before", [P, E])
        row_f = sb("row_f", [P, G])
        row_of = sb("row_of", [P, G], mybir.dt.uint32)
        past = in_gc(NT, E)
        expert_f = sb("expert_f", [P, NT])
        expert_of = sb("expert_of", [P, NT], mybir.dt.int32)
        target = sb("target", [P, 2], mybir.dt.uint32)
        trows = hc[:].rearrange("p a h t -> p (a h t)")[:, 0:G * ROW].rearrange("p (g w) -> p g w", w=ROW)
        srows = hc[:].rearrange("p a h t -> p (a h t)")[:, 0:NT * ROW].rearrange("p (g w) -> p g w", w=ROW)
        nrow = gs[:, 0, 0:2 * D].rearrange("p (s n) -> p s n", s=2)
        xT = gs[:, 1, 0:2 * P].rearrange("p (s n) -> p s n", s=2)
        orow = gs[:, 2, 0:2 * D].rearrange("p (s n) -> p s n", s=2)
        es, ey, eyT = delta, du, xs_sets[0]
        absr = sb("absr", [P, 2])
        thr = sb("thr", [P, 4])
        qtmp, qtmp2 = gs[:, 0], gs[:, 1]

        MBANK, DBANK = 0, 6
        TILES = N_HEADS * QB
        for name, per in (
                ("first_loaded", 0), ("early_loaded", 0), ("late_loaded", 0), ("w_loaded", 0), ("setup_dve", 0), ("setup_act", 0), ("setup_pe", 0),
                ("x_loaded", 16), ("even_stored", 16), ("odd_stored", 16), ("xkeep", 1),
                ("ln_centered", 1), ("ln_squared", 1), ("ln_var", 1), ("ln_logged", 1), ("ln_rstd", 1), ("ln_done", 1),
                ("rms_squared", 1), ("rms_var", 1), ("rms_logged", 1), ("rms_rstd", 1), ("rms_done", 1),
                ("dn_squared", 1), ("dn_var", 1), ("dn_logged", 1), ("dn_rstd", 1), ("dn_done", 1), ("dn_centered", 1),
                ("raw", 2), ("tap", TAPS * HALVES), ("z", 2), ("xs", 2), ("zs", 2), ("proj", 1), ("dtrows", 1),
                ("hi", 1), ("rest", 1), ("mid", 1), ("midcopy", 1), ("lo", 1), ("dtp", 2),
                ("spabs", 2), ("spmax", 2), ("spexp", 1), ("spln", 1), ("delta", 1), ("du", 1),
                ("bbc", STATE), ("cbc", STATE), ("dA", 2 * STATE), ("ccopy", STATE),
                ("dbu", STATE), ("scan", 2 * STATE), ("hc", STATE), ("yacc", STATE),
                ("yd", 2), ("yg", 2), ("out", 1), ("res", 1),
                ("q_mm", 1), ("k_mm", 1), ("v_mm", 1), ("q_copy", 1), ("k_copy", 1), ("v_copy", 1),
                ("score", TILES), ("smax", TILES), ("prob", TILES), ("probT_mm", TILES),
                ("probT", TILES), ("pv", TILES), ("pv_copy", TILES), ("recip", 1), ("att", 1), ("attT_mm", 1),
                ("attT", 1), ("o_mm", 1), ("h1", 1),
                ("gate_mm", FB), ("up_mm", FB), ("gs", FB), ("gu", FB), ("down_mm", 1),
                ("ffn_res", 1), ("x1", 1),
                ("fc_mm", MH), ("gelu", MH), ("gmean", 1), ("gcen", MH), ("gsq", MH), ("pj_mm", 1), ("pj_scaled", 1),
                ("x2", 1),
("router_mm", 1), ("router_c", 1), ("xrow_mm", SEQS), ("xrow", SEQS), ("logit_mm", 1), ("stats", G),
                ("meanvar", G), ("mlog", 1), ("rstd", 1), ("lscaled", 1), ("lbiased", 1), ("lmax", 1), ("lsub", 1),
                ("lexp", 1), ("lsum", 1), ("eqm", 1), ("cand", 1), ("first", 1), ("onehot", 1), ("count_mm", 1),
                ("route", 0), ("rows_made", 0), ("row_of", 1), ("experts", 1), ("scattered", 16), ("blanked", 16),
                ("srows_first", 16), ("srows_rest", 16),
                ("nrow", 1), ("xT_mm", 1), ("xT", 1), ("ea_mm", 1), ("eg_mm", 1), ("es", 1), ("ey", 1),
                ("eyT_mm", 1), ("eyT", 1), ("down_e", 1), ("target", 1), ("orow", 1)):
            PER[name] = per
            sems[name] = ctx.enter_context(nc.semaphore(name))

        def nth(i, name, k=1):
            return i * PER[name] + k

        STORED = ("even_stored", "odd_stored")
        FIRST_TILES = 4
        HEAD = 6
        SIDE_STEPS = HEAD + STATE
        TILE0 = 3

        def set_of(c, m):
            return c % 2 if isinstance(c, int) else 1 - m

        def xl_of(c):
            return x2 if isinstance(c, int) and c == 1 else xl

        def seq(t, k):
            return t[:, k, :] if isinstance(k, int) else t[:, bass.ds(k, 1), :].rearrange("p o t -> p (o t)")

        first = [(dst[:], d[key]) for dst, key in ((center, "center"), (mean_d, "mean_d"), (norm_m, "norm_m"))]

        def weights_of(m):
            return [(M[m]["win"][:], d[f"m{m}_win"]), (M[m]["cw"][:], d[f"m{m}_cw"]),
                    (M[m]["cb"][:], d[f"m{m}_cb"]),
                    (M[m]["A"][:], d[f"m{m}_Alog"].rearrange("h p n -> p h n")),
                    (M[m]["wx"][:], d[f"m{m}_wx"].rearrange("(h p) n -> p h n", p=P)),
                    (M[m]["wdt"][:], d[f"m{m}_dtT"]),
                    (M[m]["db"][:], d[f"m{m}_db"]),
                    (M[m]["dskip"][:], d[f"m{m}_D"]),
                    (M[m]["wo"][:], d[f"m{m}_wo"].rearrange("(h p) n -> p h n", p=P))]

        early = weights_of(0) + [(pick[:], d["pick"]), (ident[:], d["ident"])]
        late = weights_of(1)
        late += [(dst[:], d[key]) for dst, key in (
            (mean_h, "mean_h"), (causal, "causal"), (ident16, "ident16"), (eminus, "eminus"), (token_id, "token_id"),
            (earlier, "earlier"), (new_expert, "new_expert"), (tile_starts, "tile_starts"), (tile_id, "tile_id"),
            (norm_a, "norm_a"), (norm_f, "norm_f"), (wq, "qT"), (wk, "kT"), (wv, "vT"), (wo, "oT"),
            (wgate, "gateT"), (wup, "upT"), (fc, "fcT"), (router, "router"),
            (lnw, "lnw"), (lnb, "lnb"))]
        for j, rows in enumerate(FFN_ROWS):
            late.append((wdown[0:rows, j, :], d["downT"][P * j:P * j + rows, :]))
        late.append((proj[:], d["projT"].rearrange("(j p) n -> p j n", p=P)))
        late.append((router_b[:], d["router_b"].to_broadcast([P, E])))
        experts = [(w1[:], d["w1"].rearrange("e p n -> p e n")),
                   (w2[:], d["w2"].rearrange("e (j p) n -> p e j n", p=P))]

        block = ctx.enter_context(nc.Block())

        @block.sync
        def _(sp):
            def load_x(k):
                sp.dma_start(xin[:], d["xT"][bass.ds(k, 1), :, :].rearrange("o p t -> (o p) t")) \
                    .then_inc(sems["x_loaded"], 16)

            load_x(0)
            for dst, src in first:
                sp.dma_start(dst, src).then_inc(sems["first_loaded"], 16)
            for dst, src in early:
                sp.dma_start(dst, src).then_inc(sems["early_loaded"], 16)
            sp.wait_ge(sems["xkeep"], nth(0, "xkeep"))
            load_x(1)
            for dst, src in late:
                sp.dma_start(dst, src).then_inc(sems["late_loaded"], 16)
            for dst, src in experts:
                sp.dma_start(dst, src).then_inc(sems["w_loaded"], 16)
            sp.dma_start(sorted_rows, d["blank"]).then_inc(sems["blanked"], 16)
            with sp.Fori(2, SEQS) as k:
                sp.wait_ge(sems["xkeep"], nth(k - 1, "xkeep"))
                load_x(k)
            sp.wait_ge(sems["scattered"], nth(0, "scattered", 16 * G))
            by_tile = sorted_rows.rearrange("(i p) w -> p i w", p=P)
            sp.dma_start(srows[:, 0:FIRST_TILES, :], by_tile[:, 0:FIRST_TILES, :]).then_inc(sems["srows_first"], 16)
            sp.dma_start(srows[:, FIRST_TILES:, :], by_tile[:, FIRST_TILES:, :]).then_inc(sems["srows_rest"], 16)

        @block.gpsimd
        def _(pool):
            def ff_side(k, step):
                if step == 7:
                    pool.wait_ge(sems["ffn_res"], nth(k, "ffn_res"))
                    pool.tensor_tensor(x1[:], nrm[:], xkeep[:], ALU.add).then_inc(sems["x1"], 1)

            def mamba(c, side):
                for step in range(HEAD):
                    side(step)
                for n in range(STATE):
                    side(HEAD + n)
                    pool.wait_ge(sems["scan"], nth(c, "scan", 2 * n + 2))
                    pool.wait_ge(sems["ccopy"], nth(c, "ccopy", n + 1))
                    if n >= 4:
                        pool.wait_ge(sems["yacc"], nth(c, "yacc", n - 3))
                    pool.tensor_tensor(hc[:, n % 4], hst[:, n % HBUF],
                                       csb[:, n % CBUF:n % CBUF + 1, :].to_broadcast([P, HALVES, T]),
                                       ALU.mult).then_inc(sems["hc"], 1)

            mamba(0, lambda step: None)
            mamba(1, lambda step: None)
            ff_side(0, 7)
            with pool.Fori(1, SEQS - 1) as k:
                mamba(2 * k, lambda step: None)
                mamba(2 * k + 1, lambda step: ff_side(k, step))
            mamba(2 * SEQS - 2, lambda step: None)
            ff_side(SEQS - 1, 7)
            mamba(2 * SEQS - 1, lambda step: None)

            pool.wait_ge(sems["blanked"], 16)
            pool.wait_ge(sems["rows_made"], 5)
            pool.wait_ge(sems["row_of"], 1)
            for g in range(G):
                pool.indirect_dma_start(sorted_rows, bass.IndirectOffsetOnAxis(row_of[:, g:g + 1], 0),
                                        trows[:, g, :], None).then_inc(sems["scattered"], 16)

            for i in range(NT):
                pool.wait_ge(sems["orow"], nth(i, "orow"))
                pool.indirect_dma_start(out, bass.IndirectOffsetOnAxis(target[:, i % 2:i % 2 + 1], 0),
                                        orow[:, i % 2, :], None).then_inc(sems[STORED[i % 2]], 16)
            pool.wait_ge(sems["even_stored"], 16 * NT // 2)
            pool.wait_ge(sems["odd_stored"], 16 * NT // 2)

        @block.scalar
        def _(act):
            def exp_A_log(m):
                act.activation(M[m]["A"][:], M[m]["A"][:], ACT.Exp).then_inc(sems["setup_act"], 1)

            act.preload_act_table_set(EXP_LN)
            act.wait_ge(sems["setup_dve"], 1)

            def inverse_root(norm, i, var_bank, eps, tile):
                act.wait_ge(sems[norm + "_var"], nth(i, norm + "_var"))
                act.activation(tile[:], bank[:, var_bank, :], ACT.Ln, bias=eps[:]).then_inc(sems[norm + "_logged"], 1)
                act.wait_ge(sems[norm + "_logged"], nth(i, norm + "_logged"))
                act.activation(tile[:], tile[:], ACT.Exp, scale=-0.5).then_inc(sems[norm + "_rstd"], 1)

            def head_square(c, centered=0):
                act.wait_ge(sems["ln_centered"], nth(c, "ln_centered"))
                act.activation(rstd_m[:], bank[:, centered, :], ACT.Square).then_inc(sems["ln_squared"], 1)

            def head_norm(c, m, k):
                inverse_root("ln", c, 1, eps_ln, rstd_m)
                if m == 0:
                    act.wait_ge(sems["ln_done"], nth(c, "ln_done"))
                    act.activation(rstd_m[:], xl_of(c)[:], ACT.Square).then_inc(sems["rms_squared"], 1)
                    inverse_root("rms", k, 1, eps_rms, rstd_m)

            def head_silu(c, m):
                xs, zs = xs_sets[set_of(c, m)], zs_sets[set_of(c, m)]
                for h in range(HALVES):
                    act.wait_ge(sems["tap"], nth(c, "tap", HALVES * (TAPS - 1) + h + 1))
                    act.activation(xs[:, h], dbu[:, 0, h], ACT.Silu, bias=M[m]["cb"][:, h:h + 1]) \
                        .then_inc(sems["xs"], 1)
                for h in range(HALVES):
                    act.wait_ge(sems["z"], nth(c, "z", h + 1))
                    act.activation(zs[:, h], bank[:, DBANK + h, :], ACT.Silu).then_inc(sems["zs"], 1)
                act.preload_act_table_set(EXP_LN)

            def mamba(c, m, side, follower=None):
                def norm_ahead(step):
                    if follower and follower[1] == 0:
                        if step == 3:
                            head_square(follower[0], 4)
                        if step == 4:
                            inverse_root("ln", follower[0], 5, eps_ln, rstd_m)
                        if step == 5:
                            act.wait_ge(sems["ln_done"], nth(follower[0], "ln_done"))
                            act.activation(rstd_m[:], xl_of(follower[0])[:], ACT.Square) \
                                .then_inc(sems["rms_squared"], 1)
                        if step == 7:
                            inverse_root("rms", follower[2], 5, eps_rms, rstd_m)

                w = M[m]
                bc0 = 0 if m == 0 else DTR[1]
                dt0 = BCR if m == 0 else 0
                act.wait_ge(sems["proj"], nth(c, "proj"))
                act.activation(dt_rows[0:DTR[m], :], bank[dt0:dt0 + DTR[m], 0, :], ACT.Copy) \
                    .then_inc(sems["dtrows"], 1)
                act.activation(parts[0:BCR, :], bank[bc0:bc0 + BCR, 0, :], ACT.Copy).then_inc(sems["hi"], 1)
                side(0)
                act.wait_ge(sems["mid"], nth(c, "mid"))
                act.activation(parts[BCR:2 * BCR, :], mid[:], ACT.Copy).then_inc(sems["midcopy"], 1)
                for h in range(HALVES):
                    act.wait_ge(sems["dtp"], nth(c, "dtp", h + 1))
                    act.activation(sp_abs[:, h], bank[:, 2 + h, :], ACT.Abs, bias=w["db"][:, h:h + 1]) \
                        .then_inc(sems["spabs"], 1)
                act.wait_ge(sems["spabs"], nth(c, "spabs", 2))
                act.activation(sp_abs[:], sp_abs[:], ACT.Exp, scale=-1.0).then_inc(sems["spexp"], 1)
                act.wait_ge(sems["spexp"], nth(c, "spexp"))
                act.activation(sp_abs[:], sp_abs[:], ACT.Ln, bias=one_col[:]).then_inc(sems["spln"], 1)
                side(1)
                for step in range(2, HEAD):
                    norm_ahead(step)
                    side(step)
                act.wait_ge(sems["delta"], nth(c, "delta"))
                act.wait_ge(sems["spmax"], nth(c, "spmax", 2))
                for n in range(STATE):
                    act.wait_ge(sems["cbc"], nth(c, "cbc", n + 1))
                    if n >= CBUF:
                        act.wait_ge(sems["hc"], nth(c, "hc", n - CBUF + 1))
                    act.activation(csb[:, n % CBUF], bank[:, 1, :], ACT.Copy).then_inc(sems["ccopy"], 1)
                    for h in range(HALVES):
                        if n >= 1:
                            act.wait_ge(sems["scan"], nth(c, "scan", 2 * n - 1 + h))
                        act.activation(bank[:, 2 + h, :], delta[:, h], ACT.Exp,
                                       scale=w["A"][:, h, n:n + 1]).then_inc(sems["dA"], 1)
                    if follower and follower[1] == 1 and n == STATE - 1:
                        head_square(follower[0])
                    side(HEAD + n)
                    norm_ahead(HEAD + n)
                if follower:
                    if follower[1] == 1:
                        head_norm(*follower)
                    head_silu(follower[0], follower[1])

            def keep_x():
                act.activation(xkeep[:], xin[:], ACT.Copy).then_inc(sems["xkeep"], 1)

            def attention_side(k, step):
                if step == 0:
                    act.wait_ge(sems["res"], nth(side_res(k), "res"))
                    act.activation(rstd_d[:], h0[:], ACT.Square).then_inc(sems["dn_squared"], 1)
                    if not (isinstance(k, int) and k == 0):
                        keep_x()
                    inverse_root("dn", 4 * k, DBANK + 1, eps_rms, rstd_d)
                if step == 1:
                    act.wait_ge(sems["q_mm"], nth(k, "q_mm"))
                    act.activation(qs[:], bank[:, DBANK, :], ACT.Copy, scale=SCALE).then_inc(sems["q_copy"], 1)
                if step == 2:
                    act.wait_ge(sems["v_mm"], nth(k, "v_mm"))
                    act.activation(vs[:], bank[:, DBANK, :].rearrange("p (j n) -> p j n", j=QB), ACT.Copy) \
                        .then_inc(sems["v_copy"], 1)
                i = step - TILE0 - 2
                if 0 <= i < TILES:
                    keys = P * (i % QB + 1)
                    act.wait_ge(sems["probT_mm"], nth(k, "probT_mm", i + 1))
                    if i >= 2:
                        act.wait_ge(sems["pv"], nth(k, "pv", i - 1))
                    act.activation(probT[:, i % 2, 0:keys], bank[:, DBANK + i % 2, 0:keys], ACT.Copy) \
                        .then_inc(sems["probT"], 1)
                i = step - TILE0 - 1
                if 0 <= i < TILES:
                    h, j = i // QB, i % QB
                    keys = P * (j + 1)
                    act.wait_ge(sems["smax"], nth(k, "smax", i + 1))
                    if i >= 2:
                        act.wait_ge(sems["probT_mm"], nth(k, "probT_mm", i - 1))
                    act.activation(prob[:, i % 2, 0:keys], bank[:, DBANK + i % 2, 0:keys], ACT.Exp,
                                   bias=nmax[:, i:i + 1], accum_out=psums[:, j, h:h + 1]) \
                        .then_inc(sems["prob"], 1)
                i = step - TILE0 - 2
                if 0 <= i < TILES:
                    h, j = i // QB, i % QB
                    act.wait_ge(sems["pv"], nth(k, "pv", i + 1))
                    act.activation(att[:, j, HD * h:HD * h + HD], bank[:, DBANK + i % 2, 0:HD], ACT.Copy) \
                        .then_inc(sems["pv_copy"], 1)
                if step == SIDE_STEPS - 1:
                    act.wait_ge(sems["attT_mm"], nth(k, "attT_mm"))
                    act.activation(attT[:], bank[:, DBANK, :], ACT.Copy).then_inc(sems["attT"], 1)

            def ff_side(k, step):
                if step == 0:
                    act.wait_ge(sems["h1"], nth(k, "h1"))
                    act.activation(rstd_d[:], h1[:], ACT.Square).then_inc(sems["dn_squared"], 1)
                    inverse_root("dn", 4 * k + 1, DBANK + 1, eps_rms, rstd_d)
                if step == 1:
                    for j, rows in enumerate(FFN_ROWS):
                        act.wait_ge(sems["gate_mm"], nth(k, "gate_mm", j + 1))
                        act.activation(gs[0:rows, j], bank[0:rows, DBANK + j % 2, :], ACT.Silu) \
                            .then_inc(sems["gs"], 1)
                    act.preload_act_table_set(EXP_LN)
                if step == 8:
                    act.wait_ge(sems["dn_centered"], nth(k, "dn_centered"))
                    act.activation(rstd_d[:], bank[:, DBANK, :], ACT.Square).then_inc(sems["dn_squared"], 1)
                if step == 9:
                    inverse_root("dn", 4 * k + 2, DBANK + 1, eps_ln, rstd_d)
                if step == 12:
                    for j in range(MH):
                        act.wait_ge(sems["fc_mm"], nth(k, "fc_mm", j + 1))
                        act.activation(gs[:, j], bank[:, DBANK + j % 2, :], ACT.Gelu).then_inc(sems["gelu"], 1)
                    act.preload_act_table_set(EXP_LN)
                if step in (16, 17):
                    for j in range(MH // 2 * (step - 16), MH // 2 * (step - 15)):
                        act.wait_ge(sems["gcen"], nth(k, "gcen", j + 1))
                        act.activation(gs[:, j], gc[:, j], ACT.Square).then_inc(sems["gsq"], 1)
                if step == 19:
                    inverse_root("dn", 4 * k + 3, DBANK + 1, eps_ln, rstd_d)

            def side_res(k):
                return 0 if isinstance(k, int) and k == 0 else 2 * k - 1

            def beside_attention(k, follower):
                mamba(2 * k, 1, lambda step: attention_side(k, step), follower)

            def beside_ff(k):
                mamba(2 * k + 1, 0, lambda step: ff_side(k, step), (2 * k + 2, 1, k))

            head_square(0)
            head_norm(0, 0, 0)
            act.wait_ge(sems["early_loaded"], 16 * len(early))
            exp_A_log(0)
            head_silu(0, 0)
            keep_x()
            mamba(0, 0, lambda step: None, (1, 0, 1))
            act.wait_ge(sems["late_loaded"], 16 * len(late))
            exp_A_log(1)
            mamba(1, 0, lambda step: attention_side(0, step))
            for step in range(SIDE_STEPS):
                ff_side(0, step)
            head_square(2)
            head_norm(2, 1, 0)
            head_silu(2, 1)
            with act.Fori(1, SEQS - 1) as k:
                beside_attention(k, (2 * k + 1, 0, k + 1))
                beside_ff(k)
            beside_attention(SEQS - 1, None)
            for step in range(SIDE_STEPS):
                ff_side(SEQS - 1, step)
            head_square(2 * SEQS - 1)
            head_norm(2 * SEQS - 1, 1, SEQS - 1)
            head_silu(2 * SEQS - 1, 1)
            mamba(2 * SEQS - 1, 1, lambda step: None)

            act.preload_act_table_set(EXP_LN)
            act.wait_ge(sems["router_mm"], 1)
            act.activation(router_c[:], bank[:, 4, 0:E], ACT.Copy).then_inc(sems["router_c"], 1)
            act.wait_ge(sems["res"], nth(2 * SEQS - 1, "res"))
            for b in range(SEQS):
                act.wait_ge(sems["xrow_mm"], nth(0, "xrow_mm", b + 1))
                act.activation(trows[:, QB * b:QB * b + QB, 0:D], bank[:, b, :].rearrange("p (j n) -> p j n", n=D),
                               ACT.Copy).then_inc(sems["xrow"], 1)
            act.wait_ge(sems["meanvar"], nth(0, "meanvar", G))
            act.activation(trows[:, :, RSTD], meanvar[:, :, 1], ACT.Ln, bias=eps_ln[:]).then_inc(sems["mlog"], 1)
            act.wait_ge(sems["mlog"], 1)
            act.activation(trows[:, :, RSTD], trows[:, :, RSTD], ACT.Exp, scale=-0.5).then_inc(sems["rstd"], 1)
            act.wait_ge(sems["lsub"], 1)
            act.activation(le[:], lg[:], ACT.Exp).then_inc(sems["lexp"], 1)

            def turned(i, s):
                act.wait_ge(sems["xT_mm"], nth(i, "xT_mm"))
                act.activation(xT[:, s], bank[:, 0, 0:P], ACT.Copy).then_inc(sems["xT"], 1)

            def silu_of(i, s, reused):
                act.wait_ge(sems["ea_mm"], nth(i, "ea_mm"))
                if reused:
                    act.wait_ge(sems["ey"], nth(i - 2, "ey"))
                act.activation(es[:, s], bank[:, 1 + s, :], ACT.Silu).then_inc(sems["es"], 1)

            def hidden_turned(i, s, reused):
                act.wait_ge(sems["eyT_mm"], nth(i, "eyT_mm"))
                if reused:
                    act.wait_ge(sems["down_e"], nth(i - 2, "down_e"))
                act.activation(eyT[:, s], bank[:, 5, :], ACT.Copy).then_inc(sems["eyT"], 1)

            turned(0, 0)
            for i in range(2):
                silu_of(i, i, False)
                turned(i + 1, 1 - i)
                if i >= 1:
                    hidden_turned(0, 0, False)
            with act.Fori(1, NT // 2 - 1) as pair:
                for s in range(2):
                    silu_of(2 * pair + s, s, True)
                    turned(2 * pair + s + 1, 1 - s)
                    hidden_turned(2 * pair + s - 1, 1 - s, True)
            for i in range(NT - 2, NT + 1):
                if i < NT:
                    silu_of(i, i % 2, True)
                if i + 1 < NT:
                    turned(i + 1, (i + 1) % 2)
                hidden_turned(i - 1, (i - 1) % 2, True)

        @block.vector
        def _(dve):
            dve.memset(eps_ln[:], LN_EPS)
            dve.memset(eps_rms[:], RMS_EPS)
            dve.memset(ones[:], 1.0)
            dve.memset(one_col[:], 1.0).then_inc(sems["setup_dve"], 1)

            def convolve(c, m):
                for k in reversed(range(TAPS)):
                    back = TAPS - 1 - k
                    for h in range(HALVES):
                        weight = M[m]["cw"][:, h, k:k + 1]
                        if back == 0:
                            dve.wait_ge(sems["raw"], nth(c, "raw", h + 1))
                            dve.tensor_scalar(dbu[:, 0, h], bank[:, 2 + h, :], weight, None, ALU.mult) \
                                .then_inc(sems["tap"], 1)
                        else:
                            dve.wait_ge(sems["tap"], nth(c, "tap", HALVES * (back - 1) + h + 1))
                            dve.scalar_tensor_tensor(dbu[:, 0, h, back:], bank[:, 2 + h, 0:T - back], weight,
                                                     dbu[:, 0, h, back:], ALU.mult, ALU.add).then_inc(sems["tap"], 1)

            def minus_A(m):
                dve.wait_ge(sems["setup_act"], m + 1)
                dve.tensor_scalar(M[m]["A"][:], M[m]["A"][:], -1.0, None, ALU.mult)

            def ternary_weights():
                dve.wait_ge(sems["late_loaded"], 16 * len(late))
                last = [1]

                def step_done(ins):
                    ins.then_inc(sems["setup_dve"], 1)
                    last[0] += 1
                    dve.wait_ge(sems["setup_dve"], last[0])

                fcv, prv = fc[:], proj[:].rearrange("p j n -> p (j n)")
                step_done(dve.tensor_reduce(absr[:, 0:1], fcv, AX.X, ALU.add, apply_absolute_value=True))
                step_done(dve.tensor_reduce(absr[:, 1:2], prv, AX.X, ALU.add, apply_absolute_value=True))
                dve.wait_ge(sems["setup_pe"], 1)
                half = 0.5 / (MH * P * D)
                step_done(dve.tensor_scalar(thr[:, 0:2], bank[:, DBANK, 0:2], half, 0.5 * QUANT_EPS, ALU.mult, ALU.add))
                step_done(dve.tensor_scalar(thr[:, 2:4], thr[:, 0:2], -1.0, None, ALU.mult))
                for i, v in enumerate((fcv, prv)):
                    step_done(dve.tensor_scalar(qtmp, v, thr[:, i:i + 1], None, ALU.is_gt))
                    step_done(dve.tensor_scalar(qtmp2, v, thr[:, 2 + i:3 + i], None, ALU.is_lt))
                    step_done(dve.tensor_tensor(v, qtmp, qtmp2, ALU.subtract))
                for j in range(MH):
                    step_done(dve.tensor_scalar(projw[:, j, :], proj[:, j, :], lnw[:, j:j + 1], None, ALU.mult))
                SETUP_DONE.append(last[0])

            def head_ln(c, m, centered=0):
                dve.wait_ge(sems["ln_rstd"], nth(c, "ln_rstd"))
                dve.tensor_tensor(xl_of(c)[:] if m == 0 else xn[1][:], bank[:, centered, :], rstd_m[:], ALU.mult) \
                    .then_inc(sems["ln_done"], 1)

            def head_rms(c, m, k):
                if m == 0:
                    dve.wait_ge(sems["rms_rstd"], nth(k, "rms_rstd"))
                    dve.scalar_tensor_tensor(xn[0][:], xl_of(c)[:], norm_m[:], rstd_m[:], ALU.mult, ALU.mult) \
                        .then_inc(sems["rms_done"], 1)

            def mamba(c, m, k, side, follower=None):
                def norm_ahead(step):
                    if follower and follower[1] == 0:
                        if step == 4:
                            head_ln(follower[0], 0, 4)

                w = M[m]
                xs, zs = xs_sets[set_of(c, m)], zs_sets[set_of(c, m)]
                bc0 = 0 if m == 0 else DTR[1]
                dve.wait_ge(sems["hi"], nth(c, "hi"))
                dve.tensor_tensor(rest, bank[bc0:bc0 + BCR, 0, :], parts[0:BCR, :], ALU.subtract) \
                    .then_inc(sems["rest"], 1)
                dve.wait_ge(sems["rest"], nth(c, "rest"))
                dve.tensor_copy(mid[:], rest).then_inc(sems["mid"], 1)
                dve.wait_ge(sems["mid"], nth(c, "mid"))
                dve.tensor_tensor(parts[2 * BCR:3 * BCR, :], rest, mid[:], ALU.subtract).then_inc(sems["lo"], 1)
                side(0)
                for h in range(HALVES):
                    dve.wait_ge(sems["spabs"], nth(c, "spabs", h + 1))
                    dve.tensor_scalar(sp_max[:, h], bank[:, 2 + h, :], w["db"][:, h:h + 1], 0.0, ALU.add, ALU.max) \
                        .then_inc(sems["spmax"], 1)
                side(1)
                dve.wait_ge(sems["spmax"], nth(c, "spmax", 2))
                dve.wait_ge(sems["spln"], nth(c, "spln"))
                dve.tensor_tensor(delta[:], sp_max, sp_abs, ALU.add).then_inc(sems["delta"], 1)
                dve.wait_ge(sems["delta"], nth(c, "delta"))
                dve.tensor_tensor(du[:], delta[:], xs[:], ALU.mult).then_inc(sems["du"], 1)
                dve.wait_ge(sems["du"], nth(c, "du"))

                def input_of(n):
                    dve.wait_ge(sems["bbc"], nth(c, "bbc", n + 1))
                    dve.tensor_tensor(dbu[:, n % 2], du[:], bank[:, 0:1, :].to_broadcast([P, HALVES, T]),
                                      ALU.mult).then_inc(sems["dbu"], 1)

                input_of(0)
                for step in range(2, HEAD):
                    norm_ahead(step)
                    side(step)
                for n in range(STATE):
                    norm_ahead(HEAD + n)
                    side(HEAD + n)
                    if n + 1 < STATE:
                        if n >= 1:
                            dve.wait_ge(sems["scan"], nth(c, "scan", 2 * n))
                        input_of(n + 1)
                    dve.wait_ge(sems["dbu"], nth(c, "dbu", n + 1))
                    if n >= HBUF:
                        dve.wait_ge(sems["hc"], nth(c, "hc", n - HBUF + 1))
                    for h in range(HALVES):
                        dve.wait_ge(sems["dA"], nth(c, "dA", 2 * n + h + 1))
                        dve.tensor_tensor_scan(hst[:, n % HBUF, h], bank[:, 2 + h, :], dbu[:, n % 2, h],
                                               0.0, ALU.mult, ALU.add).then_inc(sems["scan"], 1)
                    if n == 1 and follower and follower[1] == 0:
                        head_rms(*follower)
                if follower:
                    if follower[1] == 1:
                        head_ln(*follower[:2])
                    convolve(*follower[:2])
                dve.wait_ge(sems["yacc"], nth(c, "yacc", STATE))
                for h in range(HALVES):
                    dve.scalar_tensor_tensor(yd[:, h], xs[:, h], w["dskip"][:, h:h + 1], bank[:, 4 + h, :],
                                             ALU.mult, ALU.add).then_inc(sems["yd"], 1)
                for h in range(HALVES):
                    dve.wait_ge(sems["yd"], nth(c, "yd", h + 1))
                    dve.tensor_tensor(yd[:, h], yd[:, h], zs[:, h], ALU.mult).then_inc(sems["yg"], 1)
                dve.wait_ge(sems["out"], nth(c, "out"))
                dst, res = (h0[:], xl_of(c)[:]) if m == 0 else (seq(x3, k), x2[:])
                dve.tensor_tensor(dst, bank[:, 1, :], res, ALU.add).then_inc(sems["res"], 1)

            def attention_side(k, step):
                if step == 0:
                    dve.wait_ge(sems["dn_rstd"], nth(4 * k, "dn_rstd"))
                    dve.scalar_tensor_tensor(nrm[:], h0[:], norm_a[:], rstd_d[:], ALU.mult, ALU.mult) \
                        .then_inc(sems["dn_done"], 1)
                if step == 1:
                    dve.wait_ge(sems["k_mm"], nth(k, "k_mm"))
                    dve.tensor_copy(ks[:], bank[:, DBANK + 1, :]).then_inc(sems["k_copy"], 1)
                i = step - TILE0 - 1
                if 0 <= i < TILES:
                    keys = P * (i % QB + 1)
                    dve.wait_ge(sems["score"], nth(k, "score", i + 1))
                    dve.tensor_reduce(nmax[:, i:i + 1], bank[:, DBANK + i % 2, 0:keys], AX.X, ALU.max,
                                      negate=True).then_inc(sems["smax"], 1)
                if step == SIDE_STEPS - 1:
                    dve.wait_ge(sems["prob"], nth(k, "prob", TILES))
                    dve.reciprocal(rsums[:], psums[:]).then_inc(sems["recip"], 1)
                    dve.wait_ge(sems["recip"], nth(k, "recip"))
                    dve.wait_ge(sems["pv_copy"], nth(k, "pv_copy", TILES))
                    heads = x1[:].rearrange("p (j n) -> p j n", n=HD)
                    dve.tensor_tensor(heads, heads, rsums[:].rearrange("p j h -> p (j h)").unsqueeze(2)
                                      .to_broadcast([P, QB * N_HEADS, HD]), ALU.mult).then_inc(sems["att"], 1)
                    dve.wait_ge(sems["o_mm"], nth(k, "o_mm"))
                    dve.tensor_tensor(h1[:], bank[:, DBANK + 1, :], h0[:], ALU.add).then_inc(sems["h1"], 1)

            def ff_side(k, step):
                if step == 0:
                    dve.wait_ge(sems["dn_rstd"], nth(4 * k + 1, "dn_rstd"))
                    dve.scalar_tensor_tensor(nrm[:], h1[:], norm_f[:], rstd_d[:], ALU.mult, ALU.mult) \
                        .then_inc(sems["dn_done"], 1)
                if step == 6:
                    for j, rows in enumerate(FFN_ROWS):
                        dve.wait_ge(sems["gs"], nth(k, "gs", j + 1))
                        dve.wait_ge(sems["up_mm"], nth(k, "up_mm", j + 1))
                        dve.tensor_tensor(gc[0:rows, j], gs[0:rows, j], bank[0:rows, DBANK + (j + 1) % 2, :],
                                          ALU.mult).then_inc(sems["gu"], 1)
                if step == 7:
                    dve.wait_ge(sems["down_mm"], nth(k, "down_mm"))
                    dve.tensor_tensor(nrm[:], bank[:, DBANK, :], h1[:], ALU.add).then_inc(sems["ffn_res"], 1)
                if step == 10:
                    dve.wait_ge(sems["dn_rstd"], nth(4 * k + 2, "dn_rstd"))
                    dve.tensor_tensor(nrm[:], bank[:, DBANK, :], rstd_d[:], ALU.mult).then_inc(sems["dn_done"], 1)
                if step in (15, 16):
                    dve.wait_ge(sems["gmean"], nth(k, "gmean"))
                    for j in range(MH // 2 * (step - 15), MH // 2 * (step - 14)):
                        dve.tensor_tensor(gc[:, j], gs[:, j], bank[:, DBANK, :], ALU.subtract) \
                            .then_inc(sems["gcen"], 1)
                if step == 20:
                    dve.wait_ge(sems["pj_mm"], nth(k, "pj_mm"))
                    dve.wait_ge(sems["dn_rstd"], nth(4 * k + 3, "dn_rstd"))
                    dve.tensor_tensor(h1[:], bank[:, DBANK, :], rstd_d[:], ALU.mult).then_inc(sems["pj_scaled"], 1)
                if step == 21:
                    dve.wait_ge(sems["pj_scaled"], nth(k, "pj_scaled"))
                    dve.scalar_tensor_tensor(x2[:], h1[:], projb[:], x1[:], ALU.add, ALU.add) \
                        .then_inc(sems["x2"], 1)

            def beside_attention(k, follower):
                mamba(2 * k, 1, k - 1, lambda step: attention_side(k, step), follower)

            def beside_ff(k):
                mamba(2 * k + 1, 0, k + 1, lambda step: ff_side(k, step), (2 * k + 2, 1, k))

            head_ln(0, 0)
            dve.wait_ge(sems["early_loaded"], 16 * len(early))
            head_rms(0, 0, 0)
            minus_A(0)
            convolve(0, 0)
            mamba(0, 0, 0, lambda step: None, (1, 0, 1))
            ternary_weights()
            mamba(1, 0, 1, lambda step: attention_side(0, step))
            minus_A(1)
            dve.wait_ge(sems["setup_pe"], 2)
            dve.tensor_copy(projb[:], bank[:, DBANK, 2:3]).then_inc(sems["setup_dve"], 1)
            dve.wait_ge(sems["setup_dve"], SETUP_DONE[0] + 1)
            for step in range(SIDE_STEPS):
                ff_side(0, step)
            head_ln(2, 1)
            convolve(2, 1)
            with dve.Fori(1, SEQS - 1) as k:
                beside_attention(k, (2 * k + 1, 0, k + 1))
                beside_ff(k)
            beside_attention(SEQS - 1, None)
            for step in range(SIDE_STEPS):
                ff_side(SEQS - 1, step)
            head_ln(2 * SEQS - 1, 1)
            convolve(2 * SEQS - 1, 1)
            mamba(2 * SEQS - 1, 1, SEQS - 1, lambda step: None)

            for g in range(G):
                if g % QB == 0:
                    dve.wait_ge(sems["xrow"], nth(0, "xrow", g // QB + 1))
                dve.bn_stats(stats[:, g, :], trows[:, g, 0:D]).then_inc(sems["stats"], 1)
            for g in range(G):
                dve.wait_ge(sems["stats"], nth(0, "stats", g + 1))
                dve.bn_aggr(meanvar[:, g, :], stats[:, g, :]).then_inc(sems["meanvar"], 1)
            dve.tensor_copy(trows[:, :, TOKEN], token_id[:]).then_inc(sems["rows_made"], 1)
            dve.wait_ge(sems["meanvar"], nth(0, "meanvar", G))
            dve.tensor_copy(trows[:, :, MEAN], meanvar[:, :, 0]).then_inc(sems["rows_made"], 1)
            dve.wait_ge(sems["logit_mm"], 1)
            dve.wait_ge(sems["rstd"], 1)
            logits = bank[:, 4, 0:G * E].rearrange("p (g e) -> p g e", e=E)
            dve.tensor_tensor(lg[:], logits, trows[:, :, RSTD:RSTD + 1].to_broadcast([P, G, E]), ALU.mult) \
                .then_inc(sems["lscaled"], 1)
            dve.wait_ge(sems["lscaled"], 1)
            dve.tensor_tensor(lg[:], lg[:], router_b[:].unsqueeze(1).to_broadcast([P, G, E]), ALU.add) \
                .then_inc(sems["lbiased"], 1)
            dve.wait_ge(sems["lbiased"], 1)
            dve.tensor_reduce(lmax[:], lg[:], AX.X, ALU.max).then_inc(sems["lmax"], 1)
            dve.wait_ge(sems["lmax"], 1)
            dve.tensor_tensor(lg[:], lg[:], lmax[:].unsqueeze(2).to_broadcast([P, G, E]),
                              ALU.subtract).then_inc(sems["lsub"], 1)
            dve.wait_ge(sems["lsub"], 1)
            dve.scalar_tensor_tensor(cand[:], lg[:], 0.0, eminus[:].unsqueeze(1).to_broadcast([P, G, E]),
                                     ALU.is_ge, ALU.mult).then_inc(sems["cand"], 1)
            dve.wait_ge(sems["cand"], 1)
            dve.tensor_reduce(first_of[:], cand[:], AX.X, ALU.min).then_inc(sems["first"], 1)
            dve.wait_ge(sems["first"], 1)
            dve.tensor_tensor(onehot[:], eminus[:].unsqueeze(2).to_broadcast([P, E, G]),
                              first_of[:].unsqueeze(1).to_broadcast([P, E, G]), ALU.is_equal).then_inc(sems["onehot"], 1)
            dve.wait_ge(sems["lexp"], 1)
            dve.tensor_reduce(lsum[:], le[:], AX.X, ALU.add).then_inc(sems["lsum"], 1)
            dve.wait_ge(sems["lsum"], 1)
            dve.reciprocal(trows[:, :, PROB], lsum[:]).then_inc(sems["rows_made"], 1)

            step = [0]

            def routed(ins):
                ins.then_inc(sems["route"], 1)
                step[0] += 1
                dve.wait_ge(sems["route"], step[0])

            flat = lambda t: t[:].rearrange("p e g -> p (e g)")
            ranks = bank[:, 5, 0:E * G].rearrange("p (e g) -> p e g", g=G)
            totals = bank[:, 6, 0:E * G].rearrange("p (e g) -> p e g", g=G)
            dve.wait_ge(sems["count_mm"], 1)
            routed(dve.tensor_tensor_scan(flat(upto), flat(new_expert), bank[:, 6, 0:E * G], 0.0, ALU.mult, ALU.add))
            dve.tensor_tensor(place[:], upto[:], totals, ALU.subtract).then_inc(sems["rows_made"], 1)
            routed(dve.tensor_tensor(starts[:], upto[:, :, G - 1:G].to_broadcast([P, E, G]),
                                     tile_starts[:].unsqueeze(1).to_broadcast([P, E, G]), ALU.is_gt))
            dve.wait_ge(sems["rows_made"], 4)
            dve.tensor_tensor(place[:], place[:], ranks, ALU.add).then_inc(sems["rows_made"], 1)
            routed(dve.tensor_reduce(tiles_of[:], starts[:], AX.X, ALU.add))
            routed(dve.tensor_tensor_scan(tiles_upto[:], ones[:, 0:E], tiles_of[:], 0.0, ALU.mult, ALU.add))
            dve.tensor_tensor(past[:], tiles_upto[:].unsqueeze(1).to_broadcast([P, NT, E]),
                              tile_id[:].unsqueeze(2).to_broadcast([P, NT, E]), ALU.is_le).then_inc(sems["route"], 1)
            routed(dve.tensor_tensor(tiles_before[:], tiles_upto[:], tiles_of[:], ALU.subtract))
            step[0] += 1
            dve.wait_ge(sems["route"], step[0])
            dve.wait_ge(sems["rows_made"], 5)
            routed(dve.scalar_tensor_tensor(place[:], tiles_before[:].unsqueeze(2).to_broadcast([P, E, G]), float(P),
                                            place[:], ALU.mult, ALU.add))
            routed(dve.tensor_tensor(place[:], place[:], onehot[:], ALU.mult))
            routed(dve.tensor_reduce(row_f[:], place[:].rearrange("p e g -> p g e"), AX.X, ALU.add))
            dve.tensor_copy(row_of[:], row_f[:]).then_inc(sems["row_of"], 1)
            routed(dve.tensor_reduce(expert_f[:], past[:], AX.X, ALU.add))
            dve.tensor_scalar(expert_of[:], expert_f[:], float(E - 1), None, ALU.min).then_inc(sems["experts"], 1)

            def normalized(i, s, reused, index):
                if reused:
                    dve.wait_ge(sems["xT_mm"], nth(i - 2, "xT_mm"))
                dve.tensor_scalar(nrow[:, s], index(0, D), index(MEAN, MEAN + 1), index(RSTD, RSTD + 1),
                                  ALU.subtract, ALU.mult).then_inc(sems["nrow"], 1)

            def gated(i, s, reused):
                dve.wait_ge(sems["es"], nth(i, "es"))
                dve.wait_ge(sems["eg_mm"], nth(i, "eg_mm"))
                if reused:
                    dve.wait_ge(sems["eyT_mm"], nth(i - 2, "eyT_mm"))
                dve.tensor_tensor(ey[:, s], es[:, s], bank[:, 3 + s, :], ALU.mult).then_inc(sems["ey"], 1)

            def finished(i, s, pair, index):
                if not (isinstance(pair, int) and pair == 0):
                    dve.wait_ge(sems[STORED[s]], nth(pair - 1, STORED[s], 16))
                dve.tensor_scalar(target[:, s:s + 1], index(TOKEN, TOKEN + 1), 0.0, None, ALU.add) \
                    .then_inc(sems["target"], 1)
                dve.wait_ge(sems["down_e"], nth(i, "down_e"))
                dve.scalar_tensor_tensor(orow[:, s], bank[:, 6 + s, 0:D], index(PROB, PROB + 1), index(0, D),
                                         ALU.mult, ALU.add).then_inc(sems["orow"], 1)

            def of_tile(i):
                if isinstance(i, int):
                    return lambda a, b: srows[:, i, a:b]
                return lambda a, b: srows[:, bass.ds(i, 1), a:b].rearrange("p o w -> p (o w)")

            dve.wait_ge(sems["srows_first"], 16)
            for i in range(2):
                normalized(i, i, False, of_tile(i))
            for i in range(2):
                gated(i, i, False)
                normalized(i + 2, i, True, of_tile(i + 2))
            dve.wait_ge(sems["srows_rest"], 16)
            for i in range(2, 4):
                gated(i, i - 2, True)
                normalized(i + 2, i - 2, True, of_tile(i + 2))
                finished(i - 2, i - 2, 0, of_tile(i - 2))
            with dve.Fori(2, NT // 2 - 1) as pair:
                for s in range(2):
                    gated(2 * pair + s, s, True)
                    normalized(2 * pair + s + 2, s, True, of_tile(2 * pair + s + 2))
                    finished(2 * pair + s - 2, s, pair - 1, of_tile(2 * pair + s - 2))
            for i in range(NT - 2, NT + 2):
                if i < NT:
                    gated(i, i % 2, True)
                finished(i - 2, i % 2, (i - 2) // 2, of_tile(i - 2))

        @block.tensor
        def _(pe):
            def mm(dst, lhsT, rhs, start=True, stop=True):
                return pe.matmul(dst, lhsT, rhs, start=start, stop=stop)

            def sum_magnitudes():
                pe.wait_ge(sems["setup_dve"], 3)
                pe.wait_ge(sems["zs"], nth(1, "zs", HALVES))
                mm(bank[:, DBANK, 0:2], ones[:], absr[:]).then_inc(sems["setup_pe"], 1)

            def project_bias():
                pe.wait_ge(sems["setup_dve"], SETUP_DONE[0])
                for j in range(MH):
                    last = mm(bank[:, DBANK, 2:3], proj[:, j, :], lnb[:, j:j + 1], j == 0, j == MH - 1)
                last.then_inc(sems["setup_pe"], 1)
                pe.wait_ge(sems["setup_dve"], SETUP_DONE[0] + 1)

            def variance(norm, i, dst_bank, tile):
                pe.wait_ge(sems[norm + "_squared"], nth(i, norm + "_squared"))
                mm(bank[:, dst_bank, :], mean_d[:], tile[:]).then_inc(sems[norm + "_var"], 1)

            def head_center(c, m, k, centered=0):
                if m == 0:
                    pe.wait_ge(sems["x_loaded"], nth(k, "x_loaded", 16))
                else:
                    pe.wait_ge(sems["x2"], nth(k, "x2"))
                mm(bank[:, centered, :], center[:], (xin if m == 0 else x2)[:]).then_inc(sems["ln_centered"], 1)

            def head_input(c, m, k, halves=tuple(range(HALVES))):
                if m == 0:
                    pe.wait_ge(sems["rms_done"], nth(k, "rms_done"))
                else:
                    pe.wait_ge(sems["ln_done"], nth(c, "ln_done"))
                for h in halves:
                    mm(bank[:, 2 + h, :], M[m]["win"][:, P * h:P * h + P], xn[m][:]).then_inc(sems["raw"], 1)

            def head_gate(c, m, k):
                if m == 0 and not (isinstance(c, int) and c <= 1):
                    pe.wait_ge(sems["h1"], nth(k - 1, "h1"))
                for h in range(HALVES):
                    mm(bank[:, DBANK + h, :], M[m]["win"][:, P * (HALVES + h):P * (HALVES + h + 1)], xn[m][:]) \
                        .then_inc(sems["z"], 1)

            def mamba(c, m, k, side, late_side, behind, follower=None):
                def norm_ahead(step):
                    if follower and follower[1] == 0:
                        if step == 3:
                            head_center(*follower, 4)
                        if step == 4:
                            variance("ln", follower[0], 5, rstd_m)
                        if step == 7:
                            variance("rms", follower[2], 5, rstd_m)

                w = M[m]
                xs = xs_sets[set_of(c, m)]
                rows = DTR[m] + BCR
                for h in range(HALVES):
                    pe.wait_ge(sems["xs"], nth(c, "xs", h + 1))
                    last = mm(bank[0:rows, 0, :], w["wx"][:, h, :], xs[:, h], h == 0, h == HALVES - 1)
                last.then_inc(sems["proj"], 1)
                side(0)
                late_side(0)
                pe.wait_ge(sems["dtrows"], nth(c, "dtrows"))
                for h in range(HALVES):
                    mm(bank[:, 2 + h, :], w["wdt"][:, P * h:P * h + P], dt_rows[0:DTR[m], :]) \
                        .then_inc(sems["dtp"], 1)
                side(1)
                late_side(1)
                pe.wait_ge(sems["hi"], nth(c, "hi"))
                pe.wait_ge(sems["midcopy"], nth(c, "midcopy"))
                pe.wait_ge(sems["lo"], nth(c, "lo"))

                def spread(n):
                    if n >= 1:
                        pe.wait_ge(sems["dbu"], nth(c, "dbu", n))
                    mm(bank[:, 0, :], pick[:, n, :], parts[:]).then_inc(sems["bbc"], 1)
                    if n >= 1:
                        pe.wait_ge(sems["ccopy"], nth(c, "ccopy", n))
                    mm(bank[:, 1, :], pick[:, STATE + n, :], parts[:]).then_inc(sems["cbc"], 1)

                def accumulate(n):
                    pe.wait_ge(sems["hc"], nth(c, "hc", n + 1))
                    if n == 0 and follower and follower[1] == 0:
                        pe.wait_ge(sems["rms_done"], nth(follower[2], "rms_done"))
                    for h in range(HALVES):
                        last = mm(bank[:, 4 + h, :], ident[:], hc[:, n % 4, h], n == 0, n == STATE - 1)
                    last.then_inc(sems["yacc"], 1)

                spread(0)
                for step in range(2, HEAD):
                    norm_ahead(step)
                    side(step)
                    late_side(step)
                spread(1)
                for n in range(STATE):
                    norm_ahead(HEAD + n)
                    if follower and follower[1] == 1 and n == STATE - 1:
                        pe.wait_ge(sems["dbu"], nth(c, "dbu", STATE))
                        head_center(*follower)
                    side(HEAD + n)
                    late_side(HEAD + n)
                    if n + 2 < STATE:
                        spread(n + 2)
                    if n >= YLAG:
                        accumulate(n - YLAG)
                    behind(HEAD + n)
                pe.wait_ge(sems["ccopy"], nth(c, "ccopy", STATE))
                if follower and follower[1] == 1:
                    variance("ln", follower[0], 1, rstd_m)
                for i in range(YLAG):
                    if i < YLAG - 1 or not follower:
                        accumulate(STATE - YLAG + i)
                    if follower and follower[1] == 0 and i < HALVES:
                        pe.wait_ge(sems["scan"], nth(c, "scan", 2 * STATE - 1 + i))
                        head_input(*follower, (i,))
                    if follower and follower[1] == 1 and i == 0:
                        pe.wait_ge(sems["scan"], nth(c, "scan", 2 * STATE))
                        head_input(*follower)
                if follower:
                    accumulate(STATE - 1)
                    head_gate(*follower)
                for h in range(HALVES):
                    pe.wait_ge(sems["yg"], nth(c, "yg", h + 1))
                    last = mm(bank[:, 1, :], w["wo"][:, h, :], yd[:, h], h == 0, h == HALVES - 1)
                last.then_inc(sems["out"], 1)

            def attention_side(k, step):
                if step == 0:
                    variance("dn", 3 * k, DBANK + 1, rstd_d)
                if step == 1:
                    pe.wait_ge(sems["dn_done"], nth(3 * k, "dn_done"))
                    mm(bank[:, DBANK, :], wq[:], nrm[:]).then_inc(sems["q_mm"], 1)
                    mm(bank[:, DBANK + 1, :], wk[:], nrm[:]).then_inc(sems["k_mm"], 1)
                if step == 2:
                    pe.wait_ge(sems["q_copy"], nth(k, "q_copy"))
                    for j in range(QB):
                        last = mm(bank[:, DBANK, P * j:P * j + P], nrm[:, P * j:P * j + P], wv[:])
                    last.then_inc(sems["v_mm"], 1)
                    pe.wait_ge(sems["k_copy"], nth(k, "k_copy"))
                i = step - TILE0 - 2
                if 0 <= i < TILES:
                    h, j = i // QB, i % QB
                    pe.wait_ge(sems["probT"], nth(k, "probT", i + 1))
                    for t in range(j + 1):
                        last = mm(bank[:, DBANK + i % 2, 0:HD], probT[:, i % 2, P * t:P * t + P],
                                  vs[:, t, HD * h:HD * h + HD], t == 0, t == j)
                    last.then_inc(sems["pv"], 1)

            def attention_late(k, step):
                i = step - TILE0 - 1
                if 0 <= i < TILES:
                    pe.wait_ge(sems["prob"], nth(k, "prob", i + 1))
                    for t in range(i % QB + 1):
                        last = pe.transpose(bank[:, DBANK + i % 2, P * t:P * t + P], prob[:, i % 2, P * t:P * t + P],
                                            ident[:])
                    last.then_inc(sems["probT_mm"], 1)
                i = step - TILE0
                if 0 <= i < TILES:
                    h, j = i // QB, i % QB
                    if i == 0:
                        pe.wait_ge(sems["v_copy"], nth(k, "v_copy"))
                    if i >= 2:
                        pe.wait_ge(sems["pv_copy"], nth(k, "pv_copy", i - 1))
                    hd = slice(HD * h, HD * h + HD)
                    mm(bank[:, DBANK + i % 2, 0:P * (j + 1)], qs[hd, P * j:P * j + P], ks[hd, 0:P * (j + 1)],
                       True, False)
                    mm(bank[:, DBANK + i % 2, P * j:P * j + P], ident16[:], causal[:], False, True) \
                        .then_inc(sems["score"], 1)
                if step == SIDE_STEPS - 1:
                    pe.wait_ge(sems["att"], nth(k, "att"))
                    for j in range(QB):
                        last = pe.transpose(bank[:, DBANK, P * j:P * j + P], att[:, j, :], ident[:])
                    last.then_inc(sems["attT_mm"], 1)
                    pe.wait_ge(sems["attT"], nth(k, "attT"))
                    mm(bank[:, DBANK + 1, :], wo[:], attT[:]).then_inc(sems["o_mm"], 1)

            def ff_side(k, step):
                if step == 0:
                    variance("dn", 3 * k + 1, DBANK + 1, rstd_d)
                if step == 1:
                    pe.wait_ge(sems["dn_done"], nth(3 * k, "dn_done", 2))
                    for j, rows in enumerate(FFN_ROWS):
                        if j >= 2:
                            pe.wait_ge(sems["gs"], nth(k, "gs", j - 1))
                        mm(bank[0:rows, DBANK + j % 2, :], wgate[:, P * j:P * j + rows], nrm[:]) \
                            .then_inc(sems["gate_mm"], 1)
                if step == 6:
                    for j, rows in enumerate(FFN_ROWS):
                        if j < 2:
                            pe.wait_ge(sems["gs"], nth(k, "gs", j + 2))
                        else:
                            pe.wait_ge(sems["gu"], nth(k, "gu", j - 1))
                        mm(bank[0:rows, DBANK + (j + 1) % 2, :], wup[:, P * j:P * j + rows], nrm[:]) \
                            .then_inc(sems["up_mm"], 1)
                if step == 8:
                    pe.wait_ge(sems["x1"], nth(k, "x1"))
                    mm(bank[:, DBANK, :], center[:], x1[:]).then_inc(sems["dn_centered"], 1)
                if step == 9:
                    variance("dn", 3 * k + 2, DBANK + 1, rstd_d)
                if step == 11:
                    pe.wait_ge(sems["dn_done"], nth(3 * k, "dn_done", 3))
                    for j in range(2):
                        mm(bank[:, DBANK + j, :], fc[:, P * j:P * j + P], nrm[:]).then_inc(sems["fc_mm"], 1)
                if step == 12:
                    for j in range(2, MH):
                        pe.wait_ge(sems["gelu"], nth(k, "gelu", j - 1))
                        mm(bank[:, DBANK + j % 2, :], fc[:, P * j:P * j + P], nrm[:]).then_inc(sems["fc_mm"], 1)

            def ff_behind(k, step):
                if step == 6:
                    for j, rows in enumerate(FFN_ROWS):
                        pe.wait_ge(sems["gu"], nth(k, "gu", max(j + 1, 2)))
                        last = mm(bank[:, DBANK, :], wdown[0:rows, j, :], gc[0:rows, j], j == 0, j == FB - 1)
                    last.then_inc(sems["down_mm"], 1)
                if step == 13:
                    pe.wait_ge(sems["gelu"], nth(k, "gelu", MH))
                if step in (13, 14):
                    for j in range(MH // 2 * (step - 13), MH // 2 * (step - 12)):
                        last = mm(bank[:, DBANK, :], mean_h[:], gs[:, j], j == 0, j == MH - 1)
                    if step == 14:
                        last.then_inc(sems["gmean"], 1)
                if step in (16, 17):
                    for j in range(MH // 2 * (step - 16), MH // 2 * (step - 15)):
                        pe.wait_ge(sems["gsq"], nth(k, "gsq", j + 1))
                        last = mm(bank[:, DBANK + 1, :], mean_h[:], gs[:, j], j == 0, j == MH - 1)
                    if step == 17:
                        last.then_inc(sems["dn_var"], 1)
                if step == 18:
                    for j in range(MH):
                        last = mm(bank[:, DBANK, :], projw[:, j, :], gc[:, j], j == 0, j == MH - 1)
                    last.then_inc(sems["pj_mm"], 1)

            def nothing(step):
                pass

            def beside_attention(k, follower):
                mamba(2 * k, 1, k - 1, lambda step: attention_side(k, step), lambda step: attention_late(k, step),
                      nothing, follower)

            def beside_ff(k):
                mamba(2 * k + 1, 0, k + 1, lambda step: ff_side(k, step), nothing, lambda step: ff_behind(k, step),
                      (2 * k + 2, 1, k))

            pe.wait_ge(sems["first_loaded"], 16 * len(first))
            head_center(0, 0, 0)
            variance("ln", 0, 1, rstd_m)
            variance("rms", 0, 1, rstd_m)
            pe.wait_ge(sems["early_loaded"], 16 * len(early))
            head_input(0, 0, 0)
            head_gate(0, 0, 0)
            mamba(0, 0, 0, nothing, nothing, nothing, (1, 0, 1))
            sum_magnitudes()
            pe.wait_ge(sems["late_loaded"], 16 * len(late))
            mamba(1, 0, 1, lambda step: attention_side(0, step), lambda step: attention_late(0, step), nothing)
            project_bias()
            for step in range(SIDE_STEPS):
                ff_side(0, step)
                ff_behind(0, step)
            head_center(2, 1, 0)
            variance("ln", 2, 1, rstd_m)
            head_input(2, 1, 0)
            head_gate(2, 1, 0)
            with pe.Fori(1, SEQS - 1) as k:
                beside_attention(k, (2 * k + 1, 0, k + 1))
                beside_ff(k)
            beside_attention(SEQS - 1, None)
            for step in range(SIDE_STEPS):
                ff_side(SEQS - 1, step)
                ff_behind(SEQS - 1, step)
            pe.wait_ge(sems["res"], nth(2 * SEQS - 2, "res"))
            head_center(2 * SEQS - 1, 1, SEQS - 1)
            variance("ln", 2 * SEQS - 1, 1, rstd_m)
            head_input(2 * SEQS - 1, 1, SEQS - 1)
            head_gate(2 * SEQS - 1, 1, SEQS - 1)
            mamba(2 * SEQS - 1, 1, SEQS - 1, nothing, nothing, nothing)

            pe.wait_ge(sems["res"], nth(2 * SEQS - 1, "res"))
            mm(bank[:, 4, 0:E], center[:], router[:]).then_inc(sems["router_mm"], 1)
            for b in range(SEQS):
                for j in range(QB):
                    last = pe.transpose(bank[:, b, P * j:P * j + P], x3[:, b, P * j:P * j + P], ident[:])
                last.then_inc(sems["xrow_mm"], 1)
            pe.wait_ge(sems["router_c"], 1)
            for g in range(G):
                last = mm(bank[:, 4, E * g:E * g + E], x3[:, g // QB, P * (g % QB):P * (g % QB) + P], router_c[:])
            last.then_inc(sems["logit_mm"], 1)
            pe.wait_ge(sems["onehot"], 1)
            mm(bank[:, 5, 0:E * G], earlier[:], onehot[:].rearrange("p e g -> p (e g)"))
            mm(bank[:, 6, 0:E * G], ones[:], onehot[:].rearrange("p e g -> p (e g)")).then_inc(sems["count_mm"], 1)

            def turn(i, s):
                pe.wait_ge(sems["nrow"], nth(i, "nrow"))
                pe.transpose(bank[:, 0, 0:P], nrow[:, s], ident[:]).then_inc(sems["xT_mm"], 1)

            def expert(i):
                return nc.values_load(expert_of[0:1, i:i + 1] if isinstance(i, int) else expert_of[0:1, bass.ds(i, 1)],
                                      engines=[mybir.EngineType.PE], min_val=0, max_val=E - 1,
                                      skip_runtime_bounds_check_because="clamped to the last expert on the chip")

            def up(i, s, reused):
                e = expert(i)
                of_expert = w1[:, bass.ds(e, 1), :].rearrange("p o n -> p (o n)")
                pe.wait_ge(sems["xT"], nth(i, "xT"))
                if reused:
                    pe.wait_ge(sems["es"], nth(i - 2, "es"))
                mm(bank[:, 1 + s, :], xT[:, s], of_expert[:, 0:MOE_H]).then_inc(sems["ea_mm"], 1)
                if reused:
                    pe.wait_ge(sems["ey"], nth(i - 2, "ey"))
                mm(bank[:, 3 + s, :], xT[:, s], of_expert[:, MOE_H:]).then_inc(sems["eg_mm"], 1)

            def turn_hidden(i, s):
                pe.wait_ge(sems["ey"], nth(i, "ey"))
                if not (isinstance(i, int) and i == 0):
                    pe.wait_ge(sems["eyT"], nth(i - 1, "eyT"))
                for j in range(MB):
                    last = pe.transpose(bank[:, 5, P * j:P * j + P], ey[:, s, P * j:P * j + P], ident[:])
                last.then_inc(sems["eyT_mm"], 1)

            def down(i, s, reused):
                e = expert(i)
                of_expert = w2[:, bass.ds(e, 1), :, :].rearrange("p o j n -> p (o j) n")
                pe.wait_ge(sems["eyT"], nth(i, "eyT"))
                if reused:
                    pe.wait_ge(sems["orow"], nth(i - 2, "orow"))
                for j in range(MB):
                    last = mm(bank[:, 6 + s, 0:D], eyT[:, s, P * j:P * j + P], of_expert[:, j, :], j == 0, j == MB - 1)
                last.then_inc(sems["down_e"], 1)

            pe.wait_ge(sems["experts"], 1)
            pe.wait_ge(sems["w_loaded"], 16 * len(experts))
            turn(0, 0)
            for i in range(4):
                up(i, i % 2, i >= 2)
                turn(i + 1, 1 - i % 2)
                if i >= 1:
                    turn_hidden(i - 1, 1 - i % 2)
                if i >= 2:
                    down(i - 2, i % 2, False)
            with pe.Fori(2, NT // 2 - 1) as pair:
                for s in range(2):
                    i = 2 * pair + s
                    up(i, s, True)
                    turn(i + 1, 1 - s)
                    turn_hidden(i - 1, 1 - s)
                    down(i - 2, s, True)
            for i in range(NT - 2, NT + 2):
                if i < NT:
                    up(i, i % 2, True)
                if i + 1 < NT:
                    turn(i + 1, (i + 1) % 2)
                if i - 1 < NT:
                    turn_hidden(i - 1, (i - 1) % 2)
                down(i - 2, i % 2, True)


def kernel(**a):
    import numpy as np
    import concourse.bacc as bacc
    from concourse import mybir
    from concourse.bass_utils import run_bass_kernel_spmd

    a = {k: np.asarray(v) for k, v in a.items()}
    x = a["L0_attn_x"]
    SEQS, T, D = x.shape
    f32 = np.float32
    half_cols = lambda v: v.reshape(2, 128).T
    halves = lambda v: v.reshape(2, 128, -1).transpose(1, 0, 2)

    STATE, E, QB, BCR = 16, 8, T // 128, 32
    xp = a["L0_attn_x_proj_w"]
    eye = np.eye(128, dtype=f32)
    pick = np.zeros((3 * BCR, BCR, 128), f32)
    for part in range(3):
        for n in range(BCR):
            pick[part * BCR + n, n, :] = 1
    TOKENS = SEQS * T
    G = TOKENS // 128
    NT = G + E + (G + E) % 2
    blank = np.zeros((NT * 128, D + 4), f32)
    blank[:, -1] = TOKENS + np.arange(NT * 128)
    heads = np.repeat(np.arange(2), 2)

    def per_head(w):
        return w.reshape(2, 32, D)[heads].reshape(128, D).T

    put = {
        "xT": x.transpose(0, 2, 1),
        "ident": eye, "ident16": eye, "center": eye - f32(1 / 128), "mean_d": np.full((128, 128), 1 / 128, f32),
        "mean_h": np.full((128, 128), 1 / 512, f32),
        "causal": np.triu(np.full((128, 128), -1e30, f32), 1),
        "pick": pick, "blank": blank,
        "eminus": np.broadcast_to(np.arange(E, dtype=f32) - E, (128, E)),
        "token_id": np.arange(TOKENS, dtype=f32).reshape(G, 128).T,
        "earlier": np.triu(np.ones((128, 128), f32), 1),
        "new_expert": np.broadcast_to((np.arange(G) > 0).astype(f32), (128, E, G)),
        "tile_starts": np.broadcast_to(128 * np.arange(G, dtype=f32), (128, G)),
        "tile_id": np.broadcast_to(np.arange(NT, dtype=f32), (128, NT)),
        "norm_m": a["L0_attn_norm_m_w"][:, None], "norm_a": a["L0_attn_norm_attn_w"][:, None],
        "norm_f": a["L0_attn_norm_ffn_w"][:, None],
        "m0_win": a["L0_attn_in_proj_w"].T, "m0_cw": halves(a["L0_attn_conv_w"][:, 0, :]),
        "m0_cb": half_cols(a["L0_attn_conv_b"]), "m0_wx": xp.T, "m0_dtT": a["L0_attn_dt_w"].T,
        "m0_db": half_cols(a["L0_attn_dt_b"]), "m0_Alog": a["L0_attn_A_log"].reshape(2, 128, STATE),
        "m0_D": half_cols(a["L0_attn_D_skip"]), "m0_wo": a["L0_attn_out_proj_w"].T,
        "m1_win": a["L1_attn_W_in"], "m1_cw": halves(a["L1_attn_conv_w"][:, 0, :].T),
        "m1_cb": half_cols(a["L1_attn_conv_b"]), "m1_wx": a["L1_attn_W_x"], "m1_dtT": a["L1_attn_W_dt"],
        "m1_db": half_cols(a["L1_attn_b_dt"]), "m1_Alog": a["L1_attn_A_log"].reshape(2, 128, STATE),
        "m1_D": half_cols(a["L1_attn_D"]), "m1_wo": a["L1_attn_W_out"],
        "qT": a["L0_attn_q_w"].T, "kT": per_head(a["L0_attn_k_w"]), "vT": per_head(a["L0_attn_v_w"]),
        "oT": a["L0_attn_o_w"].T, "gateT": a["L0_attn_gate_w"].T, "upT": a["L0_attn_up_w"].T,
        "downT": a["L0_attn_down_w"].T, "fcT": a["L0_ffn_W_fc"].T, "projT": a["L0_ffn_W_proj"].T,
        "lnw": a["L0_ffn_ln_w"].reshape(4, 128).T, "lnb": a["L0_ffn_ln_b"].reshape(4, 128).T,
        "router": a["L1_ffn_router_w"], "router_b": a["L1_ffn_router_b"][None, :],
        "w1": a["L1_ffn_w1"], "w2": a["L1_ffn_w2"],
    }
    import ml_dtypes
    for name in ("pick", "ident16", "causal"):
        put[name] = put[name].astype(ml_dtypes.bfloat16)
    nc = bacc.Bacc("TRN2", target_bir_lowering=False, num_devices=1)
    arrays, dram = {}, {}
    for name, v in put.items():
        v = np.ascontiguousarray(v)
        arrays["in_" + name] = v
        dram[name] = nc.dram_tensor("in_" + name, v.shape, mybir.dt.from_np(v.dtype), kind="ExternalInput").ap()
    out = nc.dram_tensor("out_rows", (TOKENS + NT * 128, D), mybir.dt.float32, kind="ExternalOutput").ap()
    sorted_rows = nc.dram_tensor("sorted_rows", (NT * 128, D + 4), mybir.dt.float32).ap()
    build(nc, dram, sorted_rows, out)
    r = run_bass_kernel_spmd(nc, [arrays], core_ids=[0])
    return r.results[0]["out_rows"][0:TOKENS].reshape(SEQS, T, D)
```
